# Optimizing a Trainium2 kernel written in Bass

```python
import numpy as np
import jax
import jax.numpy as jnp

def _softmax(x, axis=-1):
    return jax.nn.softmax(x, axis=axis)

def _gelu(x):
    return jax.nn.gelu(x, approximate=True)

def _silu(x):
    return jax.nn.silu(x)

def _sigmoid(x):
    return jax.nn.sigmoid(x)

def _layernorm(x, axis=-1, eps=1e-05):
    m = jnp.mean(x, axis=axis, keepdims=True)
    v = jnp.var(x, axis=axis, keepdims=True)
    return (x - m) / jnp.sqrt(v + eps)

def _scatter_add(tgt, idx, src, axis=0):
    return tgt.at[idx].add(src)

def _segment_sum(src, seg, n):
    return jax.ops.segment_sum(src, seg, n)
kernel_name = 'mk_xattn_seq_d1_seqx_r2_3ba68d'

def setup_inputs(seed: int=0):
    np.random.seed(seed)
    _w = jnp.asarray

    def _rec_inputs():
        import jax
        import jax.numpy as jnp
        _rk = jax.random.key(seed)
        x = -0.0002928 + 1 * jax.random.normal(jax.random.fold_in(_rk, 1), (2, 2048, 512), jnp.float32)
        _lenS = 2048 - jax.random.randint(jax.random.fold_in(_rk, 7), (2,), 0, max(1, 2048 // 4) + 1, jnp.int32)
        _lenS2 = 154 - jax.random.randint(jax.random.fold_in(_rk, 8), (2,), 0, max(1, 154 // 4) + 1, jnp.int32)
        _ctx_1024P = jax.random.normal(jax.random.fold_in(_rk, 11), (2, 16, 512), jnp.float32)
        _ctx_1024c = jax.random.dirichlet(jax.random.fold_in(_rk, 511), 0.3 * jnp.ones((16,), jnp.float32), (2, 154))
        _ctx_1024t = jnp.einsum('bsk,bkd->bsd', _ctx_1024c, _ctx_1024P)
        _ctx_1024t = _ctx_1024t * jax.lax.rsqrt(jnp.mean(jnp.square(_ctx_1024t)) + 1e-12) * 0.953939
        ctx_1024 = -0.000514642 + 1.00011 * (_ctx_1024t + 0.3 * jax.random.normal(jax.random.fold_in(_rk, 611), (2, 154, 512), jnp.float32))
        _validS = jnp.arange(2048)[None, :] < _lenS[:, None]
        _validS2 = jnp.arange(154)[None, :] < _lenS2[:, None]
        _causal = jnp.tril(jnp.ones((2048, 2048), dtype=bool))
        mask_BxS2_ik0 = jnp.where(jnp.broadcast_to(_validS2[:, :], (2, 154)), 0, 1).astype(jnp.int32)
        return (x, ctx_1024, mask_BxS2_ik0)
    x, ctx_1024, mask_BxS2_ik0 = _rec_inputs()

    def _L0_xattn_setup():
        import jax, jax.numpy as jnp
        import numpy as np
        DIM = 512
        HEADS = 16
        HEAD_DIM = DIM // HEADS
        HIDDEN = 4 * DIM
        EPS = 1e-05
        SCALE = HEAD_DIM ** (-0.5)

        def layer_norm(x, w, b):
            mu = jnp.mean(x, axis=-1, keepdims=True)
            var = jnp.mean(jnp.square(x - mu), axis=-1, keepdims=True)
            return (x - mu) * jax.lax.rsqrt(var + EPS) * w + b

        def _heads(t):
            B, N, C = t.shape
            return t.reshape(B, N, HEADS, HEAD_DIM).transpose(0, 2, 1, 3)

        def _merge(t):
            B, H, N, D = t.shape
            return t.transpose(0, 2, 1, 3).reshape(B, N, H * D)

        def block_forward(x, codebook_embeds, codebook_mask, ln0_w, ln0_b, qkv_w, sa_proj_w, ln1_w, ln1_b, q_w, k_w, v_w, ca_proj_w, ln2_w, ln2_b, fc1_w, fc1_b, fc2_w, fc2_b):
            xn = layer_norm(x, ln0_w, ln0_b)
            qkv = xn @ qkv_w.T
            q, k, v = jnp.split(qkv, 3, axis=-1)
            q, k, v = (_heads(q), _heads(k), _heads(v))
            attn = jnp.einsum('bhnd,bhmd->bhnm', q, k) * SCALE
            attn = jax.nn.softmax(attn, axis=-1)
            sa = _merge(jnp.einsum('bhnm,bhmd->bhnd', attn, v)) @ sa_proj_w.T
            x = x + sa
            xn = layer_norm(x, ln1_w, ln1_b)
            q = _heads(xn @ q_w.T)
            k = _heads(codebook_embeds @ k_w.T)
            v = _heads(codebook_embeds @ v_w.T)
            attn = jnp.einsum('bhnd,bhmd->bhnm', q, k) * SCALE
            bias = (1.0 - codebook_mask.astype(attn.dtype))[:, None, None, :] * -10000.0
            attn = jax.nn.softmax(attn + bias, axis=-1)
            ca = _merge(jnp.einsum('bhnm,bhmd->bhnd', attn, v)) @ ca_proj_w.T
            x = x + ca
            xn = layer_norm(x, ln2_w, ln2_b)
            h = jax.nn.gelu(xn @ fc1_w.T + fc1_b, approximate=False)
            x = x + (h @ fc2_w.T + fc2_b)
            return x
        key = jax.random.key(seed)
        ks = jax.random.split(key, 16)
        B, Nx, Nc = (4, 512, 256)
        s = DIM ** (-0.5)
        inp = {'x': jax.random.normal(ks[0], (B, Nx, DIM), jnp.float32), 'codebook_embeds': jax.random.normal(ks[1], (B, Nc, DIM), jnp.float32), 'codebook_mask': jax.random.randint(ks[2], (B, Nc), 0, 2, jnp.int32), 'ln0_w': jnp.ones((DIM,), jnp.float32), 'ln0_b': jnp.zeros((DIM,), jnp.float32), 'qkv_w': jax.random.normal(ks[3], (3 * DIM, DIM), jnp.float32) * s, 'sa_proj_w': jax.random.normal(ks[4], (DIM, DIM), jnp.float32) * s, 'ln1_w': jnp.ones((DIM,), jnp.float32), 'ln1_b': jnp.zeros((DIM,), jnp.float32), 'q_w': jax.random.normal(ks[5], (DIM, DIM), jnp.float32) * s, 'k_w': jax.random.normal(ks[6], (DIM, DIM), jnp.float32) * s, 'v_w': jax.random.normal(ks[7], (DIM, DIM), jnp.float32) * s, 'ca_proj_w': jax.random.normal(ks[8], (DIM, DIM), jnp.float32) * s, 'ln2_w': jnp.ones((DIM,), jnp.float32), 'ln2_b': jnp.zeros((DIM,), jnp.float32), 'fc1_w': jax.random.normal(ks[9], (HIDDEN, DIM), jnp.float32) * s, 'fc1_b': jnp.zeros((HIDDEN,), jnp.float32), 'fc2_w': jax.random.normal(ks[10], (DIM, HIDDEN), jnp.float32) * HIDDEN ** (-0.5), 'fc2_b': jnp.zeros((DIM,), jnp.float32)}
        return inp
    _L0_xattn_all = _L0_xattn_setup()
    _L0_xattn_in = {k: v for k, v in _L0_xattn_all.items() if k in ('ln0_w', 'ln0_b', 'qkv_w', 'sa_proj_w', 'ln1_w', 'ln1_b', 'q_w', 'k_w', 'v_w', 'ca_proj_w', 'ln2_w', 'ln2_b', 'fc1_w', 'fc1_b', 'fc2_w', 'fc2_b')}
    del _L0_xattn_all
    return {'x': x, 'ctx_1024': ctx_1024, 'mask_BxS2_ik0': mask_BxS2_ik0, 'L0_xattn_ln0_w': _L0_xattn_in['ln0_w'], 'L0_xattn_ln0_b': _L0_xattn_in['ln0_b'], 'L0_xattn_qkv_w': _L0_xattn_in['qkv_w'], 'L0_xattn_sa_proj_w': _L0_xattn_in['sa_proj_w'], 'L0_xattn_ln1_w': _L0_xattn_in['ln1_w'], 'L0_xattn_ln1_b': _L0_xattn_in['ln1_b'], 'L0_xattn_q_w': _L0_xattn_in['q_w'], 'L0_xattn_k_w': _L0_xattn_in['k_w'], 'L0_xattn_v_w': _L0_xattn_in['v_w'], 'L0_xattn_ca_proj_w': _L0_xattn_in['ca_proj_w'], 'L0_xattn_ln2_w': _L0_xattn_in['ln2_w'], 'L0_xattn_ln2_b': _L0_xattn_in['ln2_b'], 'L0_xattn_fc1_w': _L0_xattn_in['fc1_w'], 'L0_xattn_fc1_b': _L0_xattn_in['fc1_b'], 'L0_xattn_fc2_w': _L0_xattn_in['fc2_w'], 'L0_xattn_fc2_b': _L0_xattn_in['fc2_b']}

def reference(x, ctx_1024, mask_BxS2_ik0, L0_xattn_ln0_w, L0_xattn_ln0_b, L0_xattn_qkv_w, L0_xattn_sa_proj_w, L0_xattn_ln1_w, L0_xattn_ln1_b, L0_xattn_q_w, L0_xattn_k_w, L0_xattn_v_w, L0_xattn_ca_proj_w, L0_xattn_ln2_w, L0_xattn_ln2_b, L0_xattn_fc1_w, L0_xattn_fc1_b, L0_xattn_fc2_w, L0_xattn_fc2_b):
    import jax
    import jax.numpy as jnp

    def _L0_xattn_ref(x, codebook_embeds, codebook_mask, ln0_w, ln0_b, qkv_w, sa_proj_w, ln1_w, ln1_b, q_w, k_w, v_w, ca_proj_w, ln2_w, ln2_b, fc1_w, fc1_b, fc2_w, fc2_b):
        import jax, jax.numpy as jnp
        import numpy as np
        DIM = 512
        HEADS = 16
        HEAD_DIM = DIM // HEADS
        HIDDEN = 4 * DIM
        EPS = 1e-05
        SCALE = HEAD_DIM ** (-0.5)

        def layer_norm(x, w, b):
            mu = jnp.mean(x, axis=-1, keepdims=True)
            var = jnp.mean(jnp.square(x - mu), axis=-1, keepdims=True)
            return (x - mu) * jax.lax.rsqrt(var + EPS) * w + b

        def _heads(t):
            B, N, C = t.shape
            return t.reshape(B, N, HEADS, HEAD_DIM).transpose(0, 2, 1, 3)

        def _merge(t):
            B, H, N, D = t.shape
            return t.transpose(0, 2, 1, 3).reshape(B, N, H * D)

        def block_forward(x, codebook_embeds, codebook_mask, ln0_w, ln0_b, qkv_w, sa_proj_w, ln1_w, ln1_b, q_w, k_w, v_w, ca_proj_w, ln2_w, ln2_b, fc1_w, fc1_b, fc2_w, fc2_b):
            xn = layer_norm(x, ln0_w, ln0_b)
            qkv = xn @ qkv_w.T
            q, k, v = jnp.split(qkv, 3, axis=-1)
            q, k, v = (_heads(q), _heads(k), _heads(v))
            attn = jnp.einsum('bhnd,bhmd->bhnm', q, k) * SCALE
            attn = jax.nn.softmax(attn, axis=-1)
            sa = _merge(jnp.einsum('bhnm,bhmd->bhnd', attn, v)) @ sa_proj_w.T
            x = x + sa
            xn = layer_norm(x, ln1_w, ln1_b)
            q = _heads(xn @ q_w.T)
            k = _heads(codebook_embeds @ k_w.T)
            v = _heads(codebook_embeds @ v_w.T)
            attn = jnp.einsum('bhnd,bhmd->bhnm', q, k) * SCALE
            bias = (1.0 - codebook_mask.astype(attn.dtype))[:, None, None, :] * -10000.0
            attn = jax.nn.softmax(attn + bias, axis=-1)
            ca = _merge(jnp.einsum('bhnm,bhmd->bhnd', attn, v)) @ ca_proj_w.T
            x = x + ca
            xn = layer_norm(x, ln2_w, ln2_b)
            h = jax.nn.gelu(xn @ fc1_w.T + fc1_b, approximate=False)
            x = x + (h @ fc2_w.T + fc2_b)
            return x
        return block_forward(x, codebook_embeds, codebook_mask, ln0_w, ln0_b, qkv_w, sa_proj_w, ln1_w, ln1_b, q_w, k_w, v_w, ca_proj_w, ln2_w, ln2_b, fc1_w, fc1_b, fc2_w, fc2_b)
    x = _L0_xattn_ref(x, ctx_1024, mask_BxS2_ik0, L0_xattn_ln0_w, L0_xattn_ln0_b, L0_xattn_qkv_w, L0_xattn_sa_proj_w, L0_xattn_ln1_w, L0_xattn_ln1_b, L0_xattn_q_w, L0_xattn_k_w, L0_xattn_v_w, L0_xattn_ca_proj_w, L0_xattn_ln2_w, L0_xattn_ln2_b, L0_xattn_fc1_w, L0_xattn_fc1_b, L0_xattn_fc2_w, L0_xattn_fc2_b)
    return x

_drawn_inputs = setup_inputs


def setup_inputs(seed=0):
    import zlib

    import numpy as np

    out = dict(_drawn_inputs(seed))
    spreads = {'L0_xattn_ln0_w': (1.0, 0.592),
     'L0_xattn_ln0_b': (0.0, 0.1),
     'L0_xattn_ln1_w': (1.0, 0.2),
     'L0_xattn_ln1_b': (0.0, 0.321),
     'L0_xattn_ln2_w': (1.0, 0.2),
     'L0_xattn_ln2_b': (0.0, 0.1),
     'L0_xattn_fc1_b': (0.0, 0.1),
     'L0_xattn_fc2_b': (0.0, 0.1)}
    factors = {}
    for name, (base, spread) in spreads.items():
        noise = np.random.default_rng([zlib.crc32(name.encode()), seed]).standard_normal(out[name].shape)
        drawn = base * np.exp(spread * noise) if base else spread * noise
        out[name] = jnp.asarray(drawn.astype(out[name].dtype))
    for name, factor in factors.items():
        out[name] = (out[name] * factor).astype(out[name].dtype)
    return out
```

```python
import math
from contextlib import ExitStack

import concourse.bass as bass
from concourse import mybir

P = 128
ALU = mybir.AluOpType
ACT = mybir.ActivationFunctionType
F32 = mybir.dt.float32
F32R = mybir.dt.float32r
I32 = mybir.dt.int32
AX_X = mybir.AxisListType.X

HEAD_DIM = 32
HEADS_PER_GROUP = P // HEAD_DIM
TOK = 512
SUB = TOK // P
EPS = 1e-5
MASK_BIAS = -10000.0



class Memory:

    def __init__(self, nc, stack, phase):
        self.nc, self.stack, self.phase, self.sems = nc, stack, phase, []
        stack.callback(self.release)

    def release(self):
        self.nc.clear_and_free_semaphores(self.sems)
        self.nc.all_engine_barrier()

    def sbuf(self, name, shape, dtype=F32):
        return self.stack.enter_context(self.nc.sbuf_tensor(f"{self.phase}_{name}", shape, dtype))

    def psum(self, name, shape):
        return self.stack.enter_context(self.nc.psum_tensor(f"{self.phase}_{name}", shape, F32))

    def sem(self, name):
        self.sems.append(self.nc.alloc_semaphore(f"{self.phase}_{name}"))
        return self.sems[-1]


def wait_alone(eng, sem, value, passed):
    eng.wait_ge(sem, value)
    eng.sem_inc(passed, 1)


def product(nc, out, left, right, first, last):
    (left_high, left_low), (right_high, right_low) = left, right
    nc.tensor.matmul(out, left_high, right_high, start=first, stop=False)
    nc.tensor.matmul(out, left_high, right_low, start=False, stop=False)
    return nc.tensor.matmul(out, left_low, right_high, start=False, stop=last)


def make_identity(nc, pool, identity, ident_done):
    nc.gpsimd.memset(identity[:], 0.0).then_inc(ident_done, 1)
    pool.wait_ge(ident_done, 1)
    nc.gpsimd.affine_select(out=identity[:], in_=identity[:], compare_op=ALU.not_equal, fill=1.0, base=0,
                            pattern=[[-1, P]], channel_multiplier=1).then_inc(ident_done, 1)


def token_phase(nc, name, x_in, ln_w, ln_b, attn=None, proj_w=None, x_out=None, v_w=None, v_out=None,
                qk=(), xn_out=None):
    dim = x_in.shape[1]
    tiles = x_in.shape[0] // TOK
    chunks = dim // P
    out_groups = dim // P
    n_v = SUB if v_w is not None else 0
    n_qk = len(qk) * out_groups
    n_out = n_v + n_qk
    n_early = n_out - out_groups if n_out > out_groups else n_out // 2
    slots = 4
    weights = ([proj_w] if proj_w is not None else []) + ([v_w] if v_w is not None else []) + [w for w, _ in qk]
    i_proj = 0
    i_v = 1 if proj_w is not None else 0
    i_qk = i_v + (1 if v_w is not None else 0)

    with ExitStack() as stack:
        m = Memory(nc, stack, name)
        w_raw = m.sbuf("w_raw", [P, 2, chunks, dim])
        w_high = m.sbuf("w_high", [P, len(weights), chunks, dim], F32R) if weights else None
        w_low = m.sbuf("w_low", [P, len(weights), chunks, dim], F32R) if weights else None
        gain = m.sbuf("gain", [P, chunks])
        shift = m.sbuf("shift", [P, chunks])
        identity = m.sbuf("identity", [P, P])
        x = m.sbuf("x", [P, 2, SUB, dim])
        stats = m.sbuf("stats", [P, SUB, 6])
        moments = m.sbuf("moments", [P, SUB, 2])
        var = m.sbuf("var", [P, SUB])
        rstd = m.sbuf("rstd", [P, SUB])
        minus_half = m.sbuf("minus_half", [P, SUB])
        xn = m.sbuf("xn", [P, 2, SUB, dim])
        xt = m.sbuf("xt", [P, chunks, TOK])
        xt_high = m.sbuf("xt_high", [P, 2, chunks, TOK], F32R)
        xt_low = m.sbuf("xt_low", [P, 2, chunks, TOK], F32R)
        if attn is not None:
            a_high = m.sbuf("a_high", [P, 2, chunks, TOK], F32R)
            a_low = m.sbuf("a_low", [P, 2, chunks, TOK], F32R)
        if n_qk:
            r_high = m.sbuf("r_high", [P, slots, TOK], F32R)
            r_low = m.sbuf("r_low", [P, slots, TOK], F32R)
        if n_v:
            v_sb = m.sbuf("v_sb", [P, SUB, dim])
        turned = m.psum("turned", [P, 4, TOK])
        result = m.psum("result", [P, 4, TOK])

        w_loaded = [m.sem(f"w_loaded{k}") for k in range(2)]
        w_high_done = m.sem("w_high_done")
        w_ready = m.sem("w_ready")
        ln_loaded = m.sem("ln_loaded")
        ident_done = m.sem("ident_done")
        waits_passed = m.sem("waits_passed")
        x_loaded = [m.sem(f"x_loaded{u}") for u in range(2)]
        a_loaded = [m.sem(f"a_loaded{u}") for u in range(2)]
        x_stored = [m.sem(f"x_stored{u}") for u in range(2)]
        proj_done = m.sem("proj_done")
        x_ready = m.sem("x_ready")
        stats_done = m.sem("stats_done")
        moments_done = m.sem("moments_done")
        var_done = m.sem("var_done")
        rstd_done = m.sem("rstd_done")
        xn_ready = m.sem("xn_ready")
        turn_done = m.sem("turn_done")
        xt_done = m.sem("xt_done")
        xt_high_done = m.sem("xt_high_done")
        xt_ready = m.sem("xt_ready")
        xt_stored = [m.sem(f"xt_stored{u}") for u in range(2)]
        result_done = m.sem("result_done")
        high_done = m.sem("high_done")
        result_read = m.sem("result_read")
        stored = [m.sem(f"stored{k}") for k in range(slots)]
        v_stored = [m.sem(f"v_stored{s}") for s in range(SUB)]

        x_view = x_in.rearrange("(t s p) d -> t p s d", p=P, s=SUB)

        with nc.Block() as block:

            @block.sync
            def _(sp):
                def load(t, u):
                    if attn is not None:
                        for part, to in ((0, a_high), (1, a_low)):
                            sp.dma_start(to[:, u].bitcast(F32), attn[part].rearrange("(c p) t -> p c t", p=P)[
                                :, :, bass.ds(t * TOK, TOK)]).then_inc(a_loaded[u], 16)
                    sp.dma_start(x[:, u], x_view[t]).then_inc(x_loaded[u], 16)

                load(0, 0)
                sp.dma_start(gain[:], ln_w).then_inc(ln_loaded, 16)
                sp.dma_start(shift[:], ln_b).then_inc(ln_loaded, 16)
                for k, w in enumerate(weights):
                    if k >= 2:
                        sp.wait_ge(w_ready, k - 1)
                    sp.dma_start(w_raw[:, k % 2], w.rearrange("(c p) n -> p c n", p=P)).then_inc(w_loaded[k % 2], 16)
                load(1, 1)

                def store_results(t, u, items):
                    for n in items:
                        wait_alone(sp, result_read, t * n_out + n + 1, waits_passed)
                        if n < n_v:
                            sp.dma_start(v_out[bass.ds(t * TOK + n * P, P), :], v_sb[:, n]).then_inc(v_stored[n], 16)
                        else:
                            k = n - n_v
                            to, group = qk[k // out_groups][1], k % out_groups
                            for part, src in ((0, r_high), (1, r_low)):
                                sp.dma_start(to[part, group * P:(group + 1) * P, bass.ds(t * TOK, TOK)],
                                             src[:, k % slots].bitcast(F32)).then_inc(stored[k % slots], 16)

                def tile_traffic(t, u, reload):
                    if x_out is not None:
                        wait_alone(sp, x_ready, SUB * (t + 1), waits_passed)
                        sp.dma_start(x_out.rearrange("(t s p) d -> t p s d", p=P, s=SUB)[t], x[:, u]).then_inc(
                            x_stored[u], 16)
                    if xn_out is not None:
                        wait_alone(sp, xt_ready, chunks * (t + 1), waits_passed)
                        for part, src in ((0, xt_high), (1, xt_low)):
                            sp.dma_start(xn_out[part].rearrange("(c p) t -> p c t", p=P)[:, :, bass.ds(t * TOK, TOK)],
                                         src[:, u].bitcast(F32)).then_inc(xt_stored[u], 16)
                    if reload:
                        wait_alone(sp, xn_ready, SUB * (t + 1), waits_passed)
                        if x_out is not None:
                            wait_alone(sp, x_stored[u], 16 * (t // 2 + 1), waits_passed)
                        if attn is not None:
                            wait_alone(sp, proj_done, SUB * (t + 1), waits_passed)
                        load(t + 2, u)
                    store_results(t, u, range(n_out))

                with sp.Fori(0, tiles // 2 - 1) as pair:
                    tile_traffic(2 * pair, 0, True)
                    tile_traffic(2 * pair + 1, 1, True)
                tile_traffic(tiles - 2, 0, False)
                tile_traffic(tiles - 1, 1, False)
                for u in range(2):
                    if x_out is not None:
                        sp.wait_ge(x_stored[u], 16 * tiles // 2)
                    if xn_out is not None:
                        sp.wait_ge(xt_stored[u], 32 * tiles // 2)
                for k in range(slots if n_qk else 0):
                    sp.wait_ge(stored[k], 32 * tiles * (n_qk // slots))
                for s in range(n_v):
                    sp.wait_ge(v_stored[s], 16 * tiles)

            @block.gpsimd
            def _(pool):
                make_identity(nc, pool, identity, ident_done)
                nc.gpsimd.memset(minus_half[:], -0.5).then_inc(ident_done, 1)
                pool.wait_ge(ident_done, 3)

                def inverse_root(t):
                    pool.wait_ge(var_done, 2 * (t + 1))
                    nc.gpsimd.tensor_tensor(rstd[:], var[:], minus_half[:], ALU.pow).then_inc(rstd_done, 1)

                with pool.Fori(0, tiles) as t:
                    inverse_root(t)

            @block.tensor
            def _(pe):
                def w_parts(k, c, cols):
                    return w_high[:, k, c, cols], w_low[:, k, c, cols]

                def project(t, u):
                    pe.wait_ge(a_loaded[u], 32 * (t // 2 + 1))
                    pe.wait_ge(w_ready, i_proj + 1)
                    for s in range(SUB):
                        if not (isinstance(t, int) and t == 0):
                            pe.wait_ge(xt_high_done, chunks * (t - 1) + s + 1)
                        cols = slice(s * P, (s + 1) * P)
                        for c in range(chunks):
                            mm = product(nc, turned[:, s], (a_high[:, u, c, cols], a_low[:, u, c, cols]),
                                         w_parts(i_proj, c, slice(0, dim)), c == 0, c == chunks - 1)
                        mm.then_inc(proj_done, 1)

                def turn(t, u):
                    for c in range(chunks):
                        if c == 0:
                            pe.wait_ge(xn_ready, SUB * (t + 1))
                        if proj_w is None and not (isinstance(t, int) and t == 0):
                            pe.wait_ge(xt_high_done, chunks * (t - 1) + c + 1)
                        for s in range(SUB):
                            mm = nc.tensor.transpose(turned[:, c, s * P:(s + 1) * P],
                                                     xn[:, u, s, c * P:(c + 1) * P], identity[:])
                        mm.then_inc(turn_done, 1)

                def results(t, u, items):
                    for n in items:
                        if not (isinstance(t, int) and t == 0 and n < 4):
                            pe.wait_ge(result_read, t * n_out + n - 3)
                        for c in range(chunks):
                            if n < n_v:
                                mm = product(nc, result[:, n % 4],
                                             (xt_high[:, u, c, n * P:(n + 1) * P], xt_low[:, u, c, n * P:(n + 1) * P]),
                                             w_parts(i_v, c, slice(0, dim)), c == 0, c == chunks - 1)
                            else:
                                k = n - n_v
                                group = k % out_groups
                                mm = product(nc, result[:, n % 4],
                                             w_parts(i_qk + k // out_groups, c, slice(group * P, (group + 1) * P)),
                                             (xt_high[:, u, c], xt_low[:, u, c]), c == 0, c == chunks - 1)
                        mm.then_inc(result_done, 1)

                def body(t, u, has_next):
                    if has_next and proj_w is not None:
                        project(t + 1, 1 - u)
                    if n_out:
                        pe.wait_ge(xt_ready, chunks * (t + 1))
                        if isinstance(t, int) and t == 0:
                            pe.wait_ge(w_ready, len(weights))
                        results(t, u, range(n_early))
                    if has_next:
                        turn(t + 1, 1 - u)
                    results(t, u, range(n_early, n_out))

                pe.wait_ge(ident_done, 2)
                if proj_w is not None:
                    project(0, 0)
                turn(0, 0)
                body(0, 0, True)
                body(1, 1, True)
                with pe.Fori(1, tiles // 2 - 1) as pair:
                    body(2 * pair, 0, True)
                    body(2 * pair + 1, 1, True)
                body(tiles - 2, 0, True)
                body(tiles - 1, 1, False)

            @block.scalar
            def _(act):
                def split_turned(t, u):
                    for c in range(chunks):
                        act.wait_ge(turn_done, chunks * t + c + 1)
                        if not (isinstance(t, int) and t == 0):
                            act.wait_ge(xt_ready, chunks * (t - 1) + c + 1)
                        nc.scalar.activation(xt[:, c], turned[:, c], ACT.Identity, bias=shift[:, c:c + 1],
                                             scale=gain[:, c:c + 1]).then_inc(xt_done, 1)
                        if xn_out is not None and not (isinstance(t, int) and t < 2):
                            act.wait_ge(xt_stored[u], 32 * (t // 2))
                        nc.scalar.activation(xt_high[:, u, c], turned[:, c], ACT.Identity, bias=shift[:, c:c + 1],
                                             scale=gain[:, c:c + 1]).then_inc(xt_high_done, 1)

                def high_parts(t, items):
                    for n in items:
                        if n < n_v:
                            continue
                        k = n - n_v
                        act.wait_ge(result_done, t * n_out + n + 1)
                        act.wait_ge(stored[k % slots], 32 * (t * (n_qk // slots) + k // slots))
                        nc.scalar.activation(r_high[:, k % slots], result[:, n % 4], ACT.Copy).then_inc(high_done, 1)

                for k in range(len(weights)):
                    act.wait_ge(w_loaded[k % 2], 16 * (k // 2 + 1))
                    nc.scalar.activation(w_high[:, k], w_raw[:, k % 2], ACT.Copy).then_inc(w_high_done, 1)
                act.wait_ge(ln_loaded, 32)

                def body(t, u, has_next):
                    high_parts(t, range(n_early))
                    if has_next:
                        split_turned(t + 1, 1 - u)
                    high_parts(t, range(n_early, n_out))

                split_turned(0, 0)
                body(0, 0, True)
                body(1, 1, True)
                with act.Fori(1, tiles // 2 - 1) as pair:
                    body(2 * pair, 0, True)
                    body(2 * pair + 1, 1, True)
                body(tiles - 2, 0, True)
                body(tiles - 1, 1, False)

            @block.vector
            def _(dve):
                def norm(t, u):
                    dve.wait_ge(x_loaded[u], 16 * (t // 2 + 1))
                    for s in range(SUB):
                        if proj_w is not None:
                            dve.wait_ge(proj_done, SUB * t + s + 1)
                            nc.vector.tensor_tensor(x[:, u, s], turned[:, s], x[:, u, s], ALU.add).then_inc(x_ready, 1)
                    if not (isinstance(t, int) and t == 0):
                        dve.wait_ge(xn_ready, SUB * t)

                    def stats_of(s):
                        if proj_w is not None:
                            dve.wait_ge(x_ready, SUB * t + s + 1)
                        return nc.vector.bn_stats(stats[:, s], x[:, u, s]).then_inc(stats_done, 1)

                    def moments_of(s):
                        nc.vector.bn_aggr(moments[:, s], stats[:, s]).then_inc(moments_done, 1)

                    def var_of(a, b):
                        dve.wait_ge(moments_done, SUB * t + b)
                        nc.vector.tensor_scalar(var[:, a:b], moments[:, a:b, 1], EPS, None, ALU.add).then_inc(var_done, 1)

                    half = SUB // 2
                    for s in range(half):
                        stats_of(s)
                    dve.wait_ge(stats_done, SUB * t + half)
                    for s in range(half, SUB):
                        stats_of(s)
                    for s in range(half):
                        moments_of(s)
                    dve.wait_ge(stats_done, SUB * (t + 1))
                    var_of(0, half)
                    for s in range(half, SUB):
                        moments_of(s)
                    var_of(half, SUB)
                    dve.wait_ge(rstd_done, t + 1)
                    for s in range(SUB):
                        nc.vector.tensor_scalar(xn[:, u, s], x[:, u, s], moments[:, s, 0:1], rstd[:, s:s + 1],
                                                ALU.subtract, ALU.mult).then_inc(xn_ready, 1)

                def low_turned(t, u):
                    for c in range(chunks):
                        dve.wait_ge(xt_high_done, chunks * t + c + 1)
                        nc.vector.tensor_tensor(xt_low[:, u, c], xt[:, c], xt_high[:, u, c].bitcast(F32),
                                                ALU.subtract).then_inc(xt_ready, 1)

                def low_parts(t, items):
                    for n in items:
                        if n < n_v:
                            dve.wait_ge(result_done, t * n_out + n + 1)
                            dve.wait_ge(v_stored[n], 16 * t)
                            nc.vector.tensor_copy(v_sb[:, n], result[:, n % 4]).then_inc(result_read, 1)
                        else:
                            k = n - n_v
                            dve.wait_ge(high_done, t * n_qk + k + 1)
                            nc.vector.tensor_tensor(r_low[:, k % slots], result[:, n % 4],
                                                    r_high[:, k % slots].bitcast(F32), ALU.subtract).then_inc(result_read, 1)

                def body(t, u, has_next):
                    if has_next:
                        norm(t + 1, 1 - u)
                    low_parts(t, range(n_early))
                    if has_next:
                        low_turned(t + 1, 1 - u)
                    low_parts(t, range(n_early, n_out))

                for k in range(len(weights)):
                    dve.wait_ge(w_high_done, k + 1)
                    nc.vector.tensor_tensor(w_low[:, k], w_raw[:, k % 2], w_high[:, k].bitcast(F32),
                                            ALU.subtract).then_inc(w_ready, 1)
                    if k == 0:
                        norm(0, 0)
                low_turned(0, 0)
                body(0, 0, True)
                body(1, 1, True)
                with dve.Fori(1, tiles // 2 - 1) as pair:
                    body(2 * pair, 0, True)
                    body(2 * pair + 1, 1, True)
                body(tiles - 2, 0, True)
                body(tiles - 1, 1, False)


def attention_phase(nc, name, q_t, k_t, v, out, keys, mask_rows=None):
    tokens = q_t.shape[2]
    batches = k_t.shape[2] // keys
    features = q_t.shape[1]
    groups_per_batch = features // P
    tiles_per_batch = tokens // batches // TOK
    groups = batches * groups_per_batch
    stages = groups * tiles_per_batch
    heads = HEADS_PER_GROUP
    scale = 1.0 / math.sqrt(HEAD_DIM)
    masked = mask_rows is not None
    base = 3 * HEAD_DIM
    score_rows = base + (2 if masked else 0)
    exp_rows = score_rows + 2
    n_k = -(-keys // P)
    width = keys // n_k
    assert width * n_k == keys
    sets = [list(range(k, min(k + 4, n_k))) for k in range(0, n_k, 4)]
    long = keys >= TOK
    if long:
        items = [(a, s, k0) for a in range(heads) for s in range(SUB) for k0 in range(0, keys, TOK)]
    else:
        items = [(a, s, 0) for a in range(heads) for s in range(0, SUB, 2)]
    n_items = len(items)
    per_head = n_items // heads
    n_reads = n_items + 1
    items_per_key_tile = -(-n_items // max(1, n_k - 3)) if long else n_items // n_k
    p_slots = 4 if long else n_k
    pairs = n_k // 2 if long else 0
    n_sums = pairs or n_k
    v_lag = 2 if long else 1
    sum_lag = 4 if long else 1

    with ExitStack() as stack:
        m = Memory(nc, stack, name)
        k_move = m.sbuf("k_move", [P, heads, keys], F32R)
        k_hold = m.sbuf("k_hold", [P, heads, keys], F32R)
        q_hold = m.sbuf("q_hold", [P, heads, TOK], F32R)
        q_move = m.sbuf("q_move", [P, 2, heads, TOK], F32R)
        v_sb = m.sbuf("v_sb", [P, n_k, P])
        expo = m.sbuf("expo", [P, p_slots, heads, TOK])
        pair_sum = m.sbuf("pair_sum", [P, 2, heads, TOK]) if pairs else None
        ones = m.sbuf("ones", [P, HEAD_DIM])
        identity = m.sbuf("identity", [P, P])
        part_max = m.sbuf("part_max", [P, heads * SUB, keys // TOK]) if long else None
        row_max = m.sbuf("row_max", [P, heads * SUB])
        max_high = m.sbuf("max_high", [heads * SUB, P], F32R)
        max_low = m.sbuf("max_low", [heads * SUB, P], F32R)
        inverse = m.sbuf("inverse", [P, TOK])
        mean = m.sbuf("mean", [P, TOK])
        mean_high = m.sbuf("mean_high", [P, TOK], F32R)
        mean_low = m.sbuf("mean_low", [P, TOK], F32R)
        first = m.psum("first", [P, 2, TOK])
        second = m.psum("second", [P, 4, TOK])
        weighted = m.psum("weighted", [P, TOK])
        total = m.psum("total", [P, TOK])

        ident_done = m.sem("ident_done")
        constant_rows = m.sem("constant_rows")
        k_move_loaded = [m.sem(f"k_move_loaded{a}") for a in range(heads)]
        k_hold_loaded = [m.sem(f"k_hold_loaded{j}") for j in range(len(sets))]
        v_loaded = [m.sem(f"v_loaded{j}") for j in range(len(sets))]
        q_hold_loaded = [m.sem(f"q_hold_loaded{a}") for a in range(heads)]
        q_move_loaded = m.sem("q_move_loaded")
        max_loaded = m.sem("max_loaded")
        first_done = m.sem("first_done")
        first_read = m.sem("first_read")
        row_max_done = m.sem("row_max_done")
        turned = m.sem("turned")
        max_high_done = m.sem("max_high_done")
        second_done = m.sem("second_done")
        exp_done = m.sem("exp_done")
        pair_done = m.sem("pair_done")
        weighted_done = m.sem("weighted_done")
        total_done = m.sem("total_done")
        inverse_done = m.sem("inverse_done")
        mean_done = m.sem("mean_done")
        mean_high_done = m.sem("mean_high_done")
        mean_ready = m.sem("mean_ready")
        out_stored = m.sem("out_stored")
        waits_passed = m.sem("waits_passed")

        def ge(eng, sem, value, alone=False):
            if isinstance(value, int) and value <= 0:
                return
            if alone and not isinstance(value, int):
                wait_alone(eng, sem, value, waits_passed)
            else:
                eng.wait_ge(sem, value)

        k_move_count = 16 * (3 + masked)
        k_hold_count = 16 * (3 + masked)

        with nc.Block() as block:

            @block.sync
            def _(sp):
                def stacked(dst, src, parts, rows, cols, sem):
                    for j, part in enumerate(parts):
                        sp.dma_start(dst[j * HEAD_DIM:(j + 1) * HEAD_DIM].bitcast(F32),
                                     src[part, rows, cols].rearrange("(a d) t -> d a t", d=HEAD_DIM)).then_inc(sem, 16)

                def group_of(g):
                    return g // groups_per_batch, g % groups_per_batch

                def load_k_move(g, a):
                    b, group = group_of(g)
                    stacked(k_move[:, a:a + 1], k_t, (0, 0, 1), bass.ds(group * P + a * HEAD_DIM, HEAD_DIM),
                            bass.ds(b * keys, keys), k_move_loaded[a])
                    if masked:
                        sp.dma_start(k_move[base:base + 2, a].bitcast(F32), mask_rows[b]).then_inc(k_move_loaded[a], 16)

                def load_k_hold(g, j):
                    b, group = group_of(g)
                    k0, n = sets[j][0] * width, len(sets[j]) * width
                    stacked(k_hold[:, :, k0:k0 + n], k_t, (0, 0, 1), bass.ds(group * P, P),
                            bass.ds(b * keys + k0, n), k_hold_loaded[j])
                    if masked:
                        sp.dma_start(k_hold[base:base + 2, :, k0:k0 + n].bitcast(F32),
                                     mask_rows[b, :, k0:k0 + n].unsqueeze(1).to_broadcast([2, heads, n])
                                     ).then_inc(k_hold_loaded[j], 16)

                def load_v(g, j):
                    b, group = group_of(g)
                    k0, n = sets[j][0], len(sets[j])
                    sp.dma_start(v_sb[0:width, k0:k0 + n],
                                 v[bass.ds(b * keys + k0 * width, n * width), bass.ds(group * P, P)]
                                 .rearrange("(k p) d -> p k d", p=width)).then_inc(v_loaded[j], 16)

                def query_slice(i):
                    g = i // tiles_per_batch
                    b, group = group_of(g)
                    return group, bass.ds(b * (tiles_per_batch * TOK) + (i % tiles_per_batch) * TOK, TOK)

                def load_q_hold(i, a):
                    group, cols = query_slice(i)
                    stacked(q_hold[:, a:a + 1], q_t, (0, 1, 0), bass.ds(group * P + a * HEAD_DIM, HEAD_DIM), cols,
                            q_hold_loaded[a])

                def load_q_move(i):
                    group, cols = query_slice(i)
                    stacked(q_move[:, i % 2], q_t, (0, 1, 0), bass.ds(group * P, P), cols, q_move_loaded)

                def load_max(i):
                    ge(sp, first_read, n_reads * (i + 1), alone=True)
                    for row, src in ((score_rows, max_high), (score_rows + 1, max_low)):
                        sp.dma_start(q_move[row:row + 1, i % 2].rearrange("o a (s t) -> o (a s) t", t=P).bitcast(F32),
                                     src[:].bitcast(F32)).then_inc(max_loaded, 16)

                def store_out(i):
                    ge(sp, mean_ready, i + 1, alone=True)
                    group, cols = query_slice(i)
                    for part, src in ((0, mean_high), (1, mean_low)):
                        sp.dma_start(out[part, bass.ds(group * P, P), cols], src[:].bitcast(F32)).then_inc(out_stored, 16)

                def stage(i, g, qt):
                    last = isinstance(i, int) and i == stages - 1
                    last2 = isinstance(i, int) and i >= stages - 2
                    new_next = qt == tiles_per_batch - 1 and not last
                    new_after = qt == tiles_per_batch - 2 and not last2
                    load_max(i)
                    if qt == 0 and not (isinstance(g, int) and g == 0):
                        ge(sp, weighted_done, n_k * i, alone=True)
                        load_v(g, len(sets) - 1)
                    if not last:
                        ge(sp, second_done, heads * n_k * i, alone=True)
                        ge(sp, q_move_loaded, 48 * (i + 1), alone=True)
                        load_q_move(i + 1)
                    if not (isinstance(i, int) and i == 0):
                        store_out(i - 1)
                    for j in range(max(heads, len(sets))):
                        if not last2 and j < heads:
                            ge(sp, first_done, n_items * (i + 1) + per_head * (j + 1), alone=True)
                            load_q_hold(i + 2, j)
                            if new_after:
                                load_k_move(g + 1, j)
                        if new_next and j < len(sets):
                            ge(sp, second_done, heads * (n_k * i + sets[j][-1] + 1), alone=True)
                            load_k_hold(g + 1, j)
                            if j > 0:
                                ge(sp, weighted_done, n_k * i + sets[j - 1][-1] + 1, alone=True)
                                load_v(g + 1, j - 1)

                sp.wait_ge(constant_rows, 4 + 2 * masked)
                for a in range(heads):
                    load_q_hold(0, a)
                    load_k_move(0, a)
                for j in range(len(sets)):
                    load_k_hold(0, j)
                    load_v(0, j)
                load_q_move(0)
                for a in range(heads):
                    sp.wait_ge(first_done, per_head * (a + 1))
                    load_q_hold(1, a)
                for qt in range(tiles_per_batch):
                    stage(qt, 0, qt)
                with sp.Fori(1, groups - 1) as g:
                    for qt in range(tiles_per_batch):
                        stage(g * tiles_per_batch + qt, g, qt)
                for qt in range(tiles_per_batch):
                    stage((groups - 1) * tiles_per_batch + qt, groups - 1, qt)
                store_out(stages - 1)
                sp.wait_ge(out_stored, 32 * stages)

            @block.gpsimd
            def _(pool):
                make_identity(nc, pool, identity, ident_done)
                def add_pairs(i):
                    for k in range(pairs):
                        ge(pool, exp_done, heads * (n_k * i + 2 * k + 2))
                        ge(pool, total_done, pairs * i + k - 1)
                        nc.gpsimd.tensor_tensor(pair_sum[:, k % 2], expo[:, 2 * k % p_slots],
                                                expo[:, (2 * k + 1) % p_slots], ALU.add).then_inc(pair_done, 1)

                if pairs:
                    add_pairs(0)
                    with pool.Fori(1, stages) as i:
                        add_pairs(i)

            @block.tensor
            def _(pe):
                def first_pass(i, n):
                    a, s, k0 = items[n]
                    if n % per_head == 0:
                        ge(pe, q_hold_loaded[a], 48 * (i + 1))
                        ge(pe, k_move_loaded[a], k_move_count * (i // tiles_per_batch + 1))
                    ge(pe, first_read, n_reads * i + (n - 1 if n > 1 else 0))
                    if long:
                        mm = nc.tensor.matmul(first[:, n % 2], q_hold[0:score_rows, a, s * P:(s + 1) * P],
                                              k_move[0:score_rows, a, k0:k0 + TOK], start=True, stop=True)
                    else:
                        for part in range(2):
                            mm = nc.tensor.matmul(first[:, n % 2, part * keys:(part + 1) * keys],
                                                  q_hold[0:score_rows, a, (s + part) * P:(s + part + 1) * P],
                                                  k_move[0:score_rows, a], start=True, stop=True)
                    mm.then_inc(first_done, 1)

                def turn_max(i):
                    ge(pe, row_max_done, i + 1)
                    nc.tensor.transpose(first[0:heads * SUB, 0, 0:P], row_max[:], identity[:]).then_inc(turned, 1)

                def second_pass(i, k, a):
                    n = heads * k + a
                    if a == 0:
                        for j, tiles in enumerate(sets):
                            if k == tiles[0]:
                                ge(pe, k_hold_loaded[j], k_hold_count * (i // tiles_per_batch + 1))
                    if k == 0 and a == 0:
                        ge(pe, q_move_loaded, 48 * (i + 1))
                        ge(pe, max_loaded, 32 * (i + 1))
                    ge(pe, exp_done, heads * n_k * i + n - 3)
                    nc.tensor.matmul(second[0:width, n % 4], k_hold[0:exp_rows, a, k * width:(k + 1) * width],
                                     q_move[0:exp_rows, i % 2, a], start=True, stop=True).then_inc(second_done, 1)

                def weigh(i, k):
                    for j, tiles in enumerate(sets):
                        if k == tiles[0]:
                            ge(pe, v_loaded[j], 16 * (i // tiles_per_batch + 1))
                    if k == 0:
                        ge(pe, mean_done, i)
                    for a in range(heads):
                        ge(pe, exp_done, heads * (n_k * i + k) + a + 1)
                        cols = slice(a * HEAD_DIM, (a + 1) * HEAD_DIM)
                        mm = nc.tensor.matmul(weighted[cols], v_sb[0:width, k, cols], expo[0:width, k % p_slots, a],
                                              start=k == 0, stop=k == n_k - 1)
                    mm.then_inc(weighted_done, 1)

                def add_up(i, k):
                    if k == 0:
                        ge(pe, inverse_done, i)
                    if pairs:
                        ge(pe, pair_done, pairs * i + k + 1)
                    for a in range(heads):
                        cols = slice(a * HEAD_DIM, (a + 1) * HEAD_DIM)
                        src = pair_sum[0:width, k % 2, a] if pairs else expo[0:width, k % p_slots, a]
                        mm = nc.tensor.matmul(total[cols], ones[0:width], src, start=k == 0, stop=k == n_sums - 1)
                    mm.then_inc(total_done, 1)

                due = [[] for _ in range(n_k + sum_lag)]
                for k in range(n_k):
                    due[k + v_lag].append((weigh, k))
                for k in range(n_sums):
                    at = (2 * k if pairs else k) + sum_lag
                    due[min(at, n_k + v_lag - 1)].append((add_up, k))

                def stage(i, with_last, with_next):
                    n = 0
                    for k in range(n_k):
                        for a in range(heads):
                            second_pass(i, k, a)
                            todo = items_per_key_tile // heads + (1 if a < items_per_key_tile % heads else 0)
                            if with_next and n < n_items:
                                for _ in range(min(todo, n_items - n)):
                                    first_pass(i + 1, n)
                                    n += 1
                                if n == n_items:
                                    pass
                        if with_next and n >= n_items and n < 10 ** 6:
                            turn_max(i + 1)
                            n = 10 ** 6
                        if with_last and k + n_k < len(due):
                            for what, j in due[k + n_k]:
                                what(i - 1, j)
                        for what, j in due[k]:
                            what(i, j)

                pe.wait_ge(ident_done, 2)
                pe.wait_ge(constant_rows, 4 + 2 * masked)
                for n in range(n_items):
                    first_pass(0, n)
                turn_max(0)
                stage(0, False, True)
                with pe.Fori(1, stages - 1) as i:
                    stage(i, True, True)
                stage(stages - 1, True, False)
                for k in range(n_k, len(due)):
                    for what, j in due[k]:
                        what(stages - 1, j)

            @block.scalar
            def _(act):
                def exponentials(i):
                    for k in range(n_k):
                        if pairs:
                            ge(act, weighted_done, n_k * i + k - p_slots + 1)
                            if k % 2 == 0:
                                ge(act, pair_done, pairs * i + (k - p_slots) // 2 + 1)
                        else:
                            ge(act, weighted_done, n_k * i + k - p_slots + 1)
                            ge(act, total_done, n_k * i + k - p_slots + 1)
                        for a in range(heads):
                            n = heads * k + a
                            ge(act, second_done, heads * n_k * i + n + 1)
                            nc.scalar.activation(expo[0:width, k % p_slots, a], second[0:width, n % 4], ACT.Exp,
                                                 scale=scale).then_inc(exp_done, 1)

                exponentials(0)
                with act.Fori(1, stages) as i:
                    exponentials(i)

            @block.vector
            def _(dve):
                for par in range(2):
                    nc.vector.memset(q_move[base:base + 4, par].bitcast(F32), 1.0).then_inc(constant_rows, 1)
                nc.vector.memset(k_hold[base:base + 4].bitcast(F32), -1.0).then_inc(constant_rows, 1)
                nc.vector.memset(ones[:], 1.0).then_inc(constant_rows, 1)
                if masked:
                    nc.vector.memset(q_hold[base:base + 4].bitcast(F32), 1.0).then_inc(constant_rows, 1)
                    nc.vector.memset(k_move[base:base + 4].bitcast(F32), 0.0).then_inc(constant_rows, 1)

                def maxima(i, some):
                    for n in some:
                        a, s, k0 = items[n]
                        ge(dve, first_done, n_items * i + n + 1)
                        if n == 0 and long:
                            ge(dve, row_max_done, i)
                        if n == 0 and not long:
                            ge(dve, turned, i)
                        if long:
                            nc.vector.tensor_reduce(part_max[:, a * SUB + s, k0 // TOK:k0 // TOK + 1], first[:, n % 2],
                                                    AX_X, ALU.max).then_inc(first_read, 1)
                        else:
                            nc.vector.tensor_reduce(
                                row_max[:, a * SUB + s:a * SUB + s + 2],
                                first[:, n % 2, 0:2 * keys].rearrange("p (s k) -> p s k", k=keys),
                                AX_X, ALU.max).then_inc(first_read if n < n_items - 1 else row_max_done, 1)

                def split_max(i):
                    if long:
                        ge(dve, first_read, n_reads * i + n_items)
                        ge(dve, turned, i)
                        nc.vector.tensor_reduce(row_max[:], part_max[:], AX_X, ALU.max).then_inc(row_max_done, 1)
                    ge(dve, max_loaded, 32 * i)
                    ge(dve, turned, i + 1)
                    nc.vector.tensor_copy(max_high[:], first[0:heads * SUB, 0, 0:P]).then_inc(max_high_done, 1)
                    ge(dve, max_high_done, i + 1)
                    nc.vector.tensor_tensor(max_low[:], first[0:heads * SUB, 0, 0:P], max_high[:].bitcast(F32),
                                            ALU.subtract).then_inc(first_read, 1 if long else 2)

                def divide(i):
                    ge(dve, total_done, n_sums * (i + 1))
                    ge(dve, weighted_done, n_k * (i + 1))
                    ge(dve, mean_done, i)
                    nc.vector.reciprocal(inverse[:], total[:]).then_inc(inverse_done, 1)
                    ge(dve, inverse_done, i + 1)
                    ge(dve, mean_ready, i)
                    nc.vector.tensor_tensor(mean[:], weighted[:], inverse[:], ALU.mult).then_inc(mean_done, 1)
                    ge(dve, mean_done, i + 1)
                    ge(dve, out_stored, 32 * i)
                    nc.vector.tensor_copy(mean_high[:], mean[:]).then_inc(mean_high_done, 1)
                    ge(dve, mean_high_done, i + 1)
                    nc.vector.tensor_tensor(mean_low[:], mean[:], mean_high[:].bitcast(F32),
                                            ALU.subtract).then_inc(mean_ready, 1)

                before = min(n_items, 2 * items_per_key_tile)

                maxima(0, range(n_items))
                split_max(0)
                maxima(1, range(n_items))
                split_max(1)
                with dve.Fori(1, stages - 1) as i:
                    maxima(i + 1, range(before))
                    divide(i - 1)
                    maxima(i + 1, range(before, n_items))
                    split_max(i + 1)
                divide(stages - 2)
                divide(stages - 1)


def context_phase(nc, ctx_t, mask, k_w, v_w, k_t, v, mask_rows):
    dim, keys = ctx_t.shape
    batches, batch_keys = mask.shape
    chunks = dim // P
    pieces = next(n for n in range(-(-keys // P), keys) if keys % n == 0)
    piece = keys // pieces
    assert keys <= TOK

    with ExitStack() as stack:
        m = Memory(nc, stack, "context")
        raw = m.sbuf("raw", [P, 2, chunks, dim])
        w_high = m.sbuf("w_high", [P, 2, chunks, dim], F32R)
        w_low = m.sbuf("w_low", [P, 2, chunks, dim], F32R)
        c_raw = m.sbuf("c_raw", [P, chunks, keys])
        c_high = m.sbuf("c_high", [P, chunks, keys], F32R)
        c_low = m.sbuf("c_low", [P, chunks, keys], F32R)
        k_high = m.sbuf("k_high", [P, chunks, keys], F32R)
        k_low = m.sbuf("k_low", [P, chunks, keys], F32R)
        v_sb = m.sbuf("v_sb", [P, pieces, dim])
        mask_raw = m.sbuf("mask_raw", [batches, batch_keys], I32)
        bias = m.sbuf("bias", [batches, batch_keys])
        bias_high = m.sbuf("bias_high", [batches, batch_keys], F32R)
        bias_low = m.sbuf("bias_low", [batches, batch_keys], F32R)
        result = m.psum("result", [P, 4 + pieces, TOK])

        c_loaded = m.sem("c_loaded")
        mask_loaded = m.sem("mask_loaded")
        w_loaded = [m.sem(f"w_loaded{k}") for k in range(2)]
        high_done = m.sem("high_done")
        split_done = m.sem("split_done")
        bias_done = m.sem("bias_done")
        product_done = m.sem("product_done")
        k_high_done = m.sem("k_high_done")
        result_ready = m.sem("result_ready")
        stored = m.sem("stored")

        with nc.Block() as block:

            @block.sync
            def _(sp):
                sp.dma_start(c_raw[:], ctx_t.rearrange("(c p) t -> p c t", p=P)).then_inc(c_loaded, 16)
                for k, w in enumerate((k_w, v_w)):
                    sp.dma_start(raw[:, k], w.rearrange("(c p) n -> p c n", p=P)).then_inc(w_loaded[k], 16)
                sp.dma_start(mask_raw[:], mask).then_inc(mask_loaded, 16)
                sp.wait_ge(bias_done, 4)
                for part, src in ((0, bias_high), (1, bias_low)):
                    sp.dma_start(mask_rows[:, part], src[:].bitcast(F32)).then_inc(stored, 16)
                for g in range(chunks):
                    sp.wait_ge(result_ready, g + 1)
                    for part, src in ((0, k_high), (1, k_low)):
                        sp.dma_start(k_t[part, g * P:(g + 1) * P, :], src[:, g].bitcast(F32)).then_inc(stored, 16)
                for n in range(pieces):
                    sp.wait_ge(result_ready, chunks + n + 1)
                    sp.dma_start(v[n * piece:(n + 1) * piece, :], v_sb[0:piece, n]).then_inc(stored, 16)
                sp.wait_ge(stored, 16 * (2 + 2 * chunks + pieces))

            @block.scalar
            def _(act):
                act.wait_ge(c_loaded, 16)
                nc.scalar.activation(c_high[:], c_raw[:], ACT.Copy).then_inc(high_done, 1)
                for k in range(2):
                    act.wait_ge(w_loaded[k], 16)
                    nc.scalar.activation(w_high[:, k], raw[:, k], ACT.Copy).then_inc(high_done, 1)
                for g in range(chunks):
                    act.wait_ge(product_done, g + 1)
                    nc.scalar.activation(k_high[:, g], result[:, g, 0:keys], ACT.Copy).then_inc(k_high_done, 1)

            @block.vector
            def _(dve):
                dve.wait_ge(high_done, 1)
                nc.vector.tensor_tensor(c_low[:], c_raw[:], c_high[:].bitcast(F32), ALU.subtract).then_inc(split_done, 1)
                for k in range(2):
                    dve.wait_ge(high_done, k + 2)
                    nc.vector.tensor_tensor(w_low[:, k], raw[:, k], w_high[:, k].bitcast(F32),
                                            ALU.subtract).then_inc(split_done, 1)
                dve.wait_ge(mask_loaded, 16)
                nc.vector.tensor_scalar(bias[:], mask_raw[:], -1.0, 1.0, ALU.mult, ALU.add).then_inc(bias_done, 1)
                dve.wait_ge(bias_done, 1)
                nc.vector.tensor_scalar(bias[:], bias[:], MASK_BIAS * math.sqrt(HEAD_DIM), None,
                                        ALU.mult).then_inc(bias_done, 1)
                dve.wait_ge(bias_done, 2)
                nc.vector.tensor_copy(bias_high[:], bias[:]).then_inc(bias_done, 1)
                dve.wait_ge(bias_done, 3)
                nc.vector.tensor_tensor(bias_low[:], bias[:], bias_high[:].bitcast(F32), ALU.subtract).then_inc(bias_done, 1)
                for g in range(chunks):
                    dve.wait_ge(k_high_done, g + 1)
                    nc.vector.tensor_tensor(k_low[:, g], result[:, g, 0:keys], k_high[:, g].bitcast(F32),
                                            ALU.subtract).then_inc(result_ready, 1)
                for n in range(pieces):
                    dve.wait_ge(product_done, chunks + n + 1)
                    nc.vector.tensor_copy(v_sb[0:piece, n], result[0:piece, chunks + n]).then_inc(result_ready, 1)

            @block.tensor
            def _(pe):
                pe.wait_ge(split_done, 2)
                for g in range(chunks):
                    for c in range(chunks):
                        cols = slice(g * P, (g + 1) * P)
                        mm = product(nc, result[:, g, 0:keys], (w_high[:, 0, c, cols], w_low[:, 0, c, cols]),
                                     (c_high[:, c], c_low[:, c]), c == 0, c == chunks - 1)
                    mm.then_inc(product_done, 1)
                pe.wait_ge(split_done, 3)
                for n in range(pieces):
                    for c in range(chunks):
                        cols = slice(n * piece, (n + 1) * piece)
                        mm = product(nc, result[0:piece, chunks + n], (c_high[:, c, cols], c_low[:, c, cols]),
                                     (w_high[:, 1, c], w_low[:, 1, c]), c == 0, c == chunks - 1)
                    mm.then_inc(product_done, 1)


def mlp_phase(nc, x_in, xn, w1, b1, w2, b2, out):
    dim, hidden = w1.shape
    tiles = x_in.shape[0] // TOK
    chunks = dim // P
    steps = hidden // P
    lag = 2
    per_set = 4
    sets = steps // per_set
    ring = 4
    slots = 2

    with ExitStack() as stack:
        m = Memory(nc, stack, "mlp")
        raw = m.sbuf("raw", [P, 2, per_set, dim])
        w1_high = m.sbuf("w1_high", [P, sets, chunks, per_set * P], F32R)
        w1_low = m.sbuf("w1_low", [P, sets, chunks, per_set * P], F32R)
        w2_high = m.sbuf("w2_high", [P, sets, per_set, dim], F32R)
        w2_low = m.sbuf("w2_low", [P, sets, per_set, dim], F32R)
        b1_col = m.sbuf("b1_col", [P, steps])
        b2_row = m.sbuf("b2_row", [P, dim])
        xt_high = m.sbuf("xt_high", [P, 2, chunks, TOK], F32R)
        xt_low = m.sbuf("xt_low", [P, 2, chunks, TOK], F32R)
        x = m.sbuf("x", [P, 2, SUB, dim])
        h = m.sbuf("h", [P, 2, TOK])
        h_high = m.sbuf("h_high", [P, slots, TOK], F32R)
        h_low = m.sbuf("h_low", [P, slots, TOK], F32R)
        hidden_sum = m.psum("hidden_sum", [P, ring, TOK])
        out_sum = m.psum("out_sum", [P, SUB, TOK])

        w_loaded = [m.sem(f"w_loaded{k}") for k in range(2)]
        w_high_done = m.sem("w_high_done")
        w_ready = m.sem("w_ready")
        bias_loaded = m.sem("bias_loaded")
        xn_loaded = [m.sem(f"xn_loaded{u}") for u in range(2)]
        x_loaded = [m.sem(f"x_loaded{u}") for u in range(2)]
        hidden_done = m.sem("hidden_done")
        gelu_done = m.sem("gelu_done")
        h_high_done = m.sem("h_high_done")
        h_ready = m.sem("h_ready")
        h_used = m.sem("h_used")
        bias_added = m.sem("bias_added")
        out_done = m.sem("out_done")
        stored = [m.sem(f"stored{u}") for u in range(2)]
        waits_passed = m.sem("waits_passed")

        def in_pairs(eng, body):
            body(0, 0)
            body(1, 1)
            with eng.Fori(1, tiles // 2 - 1) as pair:
                body(2 * pair, 0)
                body(2 * pair + 1, 1)
            body(tiles - 2, 0)
            body(tiles - 1, 1)

        with nc.Block() as block:

            @block.sync
            def _(sp):
                x_view = x_in.rearrange("(t s p) d -> t p s d", p=P, s=SUB)
                out_view = out.rearrange("(t s p) d -> t p s d", p=P, s=SUB)

                def load(t, u):
                    for part, to in ((0, xt_high), (1, xt_low)):
                        sp.dma_start(to[:, u].bitcast(F32), xn[part].rearrange("(c p) t -> p c t", p=P)[
                            :, :, bass.ds(t * TOK, TOK)]).then_inc(xn_loaded[u], 16)
                    sp.dma_start(x[:, u], x_view[t]).then_inc(x_loaded[u], 16)

                def load_set(k):
                    j = k // 2
                    if k >= 2:
                        sp.wait_ge(w_ready, k - 1)
                    if k % 2 == 0:
                        src = w1.rearrange("(c p) n -> p c n", p=P)[:, :, j * per_set * P:(j + 1) * per_set * P]
                    else:
                        src = w2.rearrange("(k p) n -> p k n", p=P)[:, j * per_set:(j + 1) * per_set]
                    sp.dma_start(raw[:, k % 2], src).then_inc(w_loaded[k % 2], 16)

                load_set(0)
                sp.dma_start(b1_col[:], b1).then_inc(bias_loaded, 16)
                sp.dma_start(b2_row[:], b2.unsqueeze(0).to_broadcast([P, dim])).then_inc(bias_loaded, 16)
                load(0, 0)
                for k in range(1, 2 * sets):
                    load_set(k)
                load(1, 1)

                def traffic(t, u):
                    wait_alone(sp, out_done, SUB * (t + 1), waits_passed)
                    sp.dma_start(out_view[t], x[:, u]).then_inc(stored[u], 16)
                    if not (isinstance(t, int) and t >= tiles - 2):
                        wait_alone(sp, stored[u], 16 * (t // 2 + 1), waits_passed)
                        load(t + 2, u)

                in_pairs(sp, traffic)
                for u in range(2):
                    sp.wait_ge(stored[u], 16 * tiles // 2)

            @block.tensor
            def _(pe):
                def first_product(t, u, j):
                    if j == 0:
                        pe.wait_ge(xn_loaded[u], 32 * (t // 2 + 1))
                    if isinstance(t, int) and t == 0 and j % per_set == 0:
                        pe.wait_ge(w_ready, 2 * (j // per_set) + 1)
                    if not (isinstance(t, int) and t == 0 and j < ring):
                        pe.wait_ge(gelu_done, steps * t + j - ring + 1)
                    cols = slice(j % per_set * P, (j % per_set + 1) * P)
                    for c in range(chunks):
                        mm = product(nc, hidden_sum[:, j % ring],
                                     (w1_high[:, j // per_set, c, cols], w1_low[:, j // per_set, c, cols]),
                                     (xt_high[:, u, c], xt_low[:, u, c]), c == 0, c == chunks - 1)
                    mm.then_inc(hidden_done, 1)

                def second_product(t, j):
                    if isinstance(t, int) and t == 0 and j % per_set == 0:
                        pe.wait_ge(w_ready, 2 * (j // per_set) + 2)
                    pe.wait_ge(h_ready, steps * t + j + 1)
                    for s in range(SUB):
                        if j == 0 and not (isinstance(t, int) and t == 0):
                            pe.wait_ge(out_done, SUB * (t - 1) + s + 1)
                        cols = slice(s * P, (s + 1) * P)
                        mm = product(nc, out_sum[:, s], (h_high[:, j % slots, cols], h_low[:, j % slots, cols]),
                                     (w2_high[:, j // per_set, j % per_set], w2_low[:, j // per_set, j % per_set]),
                                     j == 0, j == steps - 1)
                    mm.then_inc(h_used, 1)

                def tile(t, u):
                    for j in range(steps):
                        first_product(t, u, j)
                        if j >= lag:
                            second_product(t, j - lag)
                        elif not (isinstance(t, int) and t == 0):
                            second_product(t - 1, steps - lag + j)

                in_pairs(pe, tile)
                for j in range(steps - lag, steps):
                    second_product(tiles - 1, j)

            @block.scalar
            def _(act):
                def gelu(t, j):
                    act.wait_ge(hidden_done, steps * t + j + 1)
                    if not (isinstance(t, int) and t == 0 and j < 2):
                        act.wait_ge(h_ready, steps * t + j - 1)
                    nc.scalar.activation(h[:, j % 2], hidden_sum[:, j % ring], ACT.Gelu,
                                         bias=b1_col[:, j:j + 1]).then_inc(gelu_done, 1)

                def split_high(k):
                    act.wait_ge(w_loaded[k % 2], 16 * (k // 2 + 1))
                    to = w1_high if k % 2 == 0 else w2_high
                    nc.scalar.activation(to[:, k // 2], raw[:, k % 2], ACT.Copy).then_inc(w_high_done, 1)

                def tile(t, u):
                    for j in range(steps):
                        gelu(t, j)

                for k in range(2 * sets):
                    split_high(k)
                act.wait_ge(bias_loaded, 32)
                in_pairs(act, tile)

            @block.vector
            def _(dve):
                def split_h(t, j):
                    dve.wait_ge(gelu_done, steps * t + j + 1)
                    if not (isinstance(t, int) and t == 0 and j < slots):
                        dve.wait_ge(h_used, steps * t + j - slots + 1)
                    nc.vector.tensor_copy(h_high[:, j % slots], h[:, j % 2]).then_inc(h_high_done, 1)
                    dve.wait_ge(h_high_done, steps * t + j + 1)
                    nc.vector.tensor_tensor(h_low[:, j % slots], h[:, j % 2], h_high[:, j % slots].bitcast(F32),
                                            ALU.subtract).then_inc(h_ready, 1)

                def add_bias(t, u):
                    dve.wait_ge(x_loaded[u], 16 * (t // 2 + 1))
                    for s in range(SUB):
                        nc.vector.tensor_tensor(x[:, u, s], x[:, u, s], b2_row[:], ALU.add).then_inc(bias_added, 1)

                def finish(t, u):
                    dve.wait_ge(h_used, steps * (t + 1))
                    dve.wait_ge(bias_added, SUB * (t + 1))
                    for s in range(SUB):
                        nc.vector.tensor_tensor(x[:, u, s], out_sum[:, s], x[:, u, s], ALU.add).then_inc(out_done, 1)

                def tile(t, u):
                    for j in range(steps):
                        split_h(t, j)
                        if j == lag - 1 and not (isinstance(t, int) and t == 0):
                            finish(t - 1, 1 - u)
                        if j == lag + 1:
                            add_bias(t, u)

                for k in range(2 * sets):
                    dve.wait_ge(w_high_done, k + 1)
                    high, low = (w1_high, w1_low) if k % 2 == 0 else (w2_high, w2_low)
                    nc.vector.tensor_tensor(low[:, k // 2], raw[:, k % 2], high[:, k // 2].bitcast(F32),
                                            ALU.subtract).then_inc(w_ready, 1)
                dve.wait_ge(bias_loaded, 32)
                in_pairs(dve, tile)
                finish(tiles - 1, 1)


def transformer_block(nc, x, ctx_t, mask, ln0_w, ln0_b, wq, wk, wv, sa_w, ln1_w, ln1_b, cq_w, ck_w, cv_w, ca_w,
                      ln2_w, ln2_b, fc1_w, fc1_b, fc2_w, fc2_b, out):
    tokens, dim = x.shape
    batches, batch_keys = mask.shape

    def scratch(name, shape):
        return nc.dram_tensor(name, shape, F32, kind="Internal").ap()

    q_t = scratch("q_t", [2, dim, tokens])
    k_t = scratch("k_t", [2, dim, tokens])
    v = scratch("v", [tokens, dim])
    self_t = scratch("self_t", [2, dim, tokens])
    x1 = scratch("x1", [tokens, dim])
    cq_t = scratch("cq_t", [2, dim, tokens])
    ck_t = scratch("ck_t", [2, dim, batches * batch_keys])
    cv = scratch("cv", [batches * batch_keys, dim])
    mask_rows = scratch("mask_rows", [batches, 2, batch_keys])
    cross_t = scratch("cross_t", [2, dim, tokens])
    x2 = scratch("x2", [tokens, dim])
    xn_t = scratch("xn_t", [2, dim, tokens])

    token_phase(nc, "qkv", x, ln0_w, ln0_b, v_w=wv, v_out=v, qk=[(wq, q_t), (wk, k_t)])
    attention_phase(nc, "self", q_t, k_t, v, self_t, tokens // batches)
    context_phase(nc, ctx_t, mask, ck_w, cv_w, ck_t, cv, mask_rows)
    token_phase(nc, "mid", x, ln1_w, ln1_b, attn=self_t, proj_w=sa_w, x_out=x1, qk=[(cq_w, cq_t)])
    attention_phase(nc, "cross", cq_t, ck_t, cv, cross_t, batch_keys, mask_rows)
    token_phase(nc, "late", x1, ln2_w, ln2_b, attn=cross_t, proj_w=ca_w, x_out=x2, xn_out=xn_t)
    mlp_phase(nc, x2, xn_t, fc1_w, fc1_b, fc2_w, fc2_b, out)


def kernel(**inputs):
    import numpy as np
    import concourse.bacc as bacc
    from concourse.bass_utils import run_bass_kernel_spmd

    def arr(name):
        return np.asarray(inputs[name])

    def turned(a):
        return np.ascontiguousarray(a.T)

    def columns(a):
        return np.ascontiguousarray(a.reshape(-1, P).T)

    x = arr("x")
    batches, length, dim = x.shape
    w = {k: arr(f"L0_xattn_{k}") for k in ("ln0_w", "ln0_b", "qkv_w", "sa_proj_w", "ln1_w", "ln1_b", "q_w", "k_w", "v_w",
                                           "ca_proj_w", "ln2_w", "ln2_b", "fc1_w", "fc1_b", "fc2_w", "fc2_b")}
    arrays = {
        "x": np.ascontiguousarray(x.reshape(batches * length, dim)),
        "ctx_t": turned(arr("ctx_1024").reshape(-1, dim)),
        "mask": np.ascontiguousarray(arr("mask_BxS2_ik0")),
        "ln0_w": columns(w["ln0_w"]), "ln0_b": columns(w["ln0_b"]),
        "wq": turned(w["qkv_w"][0:dim]), "wk": turned(w["qkv_w"][dim:2 * dim]), "wv": turned(w["qkv_w"][2 * dim:]),
        "sa_w": turned(w["sa_proj_w"]),
        "ln1_w": columns(w["ln1_w"]), "ln1_b": columns(w["ln1_b"]),
        "cq_w": turned(w["q_w"]), "ck_w": turned(w["k_w"]), "cv_w": turned(w["v_w"]), "ca_w": turned(w["ca_proj_w"]),
        "ln2_w": columns(w["ln2_w"]), "ln2_b": columns(w["ln2_b"]),
        "fc1_w": turned(w["fc1_w"]), "fc1_b": columns(w["fc1_b"]),
        "fc2_w": turned(w["fc2_w"]), "fc2_b": np.ascontiguousarray(w["fc2_b"]),
    }
    nc = bacc.Bacc("TRN2", target_bir_lowering=False, num_devices=1)
    args = [nc.dram_tensor(f"in_{k}", a.shape, mybir.dt.from_np(a.dtype), kind="ExternalInput").ap()
            for k, a in arrays.items()]
    out = nc.dram_tensor("out", [batches * length, dim], F32, kind="ExternalOutput").ap()
    transformer_block(nc, *args, out)
    r = run_bass_kernel_spmd(nc, [{f"in_{k}": a for k, a in arrays.items()}], core_ids=[0])
    return r.results[0]["out"].reshape(batches, length, dim)
```

```python
import math
from contextlib import ExitStack

import concourse.bass as bass
from concourse import mybir

P = 128
ALU = mybir.AluOpType
ACT = mybir.ActivationFunctionType
F32 = mybir.dt.float32
F32R = mybir.dt.float32r
I32 = mybir.dt.int32
AX_X = mybir.AxisListType.X

HEAD_DIM = 32
HEADS_PER_GROUP = P // HEAD_DIM
TOK = 512
SUB = TOK // P
EPS = 1e-5
MASK_BIAS = -10000.0



class Memory:

    def __init__(self, nc, stack, phase):
        self.nc, self.stack, self.phase, self.sems = nc, stack, phase, []
        stack.callback(self.release)

    def release(self):
        self.nc.clear_and_free_semaphores(self.sems)
        self.nc.all_engine_barrier()

    def sbuf(self, name, shape, dtype=F32):
        return self.stack.enter_context(self.nc.sbuf_tensor(f"{self.phase}_{name}", shape, dtype))

    def psum(self, name, shape):
        return self.stack.enter_context(self.nc.psum_tensor(f"{self.phase}_{name}", shape, F32))

    def sem(self, name):
        self.sems.append(self.nc.alloc_semaphore(f"{self.phase}_{name}"))
        return self.sems[-1]


def wait_alone(eng, sem, value, passed):
    eng.wait_ge(sem, value)
    eng.sem_inc(passed, 1)


def product(nc, out, left, right, first, last):
    (left_high, left_low), (right_high, right_low) = left, right
    nc.tensor.matmul(out, left_high, right_high, start=first, stop=False)
    nc.tensor.matmul(out, left_high, right_low, start=False, stop=False)
    return nc.tensor.matmul(out, left_low, right_high, start=False, stop=last)


def make_identity(nc, pool, identity, ident_done):
    nc.gpsimd.memset(identity[:], 0.0).then_inc(ident_done, 1)
    pool.wait_ge(ident_done, 1)
    nc.gpsimd.affine_select(out=identity[:], in_=identity[:], compare_op=ALU.not_equal, fill=1.0, base=0,
                            pattern=[[-1, P]], channel_multiplier=1).then_inc(ident_done, 1)


def token_phase(nc, name, x_in, ln_w, ln_b, attn=None, proj_w=None, x_out=None, v_w=None, v_out=None,
                qk=(), xn_out=None):
    dim = x_in.shape[1]
    tiles = x_in.shape[0] // TOK
    chunks = dim // P
    out_groups = dim // P
    n_v = SUB if v_w is not None else 0
    n_qk = len(qk) * out_groups
    n_out = n_v + n_qk
    n_early = n_out - out_groups if n_out > out_groups else n_out // 2
    slots = 4
    weights = ([proj_w] if proj_w is not None else []) + ([v_w] if v_w is not None else []) + [w for w, _ in qk]
    i_proj = 0
    i_v = 1 if proj_w is not None else 0
    i_qk = i_v + (1 if v_w is not None else 0)

    with ExitStack() as stack:
        m = Memory(nc, stack, name)
        w_raw = m.sbuf("w_raw", [P, 2, chunks, dim])
        w_high = m.sbuf("w_high", [P, len(weights), chunks, dim], F32R) if weights else None
        w_low = m.sbuf("w_low", [P, len(weights), chunks, dim], F32R) if weights else None
        gain = m.sbuf("gain", [P, chunks])
        shift = m.sbuf("shift", [P, chunks])
        identity = m.sbuf("identity", [P, P])
        x = m.sbuf("x", [P, 2, SUB, dim])
        stats = m.sbuf("stats", [P, SUB, 6])
        moments = m.sbuf("moments", [P, SUB, 2])
        var = m.sbuf("var", [P, SUB])
        rstd = m.sbuf("rstd", [P, SUB])
        minus_half = m.sbuf("minus_half", [P, SUB])
        xn = m.sbuf("xn", [P, 2, SUB, dim])
        xt = m.sbuf("xt", [P, chunks, TOK])
        xt_high = m.sbuf("xt_high", [P, 2, chunks, TOK], F32R)
        xt_low = m.sbuf("xt_low", [P, 2, chunks, TOK], F32R)
        if attn is not None:
            a_high = m.sbuf("a_high", [P, 2, chunks, TOK], F32R)
            a_low = m.sbuf("a_low", [P, 2, chunks, TOK], F32R)
        if n_qk:
            r_high = m.sbuf("r_high", [P, slots, TOK], F32R)
            r_low = m.sbuf("r_low", [P, slots, TOK], F32R)
        if n_v:
            v_sb = m.sbuf("v_sb", [P, SUB, dim])
        turned = m.psum("turned", [P, 4, TOK])
        result = m.psum("result", [P, 4, TOK])

        w_loaded = [m.sem(f"w_loaded{k}") for k in range(2)]
        w_high_done = m.sem("w_high_done")
        w_ready = m.sem("w_ready")
        ln_loaded = m.sem("ln_loaded")
        ident_done = m.sem("ident_done")
        waits_passed = m.sem("waits_passed")
        x_loaded = [m.sem(f"x_loaded{u}") for u in range(2)]
        a_loaded = [m.sem(f"a_loaded{u}") for u in range(2)]
        x_stored = [m.sem(f"x_stored{u}") for u in range(2)]
        proj_done = m.sem("proj_done")
        x_ready = m.sem("x_ready")
        stats_done = m.sem("stats_done")
        moments_done = m.sem("moments_done")
        var_done = m.sem("var_done")
        rstd_done = m.sem("rstd_done")
        xn_ready = m.sem("xn_ready")
        turn_done = m.sem("turn_done")
        xt_done = m.sem("xt_done")
        xt_high_done = m.sem("xt_high_done")
        xt_ready = m.sem("xt_ready")
        xt_stored = [m.sem(f"xt_stored{u}") for u in range(2)]
        result_done = m.sem("result_done")
        high_done = m.sem("high_done")
        result_read = m.sem("result_read")
        stored = [m.sem(f"stored{k}") for k in range(slots)]
        v_stored = [m.sem(f"v_stored{s}") for s in range(SUB)]

        x_view = x_in.rearrange("(t s p) d -> t p s d", p=P, s=SUB)

        with nc.Block() as block:

            @block.sync
            def _(sp):
                def load(t, u):
                    if attn is not None:
                        for part, to in ((0, a_high), (1, a_low)):
                            sp.dma_start(to[:, u].bitcast(F32), attn[part].rearrange("(c p) t -> p c t", p=P)[
                                :, :, bass.ds(t * TOK, TOK)]).then_inc(a_loaded[u], 16)
                    sp.dma_start(x[:, u], x_view[t]).then_inc(x_loaded[u], 16)

                load(0, 0)
                sp.dma_start(gain[:], ln_w).then_inc(ln_loaded, 16)
                sp.dma_start(shift[:], ln_b).then_inc(ln_loaded, 16)
                for k, w in enumerate(weights):
                    if k >= 2:
                        sp.wait_ge(w_ready, k - 1)
                    sp.dma_start(w_raw[:, k % 2], w.rearrange("(c p) n -> p c n", p=P)).then_inc(w_loaded[k % 2], 16)
                load(1, 1)

                def store_results(t, u, items):
                    for n in items:
                        wait_alone(sp, result_read, t * n_out + n + 1, waits_passed)
                        if n < n_v:
                            sp.dma_start(v_out[bass.ds(t * TOK + n * P, P), :], v_sb[:, n]).then_inc(v_stored[n], 16)
                        else:
                            k = n - n_v
                            to, group = qk[k // out_groups][1], k % out_groups
                            for part, src in ((0, r_high), (1, r_low)):
                                sp.dma_start(to[part, group * P:(group + 1) * P, bass.ds(t * TOK, TOK)],
                                             src[:, k % slots].bitcast(F32)).then_inc(stored[k % slots], 16)

                def tile_traffic(t, u, reload):
                    if x_out is not None:
                        wait_alone(sp, x_ready, SUB * (t + 1), waits_passed)
                        sp.dma_start(x_out.rearrange("(t s p) d -> t p s d", p=P, s=SUB)[t], x[:, u]).then_inc(
                            x_stored[u], 16)
                    if xn_out is not None:
                        wait_alone(sp, xt_ready, chunks * (t + 1), waits_passed)
                        for part, src in ((0, xt_high), (1, xt_low)):
                            sp.dma_start(xn_out[part].rearrange("(c p) t -> p c t", p=P)[:, :, bass.ds(t * TOK, TOK)],
                                         src[:, u].bitcast(F32)).then_inc(xt_stored[u], 16)
                    if reload:
                        wait_alone(sp, xn_ready, SUB * (t + 1), waits_passed)
                        if x_out is not None:
                            wait_alone(sp, x_stored[u], 16 * (t // 2 + 1), waits_passed)
                        if attn is not None:
                            wait_alone(sp, proj_done, SUB * (t + 1), waits_passed)
                        load(t + 2, u)
                    store_results(t, u, range(n_out))

                with sp.Fori(0, tiles // 2 - 1) as pair:
                    tile_traffic(2 * pair, 0, True)
                    tile_traffic(2 * pair + 1, 1, True)
                tile_traffic(tiles - 2, 0, False)
                tile_traffic(tiles - 1, 1, False)
                for u in range(2):
                    if x_out is not None:
                        sp.wait_ge(x_stored[u], 16 * tiles // 2)
                    if xn_out is not None:
                        sp.wait_ge(xt_stored[u], 32 * tiles // 2)
                for k in range(slots if n_qk else 0):
                    sp.wait_ge(stored[k], 32 * tiles * (n_qk // slots))
                for s in range(n_v):
                    sp.wait_ge(v_stored[s], 16 * tiles)

            @block.gpsimd
            def _(pool):
                make_identity(nc, pool, identity, ident_done)
                nc.gpsimd.memset(minus_half[:], -0.5).then_inc(ident_done, 1)
                pool.wait_ge(ident_done, 3)

                def inverse_root(t):
                    pool.wait_ge(var_done, 2 * (t + 1))
                    nc.gpsimd.tensor_tensor(rstd[:], var[:], minus_half[:], ALU.pow).then_inc(rstd_done, 1)

                with pool.Fori(0, tiles) as t:
                    inverse_root(t)

            @block.tensor
            def _(pe):
                def w_parts(k, c, cols):
                    return w_high[:, k, c, cols], w_low[:, k, c, cols]

                def project(t, u):
                    pe.wait_ge(a_loaded[u], 32 * (t // 2 + 1))
                    pe.wait_ge(w_ready, i_proj + 1)
                    for s in range(SUB):
                        if not (isinstance(t, int) and t == 0):
                            pe.wait_ge(xt_high_done, chunks * (t - 1) + s + 1)
                        cols = slice(s * P, (s + 1) * P)
                        for c in range(chunks):
                            mm = product(nc, turned[:, s], (a_high[:, u, c, cols], a_low[:, u, c, cols]),
                                         w_parts(i_proj, c, slice(0, dim)), c == 0, c == chunks - 1)
                        mm.then_inc(proj_done, 1)

                def turn(t, u):
                    for c in range(chunks):
                        if c == 0:
                            pe.wait_ge(xn_ready, SUB * (t + 1))
                        if proj_w is None and not (isinstance(t, int) and t == 0):
                            pe.wait_ge(xt_high_done, chunks * (t - 1) + c + 1)
                        for s in range(SUB):
                            mm = nc.tensor.transpose(turned[:, c, s * P:(s + 1) * P],
                                                     xn[:, u, s, c * P:(c + 1) * P], identity[:])
                        mm.then_inc(turn_done, 1)

                def results(t, u, items):
                    for n in items:
                        if not (isinstance(t, int) and t == 0 and n < 4):
                            pe.wait_ge(result_read, t * n_out + n - 3)
                        for c in range(chunks):
                            if n < n_v:
                                mm = product(nc, result[:, n % 4],
                                             (xt_high[:, u, c, n * P:(n + 1) * P], xt_low[:, u, c, n * P:(n + 1) * P]),
                                             w_parts(i_v, c, slice(0, dim)), c == 0, c == chunks - 1)
                            else:
                                k = n - n_v
                                group = k % out_groups
                                mm = product(nc, result[:, n % 4],
                                             w_parts(i_qk + k // out_groups, c, slice(group * P, (group + 1) * P)),
                                             (xt_high[:, u, c], xt_low[:, u, c]), c == 0, c == chunks - 1)
                        mm.then_inc(result_done, 1)

                def body(t, u, has_next):
                    if has_next and proj_w is not None:
                        project(t + 1, 1 - u)
                    if n_out:
                        pe.wait_ge(xt_ready, chunks * (t + 1))
                        if isinstance(t, int) and t == 0:
                            pe.wait_ge(w_ready, len(weights))
                        results(t, u, range(n_early))
                    if has_next:
                        turn(t + 1, 1 - u)
                    results(t, u, range(n_early, n_out))

                pe.wait_ge(ident_done, 2)
                if proj_w is not None:
                    project(0, 0)
                turn(0, 0)
                body(0, 0, True)
                body(1, 1, True)
                with pe.Fori(1, tiles // 2 - 1) as pair:
                    body(2 * pair, 0, True)
                    body(2 * pair + 1, 1, True)
                body(tiles - 2, 0, True)
                body(tiles - 1, 1, False)

            @block.scalar
            def _(act):
                def split_turned(t, u):
                    for c in range(chunks):
                        act.wait_ge(turn_done, chunks * t + c + 1)
                        if not (isinstance(t, int) and t == 0):
                            act.wait_ge(xt_ready, chunks * (t - 1) + c + 1)
                        nc.scalar.activation(xt[:, c], turned[:, c], ACT.Identity, bias=shift[:, c:c + 1],
                                             scale=gain[:, c:c + 1]).then_inc(xt_done, 1)
                        if xn_out is not None and not (isinstance(t, int) and t < 2):
                            act.wait_ge(xt_stored[u], 32 * (t // 2))
                        nc.scalar.activation(xt_high[:, u, c], turned[:, c], ACT.Identity, bias=shift[:, c:c + 1],
                                             scale=gain[:, c:c + 1]).then_inc(xt_high_done, 1)

                def high_parts(t, items):
                    for n in items:
                        if n < n_v:
                            continue
                        k = n - n_v
                        act.wait_ge(result_done, t * n_out + n + 1)
                        act.wait_ge(stored[k % slots], 32 * (t * (n_qk // slots) + k // slots))
                        nc.scalar.activation(r_high[:, k % slots], result[:, n % 4], ACT.Copy).then_inc(high_done, 1)

                for k in range(len(weights)):
                    act.wait_ge(w_loaded[k % 2], 16 * (k // 2 + 1))
                    nc.scalar.activation(w_high[:, k], w_raw[:, k % 2], ACT.Copy).then_inc(w_high_done, 1)
                act.wait_ge(ln_loaded, 32)

                def body(t, u, has_next):
                    high_parts(t, range(n_early))
                    if has_next:
                        split_turned(t + 1, 1 - u)
                    high_parts(t, range(n_early, n_out))

                split_turned(0, 0)
                body(0, 0, True)
                body(1, 1, True)
                with act.Fori(1, tiles // 2 - 1) as pair:
                    body(2 * pair, 0, True)
                    body(2 * pair + 1, 1, True)
                body(tiles - 2, 0, True)
                body(tiles - 1, 1, False)

            @block.vector
            def _(dve):
                def norm(t, u):
                    dve.wait_ge(x_loaded[u], 16 * (t // 2 + 1))
                    for s in range(SUB):
                        if proj_w is not None:
                            dve.wait_ge(proj_done, SUB * t + s + 1)
                            nc.vector.tensor_tensor(x[:, u, s], turned[:, s], x[:, u, s], ALU.add).then_inc(x_ready, 1)
                    if not (isinstance(t, int) and t == 0):
                        dve.wait_ge(xn_ready, SUB * t)

                    def stats_of(s):
                        if proj_w is not None:
                            dve.wait_ge(x_ready, SUB * t + s + 1)
                        return nc.vector.bn_stats(stats[:, s], x[:, u, s]).then_inc(stats_done, 1)

                    def moments_of(s):
                        nc.vector.bn_aggr(moments[:, s], stats[:, s]).then_inc(moments_done, 1)

                    def var_of(a, b):
                        dve.wait_ge(moments_done, SUB * t + b)
                        nc.vector.tensor_scalar(var[:, a:b], moments[:, a:b, 1], EPS, None, ALU.add).then_inc(var_done, 1)

                    half = SUB // 2
                    for s in range(half):
                        stats_of(s)
                    dve.wait_ge(stats_done, SUB * t + half)
                    for s in range(half, SUB):
                        stats_of(s)
                    for s in range(half):
                        moments_of(s)
                    dve.wait_ge(stats_done, SUB * (t + 1))
                    var_of(0, half)
                    for s in range(half, SUB):
                        moments_of(s)
                    var_of(half, SUB)
                    dve.wait_ge(rstd_done, t + 1)
                    for s in range(SUB):
                        nc.vector.tensor_scalar(xn[:, u, s], x[:, u, s], moments[:, s, 0:1], rstd[:, s:s + 1],
                                                ALU.subtract, ALU.mult).then_inc(xn_ready, 1)

                def low_turned(t, u):
                    for c in range(chunks):
                        dve.wait_ge(xt_high_done, chunks * t + c + 1)
                        nc.vector.tensor_tensor(xt_low[:, u, c], xt[:, c], xt_high[:, u, c].bitcast(F32),
                                                ALU.subtract).then_inc(xt_ready, 1)

                def low_parts(t, items):
                    for n in items:
                        if n < n_v:
                            dve.wait_ge(result_done, t * n_out + n + 1)
                            dve.wait_ge(v_stored[n], 16 * t)
                            nc.vector.tensor_copy(v_sb[:, n], result[:, n % 4]).then_inc(result_read, 1)
                        else:
                            k = n - n_v
                            dve.wait_ge(high_done, t * n_qk + k + 1)
                            nc.vector.tensor_tensor(r_low[:, k % slots], result[:, n % 4],
                                                    r_high[:, k % slots].bitcast(F32), ALU.subtract).then_inc(result_read, 1)

                def body(t, u, has_next):
                    if has_next:
                        norm(t + 1, 1 - u)
                    low_parts(t, range(n_early))
                    if has_next:
                        low_turned(t + 1, 1 - u)
                    low_parts(t, range(n_early, n_out))

                for k in range(len(weights)):
                    dve.wait_ge(w_high_done, k + 1)
                    nc.vector.tensor_tensor(w_low[:, k], w_raw[:, k % 2], w_high[:, k].bitcast(F32),
                                            ALU.subtract).then_inc(w_ready, 1)
                    if k == 0:
                        norm(0, 0)
                low_turned(0, 0)
                body(0, 0, True)
                body(1, 1, True)
                with dve.Fori(1, tiles // 2 - 1) as pair:
                    body(2 * pair, 0, True)
                    body(2 * pair + 1, 1, True)
                body(tiles - 2, 0, True)
                body(tiles - 1, 1, False)


def attention_phase(nc, name, q_t, k_t, v, out, keys, tiles_per_stage, mask_rows=None):
    tokens = q_t.shape[2]
    batches = k_t.shape[2] // keys
    features = q_t.shape[1]
    groups_per_batch = features // P
    r_tiles = tiles_per_stage
    span = r_tiles * TOK
    stages_per_group = tokens // batches // span
    groups = batches * groups_per_batch
    stages = groups * stages_per_group
    heads = HEADS_PER_GROUP
    scale = 1.0 / math.sqrt(HEAD_DIM)
    masked = mask_rows is not None
    base = 3 * HEAD_DIM
    score_rows = base + (2 if masked else 0)
    exp_rows = score_rows + 2
    long = keys >= TOK
    n_k = -(-keys // P)
    width = keys // n_k
    assert width * n_k == keys and n_k % 2 == 0
    steps = r_tiles * n_k
    sets = [list(range(k, min(k + 4, n_k))) for k in range(0, n_k, 4)]
    head_sets = [[a] for a in range(heads)] if long else [list(range(heads))]
    item_banks = 2 if long else 1
    if long:
        items = [(a, s, k0) for a in range(heads) for s in range(r_tiles * SUB) for k0 in range(0, keys, 2 * TOK)]
    else:
        items = [(a, s, 0) for a in range(heads) for s in range(0, r_tiles * SUB, 2)]
    n_items = len(items)
    per_head = n_items // heads
    n_reads = n_items + 1
    n_max = heads * r_tiles * SUB
    n_turned = n_max if n_max <= 32 else P
    p_slots = 4
    pairs = n_k // 2
    n_pairs = r_tiles * pairs
    n_acc = 2 if r_tiles > 1 else 1
    v_lag = 2
    sum_lag = 4

    due = [[] for _ in range(2 * steps)]
    for t in range(steps):
        due[t + v_lag].append(("weigh", t))
    for p in range(n_pairs):
        r, k = p // pairs, p % pairs
        at = r * n_k + 2 * k + sum_lag
        if n_acc == 1:
            at = min(at, (r + 1) * n_k + v_lag - 1)
        due[at].append(("add_up", p))
    schedule = []
    n_parts = 2 * n_items
    done = 0
    for t in range(steps):
        jobs = [(what, n, -1) for what, n in due[t + steps]] + [(what, n, 0) for what, n in due[t]]
        quota = -(-n_parts * (t + 1) // max(steps - 3, 1))
        for a in range(heads):
            schedule.append(("second", t * heads + a, 0))
            upto = min(n_parts, done + -(-(quota - done) * 1 // (heads - a)))
            schedule += [("first", n, 1) for n in range(done, upto)]
            done = upto
            if jobs and a % 2 == 1:
                take = len(jobs) if a == heads - 1 else -(-len(jobs) // 2)
                schedule += jobs[:take]
                jobs = jobs[take:]
            if done == n_parts and ("turn", 0, 1) not in schedule:
                schedule.append(("turn", 0, 1))
    tail = [(what, n, 0) for t in range(steps, 2 * steps) for what, n in due[t]]

    def ends_tile(what, n):
        return what == "add_up" and n % pairs == pairs - 1

    position = {job: n for n, job in enumerate(schedule)}
    store_delay = len(schedule) // steps
    traffic = []
    for job, n in position.items():
        what, number, of = job
        if ends_tile(what, number):
            at = n + store_delay
            traffic.append((at % len(schedule), "store", number // pairs, of - (at >= len(schedule))))
        if what == "first" and number % 2 == 1:
            for h, members in enumerate(head_sets):
                if number // 2 == per_head * (members[-1] + 1) - 1:
                    traffic.append((n, "heads", h, of))
        if what == "turn":
            traffic.append((n, "max", 0, of))
        for j, tiles in enumerate(sets):
            if what == "second" and number == heads * (steps - n_k + tiles[-1]) + heads - 1:
                traffic.append((n, "k", j, of))
            if what == "weigh" and number == steps - n_k + tiles[-1]:
                traffic.append((n, "v", j, of))
    traffic.sort(key=lambda event: event[0])
    assert len([event for event in traffic if event[1] == "store"]) == r_tiles

    with ExitStack() as stack:
        m = Memory(nc, stack, name)
        k_move = m.sbuf("k_move", [P, heads, keys], F32R)
        k_hold = m.sbuf("k_hold", [P, heads, keys], F32R)
        q_hold = m.sbuf("q_hold", [P, heads, span], F32R)
        q_move = m.sbuf("q_move", [P, 2, heads, span], F32R)
        v_sb = m.sbuf("v_sb", [P, n_k, P])
        expo = m.sbuf("expo", [P, p_slots, heads, TOK])
        pair_sum = m.sbuf("pair_sum", [P, 2, heads, TOK])
        ones = m.sbuf("ones", [P, HEAD_DIM])
        identity = m.sbuf("identity", [P, P])
        part_max = m.sbuf("part_max", [P, n_max, keys // (2 * TOK)]) if long else None
        row_max = m.sbuf("row_max", [P, n_turned])
        max_high = m.sbuf("max_high", [n_max, P], F32R)
        max_low = m.sbuf("max_low", [n_max, P], F32R)
        sums = m.sbuf("sums", [P, TOK])
        inverse = m.sbuf("inverse", [P, TOK])
        unscaled = m.sbuf("unscaled", [P, TOK])
        mean = m.sbuf("mean", [P, TOK])
        mean_high = m.sbuf("mean_high", [P, 2, TOK], F32R)
        mean_low = m.sbuf("mean_low", [P, 2, TOK], F32R)
        first = m.psum("first", [P, 2, item_banks * TOK])
        second = m.psum("second", [P, 2, TOK])
        weighted = m.psum("weighted", [P, n_acc, TOK])
        total = m.psum("total", [P, n_acc, TOK])

        ident_done = m.sem("ident_done")
        constant_rows = m.sem("constant_rows")
        k_move_loaded = [m.sem(f"k_move_loaded{h}") for h in range(len(head_sets))]
        k_hold_loaded = [m.sem(f"k_hold_loaded{j}") for j in range(len(sets))]
        v_loaded = [m.sem(f"v_loaded{j}") for j in range(len(sets))]
        q_hold_loaded = [m.sem(f"q_hold_loaded{h}") for h in range(len(head_sets))]
        q_move_loaded = m.sem("q_move_loaded")
        max_loaded = m.sem("max_loaded")
        first_done = m.sem("first_done")
        first_read = m.sem("first_read")
        row_max_done = m.sem("row_max_done")
        turned = m.sem("turned")
        max_high_done = m.sem("max_high_done")
        second_done = m.sem("second_done")
        exp_done = m.sem("exp_done")
        pair_done = m.sem("pair_done")
        weighted_done = m.sem("weighted_done")
        total_done = m.sem("total_done")
        sums_read = m.sem("sums_read")
        weighted_read = m.sem("weighted_read")
        inverse_done = m.sem("inverse_done")
        mean_done = m.sem("mean_done")
        mean_high_done = m.sem("mean_high_done")
        mean_ready = m.sem("mean_ready")
        out_stored = [m.sem(f"out_stored{u}") for u in range(2)]
        waits_passed = m.sem("waits_passed")

        def ge(eng, sem, value, alone=False):
            if isinstance(value, int) and value <= 0:
                return
            if alone and not isinstance(value, int):
                wait_alone(eng, sem, value, waits_passed)
            else:
                eng.wait_ge(sem, value)

        k_count = 16 * (3 + masked)

        with nc.Block() as block:

            @block.sync
            def _(sp):
                def stacked(dst, src, parts, rows, cols, sem):
                    for j, part in enumerate(parts):
                        sp.dma_start(dst[j * HEAD_DIM:(j + 1) * HEAD_DIM].bitcast(F32),
                                     src[part, rows, cols].rearrange("(a d) t -> d a t", d=HEAD_DIM)).then_inc(sem, 16)

                def group_of(g):
                    return g // groups_per_batch, g % groups_per_batch

                def mask_of(b, n_heads, k0, n):
                    return mask_rows[b, :, k0:k0 + n].unsqueeze(1).to_broadcast([2, n_heads, n])

                def load_k_move(g, h):
                    b, group = group_of(g)
                    a, n = head_sets[h][0], len(head_sets[h])
                    stacked(k_move[:, a:a + n], k_t, (0, 0, 1), bass.ds(group * P + a * HEAD_DIM, n * HEAD_DIM),
                            bass.ds(b * keys, keys), k_move_loaded[h])
                    if masked:
                        sp.dma_start(k_move[base:base + 2, a:a + n].bitcast(F32), mask_of(b, n, 0, keys)).then_inc(
                            k_move_loaded[h], 16)

                def load_k_hold(g, j):
                    b, group = group_of(g)
                    k0, n = sets[j][0] * width, len(sets[j]) * width
                    stacked(k_hold[:, :, k0:k0 + n], k_t, (0, 0, 1), bass.ds(group * P, P),
                            bass.ds(b * keys + k0, n), k_hold_loaded[j])
                    if masked:
                        sp.dma_start(k_hold[base:base + 2, :, k0:k0 + n].bitcast(F32), mask_of(b, heads, k0, n)).then_inc(
                            k_hold_loaded[j], 16)

                def load_v(g, j):
                    b, group = group_of(g)
                    k0, n = sets[j][0], len(sets[j])
                    sp.dma_start(v_sb[0:width, k0:k0 + n],
                                 v[bass.ds(b * keys + k0 * width, n * width), bass.ds(group * P, P)]
                                 .rearrange("(k p) d -> p k d", p=width)).then_inc(v_loaded[j], 16)

                def query_slice(i, r=0, n=span):
                    b, group = group_of(i // stages_per_group)
                    return group, bass.ds(b * (tokens // batches) + (i % stages_per_group) * span + r * TOK, n)

                def load_q_hold(i, h):
                    group, cols = query_slice(i)
                    a, n = head_sets[h][0], len(head_sets[h])
                    stacked(q_hold[:, a:a + n], q_t, (0, 1, 0), bass.ds(group * P + a * HEAD_DIM, n * HEAD_DIM), cols,
                            q_hold_loaded[h])

                def load_q_move(i):
                    group, cols = query_slice(i)
                    stacked(q_move[:, i % 2], q_t, (0, 1, 0), bass.ds(group * P, P), cols, q_move_loaded)

                def load_max(i):
                    ge(sp, first_read, n_reads * (i + 1), alone=True)
                    for row, src in ((score_rows, max_high), (score_rows + 1, max_low)):
                        sp.dma_start(q_move[row:row + 1, i % 2].rearrange("o a (s t) -> o (a s) t", t=P).bitcast(F32),
                                     src[:].bitcast(F32)).then_inc(max_loaded, 16)

                def store_out(i, r):
                    n = i * r_tiles + r
                    ge(sp, mean_ready, n + 1, alone=True)
                    group, cols = query_slice(i, r, TOK)
                    u = r % 2 if r_tiles > 1 else 0
                    for part, src in ((0, mean_high), (1, mean_low)):
                        sp.dma_start(out[part, bass.ds(group * P, P), cols], src[:, u].bitcast(F32)).then_inc(
                            out_stored[u], 16)

                def stage(i, g, qt):
                    first_one = isinstance(i, int) and i == 0
                    last = isinstance(i, int) and i == stages - 1
                    last2 = isinstance(i, int) and i >= stages - 2
                    new_next = (qt + 1) % stages_per_group == 0 and not last
                    new_after = (qt + 2) % stages_per_group == 0 and not last2
                    after = (i + 2) // stages_per_group if isinstance(i, int) or stages_per_group == 1 else g + 1
                    if not last:
                        ge(sp, second_done, heads * steps * i, alone=True)
                        ge(sp, q_move_loaded, 48 * (i + 1), alone=True)
                        load_q_move(i + 1)
                    for _, what, n, of in traffic:
                        if of == -1 and first_one:
                            continue
                        if what == "store":
                            store_out(i + of, n)
                        elif what == "max" and not last:
                            load_max(i + 1)
                        elif what == "heads" and not last2:
                            ge(sp, first_done, n_items * (i + 1) + per_head * (head_sets[n][-1] + 1), alone=True)
                            load_q_hold(i + 2, n)
                            if new_after:
                                load_k_move(after, n)
                        elif what == "k" and new_next:
                            ge(sp, second_done, heads * (steps * i + steps - n_k + sets[n][-1] + 1), alone=True)
                            load_k_hold(g + 1, n)
                        elif what == "v" and (new_next if of == 0 else qt == 0):
                            ge(sp, weighted_done, steps * (i + of) + steps - n_k + sets[n][-1] + 1, alone=True)
                            load_v(g + 1 + of, n)

                sp.wait_ge(constant_rows, 7)
                for h in range(len(head_sets)):
                    load_q_hold(0, h)
                    load_k_move(0, h)
                load_q_move(0)
                for j in range(len(sets)):
                    load_k_hold(0, j)
                    load_v(0, j)
                for h in range(len(head_sets)):
                    sp.wait_ge(first_done, per_head * (head_sets[h][-1] + 1))
                    load_q_hold(1, h)
                    if stages_per_group == 1:
                        load_k_move(1, h)
                load_max(0)
                peel = max(1, 2 // stages_per_group)
                for g in range(peel):
                    for qt in range(stages_per_group):
                        stage(g * stages_per_group + qt, g, qt)
                with sp.Fori(peel, groups - 2) as g:
                    for qt in range(stages_per_group):
                        stage(g * stages_per_group + qt, g, qt)
                for g in range(groups - 2, groups):
                    for qt in range(stages_per_group):
                        stage(g * stages_per_group + qt, g, qt)
                for _, what, n, of in traffic:
                    if what == "store" and of == -1:
                        store_out(stages - 1, n)
                for u in range(n_acc):
                    sp.wait_ge(out_stored[u], 32 * stages * r_tiles // n_acc)

            @block.gpsimd
            def _(pool):
                make_identity(nc, pool, identity, ident_done)

                def add_pairs(i):
                    for p in range(n_pairs):
                        t = 2 * p
                        ge(pool, exp_done, heads * (steps * i + t + 2))
                        ge(pool, total_done, n_pairs * i + p - 1)
                        nc.gpsimd.tensor_tensor(pair_sum[0:width, p % 2], expo[0:width, t % p_slots],
                                                expo[0:width, (t + 1) % p_slots], ALU.add).then_inc(pair_done, 1)

                add_pairs(0)
                with pool.Fori(1, stages) as i:
                    add_pairs(i)

            @block.tensor
            def _(pe):
                def first_pass(i, part):
                    n, half = part // 2, part % 2
                    a, s, k0 = items[n]
                    if half == 0:
                        for h, members in enumerate(head_sets):
                            if a == members[0] and n % per_head == 0:
                                ge(pe, q_hold_loaded[h], 48 * (i + 1))
                                ge(pe, k_move_loaded[h], k_count * (i // stages_per_group + 1))
                        ge(pe, first_read, n_reads * i + (n - 1 if n > 1 else 0))
                    if long:
                        mm = nc.tensor.matmul(first[:, n % 2, half * TOK:(half + 1) * TOK],
                                              q_hold[0:score_rows, a, s * P:(s + 1) * P],
                                              k_move[0:score_rows, a, k0 + half * TOK:k0 + (half + 1) * TOK],
                                              start=True, stop=True)
                    else:
                        mm = nc.tensor.matmul(first[:, n % 2, half * keys:(half + 1) * keys],
                                              q_hold[0:score_rows, a, (s + half) * P:(s + half + 1) * P],
                                              k_move[0:score_rows, a], start=True, stop=True)
                    if half == 1:
                        mm.then_inc(first_done, 1)

                def turn_max(i):
                    ge(pe, row_max_done, i + 1)
                    nc.tensor.transpose(first[0:n_turned, 0, 0:P], row_max[:], identity[:]).then_inc(turned, 1)

                def second_pass(i, n):
                    t, a = n // heads, n % heads
                    r, k = t // n_k, t % n_k
                    if a == 0 and r == 0:
                        for j, tiles in enumerate(sets):
                            if k == tiles[0]:
                                ge(pe, k_hold_loaded[j], k_count * (i // stages_per_group + 1))
                    if n == 0:
                        ge(pe, q_move_loaded, 48 * (i + 1))
                        ge(pe, max_loaded, 32 * (i + 1))
                    ge(pe, exp_done, heads * steps * i + n - 1)
                    nc.tensor.matmul(second[0:width, n % 2], k_hold[0:exp_rows, a, k * width:(k + 1) * width],
                                     q_move[0:exp_rows, i % 2, a, r * TOK:(r + 1) * TOK],
                                     start=True, stop=True).then_inc(second_done, 1)

                def weigh(i, t):
                    r, k = t // n_k, t % n_k
                    if r == 0:
                        for j, tiles in enumerate(sets):
                            if k == tiles[0]:
                                ge(pe, v_loaded[j], 16 * (i // stages_per_group + 1))
                    if k == 0:
                        ge(pe, weighted_read, i * r_tiles + r - n_acc + 1)
                    ge(pe, exp_done, heads * (steps * i + t) + heads)
                    for a in range(heads):
                        cols = slice(a * HEAD_DIM, (a + 1) * HEAD_DIM)
                        mm = nc.tensor.matmul(weighted[cols, r % n_acc], v_sb[0:width, k, cols],
                                              expo[0:width, t % p_slots, a], start=k == 0, stop=k == n_k - 1)
                    mm.then_inc(weighted_done, 1)

                def add_up(i, p):
                    r, k = p // pairs, p % pairs
                    if k == 0:
                        ge(pe, sums_read, i * r_tiles + r - n_acc + 1)
                    ge(pe, pair_done, n_pairs * i + p + 1)
                    for a in range(heads):
                        cols = slice(a * HEAD_DIM, (a + 1) * HEAD_DIM)
                        mm = nc.tensor.matmul(total[cols, r % n_acc], ones[0:width], pair_sum[0:width, p % 2, a],
                                              start=k == 0, stop=k == pairs - 1)
                    mm.then_inc(total_done, 1)

                def stage(i, with_last, with_next):
                    for what, n, of in schedule:
                        if of == -1 and not with_last or of == 1 and not with_next:
                            continue
                        if what == "second":
                            second_pass(i, n)
                        elif what == "first":
                            first_pass(i + 1, n)
                        elif what == "turn":
                            turn_max(i + 1)
                        elif what == "weigh":
                            weigh(i + of, n)
                        else:
                            add_up(i + of, n)

                pe.wait_ge(ident_done, 2)
                pe.wait_ge(constant_rows, 7)
                for n in range(n_parts):
                    first_pass(0, n)
                turn_max(0)
                stage(0, False, True)
                with pe.Fori(1, stages - 1) as i:
                    stage(i, True, True)
                stage(stages - 1, True, False)
                for what, n, _ in tail:
                    (weigh if what == "weigh" else add_up)(stages - 1, n)

            @block.scalar
            def _(act):
                def exponential(i, n):
                    t, a = n // heads, n % heads
                    if a == 0:
                        ge(act, weighted_done, steps * i + t - p_slots + 1)
                        if t % 2 == 0:
                            ge(act, pair_done, n_pairs * i + (t - p_slots) // 2 + 1)
                    ge(act, second_done, heads * steps * i + n + 1)
                    nc.scalar.activation(expo[0:width, t % p_slots, a], second[0:width, n % 2], ACT.Exp,
                                         scale=scale).then_inc(exp_done, 1)

                def take_out(i, r):
                    n = i * r_tiles + r
                    ge(act, total_done, n_pairs * i + pairs * (r + 1))
                    ge(act, inverse_done, 2 * n)
                    nc.scalar.activation(sums[:], total[:, r % n_acc], ACT.Copy).then_inc(sums_read, 1)
                    ge(act, weighted_done, steps * i + n_k * (r + 1))
                    ge(act, mean_done, n)
                    nc.scalar.activation(unscaled[:], weighted[:, r % n_acc], ACT.Copy).then_inc(weighted_read, 1)

                def stage(i, with_last):
                    for what, n, of in schedule:
                        if of == -1 and not with_last:
                            continue
                        if what == "second":
                            exponential(i, n)
                        elif ends_tile(what, n):
                            take_out(i + of, n // pairs)

                stage(0, False)
                with act.Fori(1, stages) as i:
                    stage(i, True)
                for what, n, _ in tail:
                    if ends_tile(what, n):
                        take_out(stages - 1, n // pairs)

            @block.vector
            def _(dve):
                for par in range(2):
                    nc.vector.memset(q_move[base:base + 4, par].bitcast(F32), 1.0).then_inc(constant_rows, 1)
                nc.vector.memset(k_hold[base:base + 4].bitcast(F32), -1.0).then_inc(constant_rows, 1)
                nc.vector.memset(row_max[:], 0.0).then_inc(constant_rows, 1)
                nc.vector.memset(ones[:], 1.0).then_inc(constant_rows, 1)
                nc.vector.memset(q_hold[base:base + 4].bitcast(F32), 1.0).then_inc(constant_rows, 1)
                nc.vector.memset(k_move[base:base + 4].bitcast(F32), 0.0).then_inc(constant_rows, 1)

                dve.wait_ge(constant_rows, 7)

                def maxima(i, n):
                    a, s, k0 = items[n]
                    ge(dve, first_done, n_items * i + n + 1)
                    if long:
                        if n == 0:
                            ge(dve, row_max_done, i)
                        k = k0 // (2 * TOK)
                        nc.vector.tensor_reduce(part_max[:, a * r_tiles * SUB + s, k:k + 1], first[:, n % 2],
                                                AX_X, ALU.max).then_inc(first_read, 1)
                    else:
                        if n == 0:
                            ge(dve, turned, i)
                        at = a * r_tiles * SUB + s
                        nc.vector.tensor_reduce(
                            row_max[:, at:at + 2], first[:, n % 2, 0:2 * keys].rearrange("p (s k) -> p s k", k=keys),
                            AX_X, ALU.max).then_inc(first_read if n < n_items - 1 else row_max_done, 1)

                def split_max(i):
                    if long:
                        ge(dve, first_read, n_reads * i + n_items)
                        ge(dve, turned, i)
                        nc.vector.tensor_reduce(row_max[:, 0:n_max], part_max[:], AX_X, ALU.max).then_inc(row_max_done, 1)
                    ge(dve, max_loaded, 32 * i)
                    ge(dve, turned, i + 1)
                    nc.vector.tensor_copy(max_high[:], first[0:n_max, 0, 0:P]).then_inc(max_high_done, 1)
                    ge(dve, max_high_done, i + 1)
                    nc.vector.tensor_tensor(max_low[:], first[0:n_max, 0, 0:P], max_high[:].bitcast(F32),
                                            ALU.subtract).then_inc(first_read, 1 if long else 2)

                def divide(i, r, part):
                    n = i * r_tiles + r
                    u = r % n_acc
                    if part < 2:
                        ge(dve, sums_read, n + 1)
                        ge(dve, mean_done, n)
                        cols = slice(part * (TOK // 2), (part + 1) * (TOK // 2))
                        nc.vector.reciprocal(inverse[:, cols], sums[:, cols]).then_inc(inverse_done, 1)
                    elif part == 2:
                        ge(dve, inverse_done, 2 * (n + 1))
                        ge(dve, weighted_read, n + 1)
                        ge(dve, mean_ready, n)
                        nc.vector.tensor_tensor(mean[:], unscaled[:], inverse[:], ALU.mult).then_inc(mean_done, 1)
                    elif part == 3:
                        ge(dve, mean_done, n + 1)
                        ge(dve, out_stored[u], 32 * (i * (r_tiles // n_acc) + r // n_acc))
                        nc.vector.tensor_copy(mean_high[:, u], mean[:]).then_inc(mean_high_done, 1)
                    else:
                        ge(dve, mean_high_done, n + 1)
                        nc.vector.tensor_tensor(mean_low[:, u], mean[:], mean_high[:, u].bitcast(F32),
                                                ALU.subtract).then_inc(mean_ready, 1)

                def stage(i, with_last, with_next):
                    pending = []
                    for what, n, of in schedule:
                        if of == -1 and not with_last or of == 1 and not with_next:
                            continue
                        if what == "first" and n % 2 == 1:
                            maxima(i + 1, n // 2)
                        elif what == "turn":
                            split_max(i + 1)
                        elif ends_tile(what, n):
                            pending += [(i + of, n // pairs, part) for part in range(5)]
                        if pending and (what == "second" and n % 2 == 1 or not with_next):
                            divide(*pending.pop(0))
                    for job in pending:
                        divide(*job)

                for n in range(n_items):
                    maxima(0, n)
                split_max(0)
                stage(0, False, True)
                with dve.Fori(1, stages - 1) as i:
                    stage(i, True, True)
                stage(stages - 1, True, False)
                for what, n, _ in tail:
                    if ends_tile(what, n):
                        for part in range(5):
                            divide(stages - 1, n // pairs, part)


def context_phase(nc, ctx_t, mask, k_w, v_w, k_t, v, mask_rows):
    dim, keys = ctx_t.shape
    batches, batch_keys = mask.shape
    chunks = dim // P
    pieces = next(n for n in range(-(-keys // P), keys) if keys % n == 0)
    piece = keys // pieces
    assert keys <= TOK

    with ExitStack() as stack:
        m = Memory(nc, stack, "context")
        raw = m.sbuf("raw", [P, 2, chunks, dim])
        w_high = m.sbuf("w_high", [P, 2, chunks, dim], F32R)
        w_low = m.sbuf("w_low", [P, 2, chunks, dim], F32R)
        c_raw = m.sbuf("c_raw", [P, chunks, keys])
        c_high = m.sbuf("c_high", [P, chunks, keys], F32R)
        c_low = m.sbuf("c_low", [P, chunks, keys], F32R)
        k_high = m.sbuf("k_high", [P, chunks, keys], F32R)
        k_low = m.sbuf("k_low", [P, chunks, keys], F32R)
        v_sb = m.sbuf("v_sb", [P, pieces, dim])
        mask_raw = m.sbuf("mask_raw", [batches, batch_keys], I32)
        bias = m.sbuf("bias", [batches, batch_keys])
        bias_high = m.sbuf("bias_high", [batches, batch_keys], F32R)
        bias_low = m.sbuf("bias_low", [batches, batch_keys], F32R)
        result = m.psum("result", [P, 4 + pieces, TOK])

        c_loaded = m.sem("c_loaded")
        mask_loaded = m.sem("mask_loaded")
        w_loaded = [m.sem(f"w_loaded{k}") for k in range(2)]
        high_done = m.sem("high_done")
        split_done = m.sem("split_done")
        bias_done = m.sem("bias_done")
        product_done = m.sem("product_done")
        k_high_done = m.sem("k_high_done")
        result_ready = m.sem("result_ready")
        stored = m.sem("stored")

        with nc.Block() as block:

            @block.sync
            def _(sp):
                sp.dma_start(c_raw[:], ctx_t.rearrange("(c p) t -> p c t", p=P)).then_inc(c_loaded, 16)
                for k, w in enumerate((k_w, v_w)):
                    sp.dma_start(raw[:, k], w.rearrange("(c p) n -> p c n", p=P)).then_inc(w_loaded[k], 16)
                sp.dma_start(mask_raw[:], mask).then_inc(mask_loaded, 16)
                sp.wait_ge(bias_done, 4)
                for part, src in ((0, bias_high), (1, bias_low)):
                    sp.dma_start(mask_rows[:, part], src[:].bitcast(F32)).then_inc(stored, 16)
                for g in range(chunks):
                    sp.wait_ge(result_ready, g + 1)
                    for part, src in ((0, k_high), (1, k_low)):
                        sp.dma_start(k_t[part, g * P:(g + 1) * P, :], src[:, g].bitcast(F32)).then_inc(stored, 16)
                for n in range(pieces):
                    sp.wait_ge(result_ready, chunks + n + 1)
                    sp.dma_start(v[n * piece:(n + 1) * piece, :], v_sb[0:piece, n]).then_inc(stored, 16)
                sp.wait_ge(stored, 16 * (2 + 2 * chunks + pieces))

            @block.scalar
            def _(act):
                act.wait_ge(c_loaded, 16)
                nc.scalar.activation(c_high[:], c_raw[:], ACT.Copy).then_inc(high_done, 1)
                for k in range(2):
                    act.wait_ge(w_loaded[k], 16)
                    nc.scalar.activation(w_high[:, k], raw[:, k], ACT.Copy).then_inc(high_done, 1)
                for g in range(chunks):
                    act.wait_ge(product_done, g + 1)
                    nc.scalar.activation(k_high[:, g], result[:, g, 0:keys], ACT.Copy).then_inc(k_high_done, 1)

            @block.vector
            def _(dve):
                dve.wait_ge(high_done, 1)
                nc.vector.tensor_tensor(c_low[:], c_raw[:], c_high[:].bitcast(F32), ALU.subtract).then_inc(split_done, 1)
                for k in range(2):
                    dve.wait_ge(high_done, k + 2)
                    nc.vector.tensor_tensor(w_low[:, k], raw[:, k], w_high[:, k].bitcast(F32),
                                            ALU.subtract).then_inc(split_done, 1)
                dve.wait_ge(mask_loaded, 16)
                nc.vector.tensor_scalar(bias[:], mask_raw[:], -1.0, 1.0, ALU.mult, ALU.add).then_inc(bias_done, 1)
                dve.wait_ge(bias_done, 1)
                nc.vector.tensor_scalar(bias[:], bias[:], MASK_BIAS * math.sqrt(HEAD_DIM), None,
                                        ALU.mult).then_inc(bias_done, 1)
                dve.wait_ge(bias_done, 2)
                nc.vector.tensor_copy(bias_high[:], bias[:]).then_inc(bias_done, 1)
                dve.wait_ge(bias_done, 3)
                nc.vector.tensor_tensor(bias_low[:], bias[:], bias_high[:].bitcast(F32), ALU.subtract).then_inc(bias_done, 1)
                for g in range(chunks):
                    dve.wait_ge(k_high_done, g + 1)
                    nc.vector.tensor_tensor(k_low[:, g], result[:, g, 0:keys], k_high[:, g].bitcast(F32),
                                            ALU.subtract).then_inc(result_ready, 1)
                for n in range(pieces):
                    dve.wait_ge(product_done, chunks + n + 1)
                    nc.vector.tensor_copy(v_sb[0:piece, n], result[0:piece, chunks + n]).then_inc(result_ready, 1)

            @block.tensor
            def _(pe):
                pe.wait_ge(split_done, 2)
                for g in range(chunks):
                    for c in range(chunks):
                        cols = slice(g * P, (g + 1) * P)
                        mm = product(nc, result[:, g, 0:keys], (w_high[:, 0, c, cols], w_low[:, 0, c, cols]),
                                     (c_high[:, c], c_low[:, c]), c == 0, c == chunks - 1)
                    mm.then_inc(product_done, 1)
                pe.wait_ge(split_done, 3)
                for n in range(pieces):
                    for c in range(chunks):
                        cols = slice(n * piece, (n + 1) * piece)
                        mm = product(nc, result[0:piece, chunks + n], (c_high[:, c, cols], c_low[:, c, cols]),
                                     (w_high[:, 1, c], w_low[:, 1, c]), c == 0, c == chunks - 1)
                    mm.then_inc(product_done, 1)


def mlp_phase(nc, x_in, xn, w1, b1, w2, b2, out):
    dim, hidden = w1.shape
    tiles = x_in.shape[0] // TOK
    chunks = dim // P
    steps = hidden // P
    lag = 2
    per_set = 4
    sets = steps // per_set
    ring = 4
    slots = 2

    with ExitStack() as stack:
        m = Memory(nc, stack, "mlp")
        raw = m.sbuf("raw", [P, 2, per_set, dim])
        w1_high = m.sbuf("w1_high", [P, sets, chunks, per_set * P], F32R)
        w1_low = m.sbuf("w1_low", [P, sets, chunks, per_set * P], F32R)
        w2_high = m.sbuf("w2_high", [P, sets, per_set, dim], F32R)
        w2_low = m.sbuf("w2_low", [P, sets, per_set, dim], F32R)
        b1_col = m.sbuf("b1_col", [P, steps])
        b2_row = m.sbuf("b2_row", [P, dim])
        xt_high = m.sbuf("xt_high", [P, 2, chunks, TOK], F32R)
        xt_low = m.sbuf("xt_low", [P, 2, chunks, TOK], F32R)
        x = m.sbuf("x", [P, 2, SUB, dim])
        h = m.sbuf("h", [P, 2, TOK])
        h_high = m.sbuf("h_high", [P, slots, TOK], F32R)
        h_low = m.sbuf("h_low", [P, slots, TOK], F32R)
        hidden_sum = m.psum("hidden_sum", [P, ring, TOK])
        out_sum = m.psum("out_sum", [P, SUB, TOK])

        w_loaded = [m.sem(f"w_loaded{k}") for k in range(2)]
        w_high_done = m.sem("w_high_done")
        w_ready = m.sem("w_ready")
        bias_loaded = m.sem("bias_loaded")
        xn_loaded = [m.sem(f"xn_loaded{u}") for u in range(2)]
        x_loaded = [m.sem(f"x_loaded{u}") for u in range(2)]
        hidden_done = m.sem("hidden_done")
        gelu_done = m.sem("gelu_done")
        h_high_done = m.sem("h_high_done")
        h_ready = m.sem("h_ready")
        h_used = m.sem("h_used")
        bias_added = m.sem("bias_added")
        out_done = m.sem("out_done")
        stored = [m.sem(f"stored{u}") for u in range(2)]
        waits_passed = m.sem("waits_passed")

        def in_pairs(eng, body):
            body(0, 0)
            body(1, 1)
            with eng.Fori(1, tiles // 2 - 1) as pair:
                body(2 * pair, 0)
                body(2 * pair + 1, 1)
            body(tiles - 2, 0)
            body(tiles - 1, 1)

        with nc.Block() as block:

            @block.sync
            def _(sp):
                x_view = x_in.rearrange("(t s p) d -> t p s d", p=P, s=SUB)
                out_view = out.rearrange("(t s p) d -> t p s d", p=P, s=SUB)

                def load(t, u):
                    for part, to in ((0, xt_high), (1, xt_low)):
                        sp.dma_start(to[:, u].bitcast(F32), xn[part].rearrange("(c p) t -> p c t", p=P)[
                            :, :, bass.ds(t * TOK, TOK)]).then_inc(xn_loaded[u], 16)
                    sp.dma_start(x[:, u], x_view[t]).then_inc(x_loaded[u], 16)

                def load_set(k):
                    j = k // 2
                    if k >= 2:
                        sp.wait_ge(w_ready, k - 1)
                    if k % 2 == 0:
                        src = w1.rearrange("(c p) n -> p c n", p=P)[:, :, j * per_set * P:(j + 1) * per_set * P]
                    else:
                        src = w2.rearrange("(k p) n -> p k n", p=P)[:, j * per_set:(j + 1) * per_set]
                    sp.dma_start(raw[:, k % 2], src).then_inc(w_loaded[k % 2], 16)

                load_set(0)
                sp.dma_start(b1_col[:], b1).then_inc(bias_loaded, 16)
                sp.dma_start(b2_row[:], b2.unsqueeze(0).to_broadcast([P, dim])).then_inc(bias_loaded, 16)
                load(0, 0)
                for k in range(1, 2 * sets):
                    load_set(k)
                load(1, 1)

                def traffic(t, u):
                    wait_alone(sp, out_done, SUB * (t + 1), waits_passed)
                    sp.dma_start(out_view[t], x[:, u]).then_inc(stored[u], 16)
                    if not (isinstance(t, int) and t >= tiles - 2):
                        wait_alone(sp, stored[u], 16 * (t // 2 + 1), waits_passed)
                        load(t + 2, u)

                in_pairs(sp, traffic)
                for u in range(2):
                    sp.wait_ge(stored[u], 16 * tiles // 2)

            @block.tensor
            def _(pe):
                def first_product(t, u, j):
                    if j == 0:
                        pe.wait_ge(xn_loaded[u], 32 * (t // 2 + 1))
                    if isinstance(t, int) and t == 0 and j % per_set == 0:
                        pe.wait_ge(w_ready, 2 * (j // per_set) + 1)
                    if not (isinstance(t, int) and t == 0 and j < ring):
                        pe.wait_ge(gelu_done, steps * t + j - ring + 1)
                    cols = slice(j % per_set * P, (j % per_set + 1) * P)
                    for c in range(chunks):
                        mm = product(nc, hidden_sum[:, j % ring],
                                     (w1_high[:, j // per_set, c, cols], w1_low[:, j // per_set, c, cols]),
                                     (xt_high[:, u, c], xt_low[:, u, c]), c == 0, c == chunks - 1)
                    mm.then_inc(hidden_done, 1)

                def second_product(t, j):
                    if isinstance(t, int) and t == 0 and j % per_set == 0:
                        pe.wait_ge(w_ready, 2 * (j // per_set) + 2)
                    pe.wait_ge(h_ready, steps * t + j + 1)
                    for s in range(SUB):
                        if j == 0 and not (isinstance(t, int) and t == 0):
                            pe.wait_ge(out_done, SUB * (t - 1) + s + 1)
                        cols = slice(s * P, (s + 1) * P)
                        mm = product(nc, out_sum[:, s], (h_high[:, j % slots, cols], h_low[:, j % slots, cols]),
                                     (w2_high[:, j // per_set, j % per_set], w2_low[:, j // per_set, j % per_set]),
                                     j == 0, j == steps - 1)
                    mm.then_inc(h_used, 1)

                def tile(t, u):
                    for j in range(steps):
                        first_product(t, u, j)
                        if j >= lag:
                            second_product(t, j - lag)
                        elif not (isinstance(t, int) and t == 0):
                            second_product(t - 1, steps - lag + j)

                in_pairs(pe, tile)
                for j in range(steps - lag, steps):
                    second_product(tiles - 1, j)

            @block.scalar
            def _(act):
                def gelu(t, j):
                    act.wait_ge(hidden_done, steps * t + j + 1)
                    if not (isinstance(t, int) and t == 0 and j < 2):
                        act.wait_ge(h_ready, steps * t + j - 1)
                    nc.scalar.activation(h[:, j % 2], hidden_sum[:, j % ring], ACT.Gelu,
                                         bias=b1_col[:, j:j + 1]).then_inc(gelu_done, 1)

                def split_high(k):
                    act.wait_ge(w_loaded[k % 2], 16 * (k // 2 + 1))
                    to = w1_high if k % 2 == 0 else w2_high
                    nc.scalar.activation(to[:, k // 2], raw[:, k % 2], ACT.Copy).then_inc(w_high_done, 1)

                def tile(t, u):
                    for j in range(steps):
                        gelu(t, j)

                for k in range(2 * sets):
                    split_high(k)
                act.wait_ge(bias_loaded, 32)
                in_pairs(act, tile)

            @block.vector
            def _(dve):
                def split_h(t, j):
                    dve.wait_ge(gelu_done, steps * t + j + 1)
                    if not (isinstance(t, int) and t == 0 and j < slots):
                        dve.wait_ge(h_used, steps * t + j - slots + 1)
                    nc.vector.tensor_copy(h_high[:, j % slots], h[:, j % 2]).then_inc(h_high_done, 1)
                    dve.wait_ge(h_high_done, steps * t + j + 1)
                    nc.vector.tensor_tensor(h_low[:, j % slots], h[:, j % 2], h_high[:, j % slots].bitcast(F32),
                                            ALU.subtract).then_inc(h_ready, 1)

                def add_bias(t, u):
                    dve.wait_ge(x_loaded[u], 16 * (t // 2 + 1))
                    for s in range(SUB):
                        nc.vector.tensor_tensor(x[:, u, s], x[:, u, s], b2_row[:], ALU.add).then_inc(bias_added, 1)

                def finish(t, u):
                    dve.wait_ge(h_used, steps * (t + 1))
                    dve.wait_ge(bias_added, SUB * (t + 1))
                    for s in range(SUB):
                        nc.vector.tensor_tensor(x[:, u, s], out_sum[:, s], x[:, u, s], ALU.add).then_inc(out_done, 1)

                def tile(t, u):
                    for j in range(steps):
                        split_h(t, j)
                        if j == lag - 1 and not (isinstance(t, int) and t == 0):
                            finish(t - 1, 1 - u)
                        if j == lag + 1:
                            add_bias(t, u)

                for k in range(2 * sets):
                    dve.wait_ge(w_high_done, k + 1)
                    high, low = (w1_high, w1_low) if k % 2 == 0 else (w2_high, w2_low)
                    nc.vector.tensor_tensor(low[:, k // 2], raw[:, k % 2], high[:, k // 2].bitcast(F32),
                                            ALU.subtract).then_inc(w_ready, 1)
                dve.wait_ge(bias_loaded, 32)
                in_pairs(dve, tile)
                finish(tiles - 1, 1)


def transformer_block(nc, x, ctx_t, mask, ln0_w, ln0_b, wq, wk, wv, sa_w, ln1_w, ln1_b, cq_w, ck_w, cv_w, ca_w,
                      ln2_w, ln2_b, fc1_w, fc1_b, fc2_w, fc2_b, out):
    tokens, dim = x.shape
    batches, batch_keys = mask.shape

    def scratch(name, shape):
        return nc.dram_tensor(name, shape, F32, kind="Internal").ap()

    q_t = scratch("q_t", [2, dim, tokens])
    k_t = scratch("k_t", [2, dim, tokens])
    v = scratch("v", [tokens, dim])
    self_t = scratch("self_t", [2, dim, tokens])
    x1 = scratch("x1", [tokens, dim])
    cq_t = scratch("cq_t", [2, dim, tokens])
    ck_t = scratch("ck_t", [2, dim, batches * batch_keys])
    cv = scratch("cv", [batches * batch_keys, dim])
    mask_rows = scratch("mask_rows", [batches, 2, batch_keys])
    cross_t = scratch("cross_t", [2, dim, tokens])
    x2 = scratch("x2", [tokens, dim])
    xn_t = scratch("xn_t", [2, dim, tokens])

    token_phase(nc, "qkv", x, ln0_w, ln0_b, v_w=wv, v_out=v, qk=[(wq, q_t), (wk, k_t)])
    attention_phase(nc, "self", q_t, k_t, v, self_t, tokens // batches, 1)
    context_phase(nc, ctx_t, mask, ck_w, cv_w, ck_t, cv, mask_rows)
    token_phase(nc, "mid", x, ln1_w, ln1_b, attn=self_t, proj_w=sa_w, x_out=x1, qk=[(cq_w, cq_t)])
    attention_phase(nc, "cross", cq_t, ck_t, cv, cross_t, batch_keys, 4, mask_rows)
    token_phase(nc, "late", x1, ln2_w, ln2_b, attn=cross_t, proj_w=ca_w, x_out=x2, xn_out=xn_t)
    mlp_phase(nc, x2, xn_t, fc1_w, fc1_b, fc2_w, fc2_b, out)


def kernel(**inputs):
    import numpy as np
    import concourse.bacc as bacc
    from concourse.bass_utils import run_bass_kernel_spmd

    def arr(name):
        return np.asarray(inputs[name])

    def turned(a):
        return np.ascontiguousarray(a.T)

    def columns(a):
        return np.ascontiguousarray(a.reshape(-1, P).T)

    x = arr("x")
    batches, length, dim = x.shape
    w = {k: arr(f"L0_xattn_{k}") for k in ("ln0_w", "ln0_b", "qkv_w", "sa_proj_w", "ln1_w", "ln1_b", "q_w", "k_w", "v_w",
                                           "ca_proj_w", "ln2_w", "ln2_b", "fc1_w", "fc1_b", "fc2_w", "fc2_b")}
    arrays = {
        "x": np.ascontiguousarray(x.reshape(batches * length, dim)),
        "ctx_t": turned(arr("ctx_1024").reshape(-1, dim)),
        "mask": np.ascontiguousarray(arr("mask_BxS2_ik0")),
        "ln0_w": columns(w["ln0_w"]), "ln0_b": columns(w["ln0_b"]),
        "wq": turned(w["qkv_w"][0:dim]), "wk": turned(w["qkv_w"][dim:2 * dim]), "wv": turned(w["qkv_w"][2 * dim:]),
        "sa_w": turned(w["sa_proj_w"]),
        "ln1_w": columns(w["ln1_w"]), "ln1_b": columns(w["ln1_b"]),
        "cq_w": turned(w["q_w"]), "ck_w": turned(w["k_w"]), "cv_w": turned(w["v_w"]), "ca_w": turned(w["ca_proj_w"]),
        "ln2_w": columns(w["ln2_w"]), "ln2_b": columns(w["ln2_b"]),
        "fc1_w": turned(w["fc1_w"]), "fc1_b": columns(w["fc1_b"]),
        "fc2_w": turned(w["fc2_w"]), "fc2_b": np.ascontiguousarray(w["fc2_b"]),
    }
    nc = bacc.Bacc("TRN2", target_bir_lowering=False, num_devices=1)
    args = [nc.dram_tensor(f"in_{k}", a.shape, mybir.dt.from_np(a.dtype), kind="ExternalInput").ap()
            for k, a in arrays.items()]
    out = nc.dram_tensor("out", [batches * length, dim], F32, kind="ExternalOutput").ap()
    transformer_block(nc, *args, out)
    r = run_bass_kernel_spmd(nc, [{f"in_{k}": a for k, a in arrays.items()}], core_ids=[0])
    return r.results[0]["out"].reshape(batches, length, dim)
```

```python
import math
from contextlib import ExitStack

import concourse.bass as bass
from concourse import mybir

P = 128
ALU = mybir.AluOpType
ACT = mybir.ActivationFunctionType
F32 = mybir.dt.float32
F32R = mybir.dt.float32r
I32 = mybir.dt.int32
AX_X = mybir.AxisListType.X

HEAD_DIM = 32
HEADS_PER_GROUP = P // HEAD_DIM
TOK = 512
SUB = TOK // P
EPS = 1e-5
MASK_BIAS = -10000.0



class Memory:

    def __init__(self, nc, stack, phase):
        self.nc, self.stack, self.phase, self.sems = nc, stack, phase, []
        stack.callback(self.release)

    def release(self):
        self.nc.clear_and_free_semaphores(self.sems)
        self.nc.all_engine_barrier()

    def sbuf(self, name, shape, dtype=F32):
        return self.stack.enter_context(self.nc.sbuf_tensor(f"{self.phase}_{name}", shape, dtype))

    def psum(self, name, shape):
        return self.stack.enter_context(self.nc.psum_tensor(f"{self.phase}_{name}", shape, F32))

    def sem(self, name):
        self.sems.append(self.nc.alloc_semaphore(f"{self.phase}_{name}"))
        return self.sems[-1]


def wait_alone(eng, sem, value, passed):
    eng.wait_ge(sem, value)
    eng.sem_inc(passed, 1)


def product(nc, out, left, right, first, last):
    (left_high, left_low), (right_high, right_low) = left, right
    nc.tensor.matmul(out, left_high, right_high, start=first, stop=False)
    nc.tensor.matmul(out, left_high, right_low, start=False, stop=False)
    return nc.tensor.matmul(out, left_low, right_high, start=False, stop=last)


def make_identity(nc, pool, identity, ident_done):
    nc.gpsimd.memset(identity[:], 0.0).then_inc(ident_done, 1)
    pool.wait_ge(ident_done, 1)
    nc.gpsimd.affine_select(out=identity[:], in_=identity[:], compare_op=ALU.not_equal, fill=1.0, base=0,
                            pattern=[[-1, P]], channel_multiplier=1).then_inc(ident_done, 1)


def token_phase(nc, name, x_in, ln_w, ln_b, attn=None, proj_w=None, x_out=None, v_w=None, v_out=None,
                qk=(), xn_out=None):
    dim = x_in.shape[1]
    tiles = x_in.shape[0] // TOK
    chunks = dim // P
    out_groups = dim // P
    n_v = SUB if v_w is not None else 0
    n_qk = len(qk) * out_groups
    n_out = n_v + n_qk
    n_early = n_out - out_groups if n_out > out_groups else n_out // 2
    slots = 4
    weights = ([proj_w] if proj_w is not None else []) + ([v_w] if v_w is not None else []) + [w for w, _ in qk]
    i_proj = 0
    i_v = 1 if proj_w is not None else 0
    i_qk = i_v + (1 if v_w is not None else 0)

    with ExitStack() as stack:
        m = Memory(nc, stack, name)
        w_raw = m.sbuf("w_raw", [P, 2, chunks, dim])
        w_high = m.sbuf("w_high", [P, len(weights), chunks, dim], F32R) if weights else None
        w_low = m.sbuf("w_low", [P, len(weights), chunks, dim], F32R) if weights else None
        gain = m.sbuf("gain", [P, chunks])
        shift = m.sbuf("shift", [P, chunks])
        identity = m.sbuf("identity", [P, P])
        x = m.sbuf("x", [P, 2, SUB, dim])
        stats = m.sbuf("stats", [P, SUB, 6])
        moments = m.sbuf("moments", [P, SUB, 2])
        var = m.sbuf("var", [P, SUB])
        rstd = m.sbuf("rstd", [P, SUB])
        minus_half = m.sbuf("minus_half", [P, SUB])
        xn = m.sbuf("xn", [P, 2, SUB, dim])
        xt = m.sbuf("xt", [P, chunks, TOK])
        xt_high = m.sbuf("xt_high", [P, 2, chunks, TOK], F32R)
        xt_low = m.sbuf("xt_low", [P, 2, chunks, TOK], F32R)
        if attn is not None:
            a_raw = m.sbuf("a_raw", [P, 2, chunks, TOK])
            a_high = m.sbuf("a_high", [P, 2, chunks, TOK], F32R)
            a_low = m.sbuf("a_low", [P, 2, chunks, TOK], F32R)
        if n_qk:
            r_high = m.sbuf("r_high", [P, slots, TOK], F32R)
            r_low = m.sbuf("r_low", [P, slots, TOK], F32R)
        if n_v:
            v_sb = m.sbuf("v_sb", [P, SUB, dim])
        n_proj = SUB if attn is not None else 0
        n_result = 0 if not n_out else 2 if n_proj else 4
        n_turned = min(chunks, 8 - n_result - n_proj)
        projected = m.psum("projected", [P, n_proj, TOK]) if n_proj else None
        turned = m.psum("turned", [P, n_turned, TOK])
        result = m.psum("result", [P, n_result, TOK]) if n_result else None

        w_loaded = [m.sem(f"w_loaded{k}") for k in range(2)]
        w_high_done = m.sem("w_high_done")
        w_ready = m.sem("w_ready")
        ln_loaded = m.sem("ln_loaded")
        ident_done = m.sem("ident_done")
        waits_passed = m.sem("waits_passed")
        x_loaded = [m.sem(f"x_loaded{u}") for u in range(2)]
        a_loaded = [m.sem(f"a_loaded{u}") for u in range(2)]
        a_high_done = m.sem("a_high_done")
        a_ready = m.sem("a_ready")
        x_stored = [m.sem(f"x_stored{u}") for u in range(2)]
        proj_done = m.sem("proj_done")
        x_ready = m.sem("x_ready")
        stats_done = m.sem("stats_done")
        moments_done = m.sem("moments_done")
        var_done = m.sem("var_done")
        rstd_done = m.sem("rstd_done")
        xn_ready = m.sem("xn_ready")
        turn_done = m.sem("turn_done")
        xt_done = m.sem("xt_done")
        xt_high_done = m.sem("xt_high_done")
        xt_ready = m.sem("xt_ready")
        xt_stored = [m.sem(f"xt_stored{u}") for u in range(2)]
        result_done = m.sem("result_done")
        high_done = m.sem("high_done")
        result_read = m.sem("result_read")
        stored = [m.sem(f"stored{k}") for k in range(slots)]
        v_stored = [m.sem(f"v_stored{s}") for s in range(SUB)]

        x_view = x_in.rearrange("(t s p) d -> t p s d", p=P, s=SUB)

        with nc.Block() as block:

            @block.sync
            def _(sp):
                def load_attn(t, u):
                    sp.dma_start(a_raw[:, u], attn.rearrange("(c p) t -> p c t", p=P)[:, :, bass.ds(t * TOK, TOK)]
                                 ).then_inc(a_loaded[u], 16)

                def load_x(t, u):
                    sp.dma_start(x[:, u], x_view[t]).then_inc(x_loaded[u], 16)

                if attn is not None:
                    load_attn(0, 0)
                load_x(0, 0)
                sp.dma_start(gain[:], ln_w).then_inc(ln_loaded, 16)
                sp.dma_start(shift[:], ln_b).then_inc(ln_loaded, 16)
                for k, w in enumerate(weights):
                    if k >= 2:
                        sp.wait_ge(w_ready, k - 1)
                    sp.dma_start(w_raw[:, k % 2], w.rearrange("(c p) n -> p c n", p=P)).then_inc(w_loaded[k % 2], 16)
                if attn is not None:
                    load_attn(1, 1)
                load_x(1, 1)

                def store_results(t, u, items):
                    for n in items:
                        wait_alone(sp, result_read, t * n_out + n + 1, waits_passed)
                        if n < n_v:
                            sp.dma_start(v_out[bass.ds(t * TOK + n * P, P), :], v_sb[:, n]).then_inc(v_stored[n], 16)
                        else:
                            k = n - n_v
                            to, group = qk[k // out_groups][1], k % out_groups
                            for part, src in ((0, r_high), (1, r_low)):
                                sp.dma_start(to[part, group * P:(group + 1) * P, bass.ds(t * TOK, TOK)],
                                             src[:, k % slots].bitcast(F32)).then_inc(stored[k % slots], 16)

                def tile_traffic(t, u, reload, reload_attn):
                    if x_out is not None:
                        wait_alone(sp, x_ready, SUB * (t + 1), waits_passed)
                        sp.dma_start(x_out.rearrange("(t s p) d -> t p s d", p=P, s=SUB)[t], x[:, u]).then_inc(
                            x_stored[u], 16)
                    if xn_out is not None:
                        wait_alone(sp, xt_ready, chunks * (t + 1), waits_passed)
                        for part, src in ((0, xt_high), (1, xt_low)):
                            sp.dma_start(xn_out[part].rearrange("(c p) t -> p c t", p=P)[:, :, bass.ds(t * TOK, TOK)],
                                         src[:, u].bitcast(F32)).then_inc(xt_stored[u], 16)
                    if reload:
                        wait_alone(sp, xn_ready, SUB * (t + 1), waits_passed)
                        if x_out is not None:
                            wait_alone(sp, x_stored[u], 16 * (t // 2 + 1), waits_passed)
                        load_x(t + 2, u)
                    if reload_attn and attn is not None:
                        wait_alone(sp, a_ready, t + 3, waits_passed)
                        load_attn(t + 4, u)
                    store_results(t, u, range(n_out))

                if attn is not None:
                    sp.wait_ge(a_ready, 1)
                    load_attn(2, 0)
                    sp.wait_ge(a_ready, 2)
                    load_attn(3, 1)
                with sp.Fori(0, tiles // 2 - 2) as pair:
                    tile_traffic(2 * pair, 0, True, True)
                    tile_traffic(2 * pair + 1, 1, True, True)
                tile_traffic(tiles - 4, 0, True, False)
                tile_traffic(tiles - 3, 1, True, False)
                tile_traffic(tiles - 2, 0, False, False)
                tile_traffic(tiles - 1, 1, False, False)
                for u in range(2):
                    if x_out is not None:
                        sp.wait_ge(x_stored[u], 16 * tiles // 2)
                    if xn_out is not None:
                        sp.wait_ge(xt_stored[u], 32 * tiles // 2)
                for k in range(slots if n_qk else 0):
                    sp.wait_ge(stored[k], 32 * tiles * (n_qk // slots))
                for s in range(n_v):
                    sp.wait_ge(v_stored[s], 16 * tiles)

            @block.gpsimd
            def _(pool):
                make_identity(nc, pool, identity, ident_done)
                nc.gpsimd.memset(minus_half[:], -0.5).then_inc(ident_done, 1)
                pool.wait_ge(ident_done, 3)

                def inverse_root(t):
                    pool.wait_ge(var_done, 2 * (t + 1))
                    nc.gpsimd.tensor_tensor(rstd[:], var[:], minus_half[:], ALU.pow).then_inc(rstd_done, 1)

                def low_attn(t, u):
                    pool.wait_ge(a_high_done, t + 1)
                    nc.gpsimd.tensor_tensor(a_low[:, u], a_raw[:, u], a_high[:, u].bitcast(F32), ALU.subtract).then_inc(
                        a_ready, 1)

                if attn is None:
                    with pool.Fori(0, tiles) as t:
                        inverse_root(t)
                else:
                    low_attn(0, 0)
                    low_attn(1, 1)
                    inverse_root(0)
                    low_attn(2, 0)
                    inverse_root(1)
                    low_attn(3, 1)
                    with pool.Fori(1, tiles // 2 - 1) as pair:
                        inverse_root(2 * pair)
                        low_attn(2 * pair + 2, 0)
                        inverse_root(2 * pair + 1)
                        low_attn(2 * pair + 3, 1)
                    inverse_root(tiles - 2)
                    inverse_root(tiles - 1)

            @block.tensor
            def _(pe):
                def w_parts(k, c, cols):
                    return w_high[:, k, c, cols], w_low[:, k, c, cols]

                def project(t, u):
                    pe.wait_ge(a_ready, t + 1)
                    if isinstance(t, int) and t == 0:
                        pe.wait_ge(w_ready, i_proj + 1)
                    for s in range(SUB):
                        if not (isinstance(t, int) and SUB * t + s - n_proj < 0):
                            pe.wait_ge(x_ready, SUB * t + s - n_proj + 1)
                        cols = slice(s * P, (s + 1) * P)
                        for c in range(chunks):
                            mm = product(nc, projected[:, s % n_proj], (a_high[:, u, c, cols], a_low[:, u, c, cols]),
                                         w_parts(i_proj, c, slice(0, dim)), c == 0, c == chunks - 1)
                        mm.then_inc(proj_done, 1)

                def turn(t, u):
                    pe.wait_ge(xn_ready, SUB * (t + 1))
                    for c in range(chunks):
                        if not (isinstance(t, int) and chunks * t + c - n_turned < 0):
                            pe.wait_ge(xt_high_done, chunks * t + c - n_turned + 1)
                        for s in range(SUB):
                            mm = nc.tensor.transpose(turned[:, c % n_turned, s * P:(s + 1) * P],
                                                     xn[:, u, s, c * P:(c + 1) * P], identity[:])
                        mm.then_inc(turn_done, 1)

                def results(t, u, items):
                    for n in items:
                        if not (isinstance(t, int) and t == 0 and n < n_result):
                            pe.wait_ge(result_read, t * n_out + n - n_result + 1)
                        for c in range(chunks):
                            if n < n_v:
                                mm = product(nc, result[:, n % n_result],
                                             (xt_high[:, u, c, n * P:(n + 1) * P], xt_low[:, u, c, n * P:(n + 1) * P]),
                                             w_parts(i_v, c, slice(0, dim)), c == 0, c == chunks - 1)
                            else:
                                k = n - n_v
                                group = k % out_groups
                                mm = product(nc, result[:, n % n_result],
                                             w_parts(i_qk + k // out_groups, c, slice(group * P, (group + 1) * P)),
                                             (xt_high[:, u, c], xt_low[:, u, c]), c == 0, c == chunks - 1)
                        mm.then_inc(result_done, 1)

                def body(t, u, has_next, has_second):
                    if n_out:
                        pe.wait_ge(xt_ready, chunks * (t + 1))
                        if isinstance(t, int) and t == 0:
                            pe.wait_ge(w_ready, len(weights))
                        results(t, u, range(n_early))
                    if has_second and attn is not None:
                        project(t + 2, u)
                    if has_next:
                        turn(t + 1, 1 - u)
                    results(t, u, range(n_early, n_out))

                pe.wait_ge(ident_done, 2)
                if attn is not None:
                    project(0, 0)
                turn(0, 0)
                if attn is not None:
                    project(1, 1)
                body(0, 0, True, True)
                body(1, 1, True, True)
                with pe.Fori(1, tiles // 2 - 1) as pair:
                    body(2 * pair, 0, True, True)
                    body(2 * pair + 1, 1, True, True)
                body(tiles - 2, 0, True, False)
                body(tiles - 1, 1, False, False)

            @block.scalar
            def _(act):
                def split_turned(t, u):
                    for c in range(chunks):
                        act.wait_ge(turn_done, chunks * t + c + 1)
                        if not (isinstance(t, int) and t == 0):
                            act.wait_ge(xt_ready, chunks * (t - 1) + c + 1)
                        nc.scalar.activation(xt[:, c], turned[:, c % n_turned], ACT.Identity, bias=shift[:, c:c + 1],
                                             scale=gain[:, c:c + 1]).then_inc(xt_done, 1)
                        if xn_out is not None and not (isinstance(t, int) and t < 2):
                            act.wait_ge(xt_stored[u], 32 * (t // 2))
                        nc.scalar.activation(xt_high[:, u, c], turned[:, c % n_turned], ACT.Identity, bias=shift[:, c:c + 1],
                                             scale=gain[:, c:c + 1]).then_inc(xt_high_done, 1)

                def high_parts(t, items):
                    for n in items:
                        if n < n_v:
                            continue
                        k = n - n_v
                        act.wait_ge(result_done, t * n_out + n + 1)
                        act.wait_ge(stored[k % slots], 32 * (t * (n_qk // slots) + k // slots))
                        nc.scalar.activation(r_high[:, k % slots], result[:, n % n_result], ACT.Copy).then_inc(high_done, 1)

                def high_attn(t, u):
                    act.wait_ge(a_loaded[u], 16 * (t // 2 + 1))
                    if not (isinstance(t, int) and t < 2):
                        act.wait_ge(proj_done, SUB * (t - 1))
                    nc.scalar.activation(a_high[:, u], a_raw[:, u], ACT.Copy).then_inc(a_high_done, 1)

                if attn is not None:
                    high_attn(0, 0)
                for k in range(len(weights)):
                    act.wait_ge(w_loaded[k % 2], 16 * (k // 2 + 1))
                    nc.scalar.activation(w_high[:, k], w_raw[:, k % 2], ACT.Copy).then_inc(w_high_done, 1)
                act.wait_ge(ln_loaded, 32)

                def body(t, u, has_next, has_third):
                    high_parts(t, range(n_early))
                    if has_third and attn is not None:
                        high_attn(t + 3, 1 - u)
                    if has_next:
                        split_turned(t + 1, 1 - u)
                    high_parts(t, range(n_early, n_out))

                if attn is not None:
                    high_attn(1, 1)
                split_turned(0, 0)
                if attn is not None:
                    high_attn(2, 0)
                body(0, 0, True, True)
                body(1, 1, True, True)
                with act.Fori(1, tiles // 2 - 2) as pair:
                    body(2 * pair, 0, True, True)
                    body(2 * pair + 1, 1, True, True)
                body(tiles - 4, 0, True, True)
                body(tiles - 3, 1, True, False)
                body(tiles - 2, 0, True, False)
                body(tiles - 1, 1, False, False)

            @block.vector
            def _(dve):
                def add_projection(t, u):
                    dve.wait_ge(x_loaded[u], 16 * (t // 2 + 1))
                    for s in range(SUB):
                        dve.wait_ge(proj_done, SUB * t + s + 1)
                        nc.vector.tensor_tensor(x[:, u, s], projected[:, s % n_proj], x[:, u, s], ALU.add).then_inc(
                            x_ready, 1)

                def norm(t, u):
                    if attn is None:
                        dve.wait_ge(x_loaded[u], 16 * (t // 2 + 1))
                    if not (isinstance(t, int) and t == 0):
                        dve.wait_ge(xn_ready, SUB * t)

                    def stats_of(s):
                        if attn is not None:
                            dve.wait_ge(x_ready, SUB * t + s + 1)
                        return nc.vector.bn_stats(stats[:, s], x[:, u, s]).then_inc(stats_done, 1)

                    def moments_of(s):
                        nc.vector.bn_aggr(moments[:, s], stats[:, s]).then_inc(moments_done, 1)

                    def var_of(a, b):
                        dve.wait_ge(moments_done, SUB * t + b)
                        nc.vector.tensor_scalar(var[:, a:b], moments[:, a:b, 1], EPS, None, ALU.add).then_inc(var_done, 1)

                    half = SUB // 2
                    for s in range(half):
                        stats_of(s)
                    dve.wait_ge(stats_done, SUB * t + half)
                    for s in range(half, SUB):
                        stats_of(s)
                    for s in range(half):
                        moments_of(s)
                    dve.wait_ge(stats_done, SUB * (t + 1))
                    var_of(0, half)
                    for s in range(half, SUB):
                        moments_of(s)
                    var_of(half, SUB)
                    dve.wait_ge(rstd_done, t + 1)
                    for s in range(SUB):
                        nc.vector.tensor_scalar(xn[:, u, s], x[:, u, s], moments[:, s, 0:1], rstd[:, s:s + 1],
                                                ALU.subtract, ALU.mult).then_inc(xn_ready, 1)

                def low_turned(t, u):
                    for c in range(chunks):
                        dve.wait_ge(xt_high_done, chunks * t + c + 1)
                        nc.vector.tensor_tensor(xt_low[:, u, c], xt[:, c], xt_high[:, u, c].bitcast(F32),
                                                ALU.subtract).then_inc(xt_ready, 1)

                def low_parts(t, items):
                    for n in items:
                        if n < n_v:
                            dve.wait_ge(result_done, t * n_out + n + 1)
                            dve.wait_ge(v_stored[n], 16 * t)
                            nc.vector.tensor_copy(v_sb[:, n], result[:, n % n_result]).then_inc(result_read, 1)
                        else:
                            k = n - n_v
                            dve.wait_ge(high_done, t * n_qk + k + 1)
                            nc.vector.tensor_tensor(r_low[:, k % slots], result[:, n % n_result],
                                                    r_high[:, k % slots].bitcast(F32), ALU.subtract).then_inc(result_read, 1)

                def body(t, u, has_next, has_second):
                    if has_next:
                        norm(t + 1, 1 - u)
                    if has_second and attn is not None:
                        add_projection(t + 2, u)
                    low_parts(t, range(n_early))
                    if has_next:
                        low_turned(t + 1, 1 - u)
                    low_parts(t, range(n_early, n_out))

                for k in range(len(weights)):
                    dve.wait_ge(w_high_done, k + 1)
                    nc.vector.tensor_tensor(w_low[:, k], w_raw[:, k % 2], w_high[:, k].bitcast(F32),
                                            ALU.subtract).then_inc(w_ready, 1)
                    if k == 0:
                        if attn is not None:
                            add_projection(0, 0)
                        norm(0, 0)
                if attn is not None:
                    add_projection(1, 1)
                low_turned(0, 0)
                body(0, 0, True, True)
                body(1, 1, True, True)
                with dve.Fori(1, tiles // 2 - 1) as pair:
                    body(2 * pair, 0, True, True)
                    body(2 * pair + 1, 1, True, True)
                body(tiles - 2, 0, True, False)
                body(tiles - 1, 1, False, False)


def order_of_work(steps, heads, n_parts, products, sums, n_sums, first_steps, item_cost):
    group_cost = 4.3
    exp_cost = 2.2
    bank_turn = 4.6
    pool_cost = 20.8
    signal = 1.2
    products, sums = list(products), list(sums)
    order = []
    clock = 0.0
    second = first = 0
    second_end = [-9.0, -9.0]
    item_read = [-9.0, -9.0]
    exp_end = []
    exp_free, pool_free = 0.0, 22.0
    sum_ready = {}
    while second < steps * heads or first < n_parts or products or sums:
        behind = first < n_parts * (second / heads / first_steps + 0.02)
        choices = []
        if second < steps * heads and first >= min(n_parts, n_parts * (second / heads / first_steps - 0.04)):
            if second // heads - 4 not in [n + of * steps for _, (_, n, of) in products]:
                choices.append((second_end[-2] + bank_turn, 0, "second"))
        if first < n_parts and behind:
            choices.append((item_read[-2] + signal if first % 2 == 0 else 0.0, 1, "first"))
        if products:
            step, (_, n, of) = products[0]
            if second >= step * heads and (of == -1 or len(exp_end) >= heads * (n + 1)):
                late = second >= (step - 1) * heads + 6
                choices.append((exp_end[heads * (n + 1) - 1] + signal if of == 0 else 0.0, 0.5 if late else 2, "product"))
        if sums:
            step, (_, n, of) = sums[0]
            if second >= step * heads and of == -1:
                choices.append(((22.0 if n == n_sums - 1 else 4.0) + signal, 2.5, "sum"))
            elif second >= step * heads and n in sum_ready:
                choices.append((sum_ready[n] + signal, 2.5, "sum"))
        if not choices:
            choices = [(0.0, 0, "first" if first < n_parts else "product" if products else "sum")]
        ready = [choice for choice in choices if choice[0] <= clock]
        start, _, what = min(ready, key=lambda choice: choice[1]) if ready else min(choices)
        clock = max(clock, start)
        if what == "second":
            order.append(("second", second, 0))
            clock += 1
            second_end.append(clock)
            exp_free = max(exp_free + 0.2, clock + 0.9) + exp_cost
            exp_end.append(exp_free)
            second += 1
            if second % (2 * heads) == 0:
                pool_free = max(pool_free, exp_free + 0.6) + pool_cost
                sum_ready[second // (2 * heads) - 1] = pool_free
        elif what == "first":
            order.append(("first", first, 1))
            clock += 1
            if first % 2 == 1:
                item_read.append(max(item_read[-1] + 0.4, clock + 0.6) + item_cost)
            first += 1
        else:
            order.append((products if what == "product" else sums).pop(0)[1])
            clock += group_cost
    return order


def attention_phase(nc, name, q_t, k_t, v, out, keys, tiles_per_stage, mask_rows=None):
    tokens = q_t.shape[2]
    batches = k_t.shape[2] // keys
    features = q_t.shape[1]
    groups_per_batch = features // P
    r_tiles = tiles_per_stage
    span = r_tiles * TOK
    stages_per_group = tokens // batches // span
    groups = batches * groups_per_batch
    stages = groups * stages_per_group
    heads = HEADS_PER_GROUP
    scale = 1.0 / math.sqrt(HEAD_DIM)
    masked = mask_rows is not None
    base = 3 * HEAD_DIM
    score_rows = base + (2 if masked else 0)
    exp_rows = score_rows + 2
    long = keys >= TOK
    n_k = -(-keys // P)
    width = keys // n_k
    assert width * n_k == keys and n_k % 2 == 0
    steps = r_tiles * n_k
    set_size = 4 if long else 1
    sets = [list(range(k, k + set_size)) for k in range(0, n_k, set_size)]
    head_sets = [[a] for a in range(heads)] if long else [list(range(heads))]
    item_banks = 2 if long else 1
    if long:
        items = [(a, s, k0) for a in range(heads) for s in range(r_tiles * SUB) for k0 in range(0, keys, 2 * TOK)]
    else:
        items = [(a, s, 0) for a in range(heads) for s in range(0, r_tiles * SUB, 2)]
    n_items = len(items)
    per_head = n_items // heads
    n_reads = n_items + 1
    n_max = heads * r_tiles * SUB
    n_turned = n_max if n_max <= 32 else P
    p_slots = 4
    sums_per_tile = n_k // 2
    n_sums = r_tiles * sums_per_tile
    n_acc = 2 if r_tiles > 1 else 1
    v_lag = 2
    sum_lag = 4
    first_steps = 13.5 if long else 3.5
    item_cost = 5.2 if long else 1.8
    divide_late = n_acc == 1

    due = [[] for _ in range(2 * steps)]
    for t in range(steps):
        due[t + v_lag].append(("weigh", t))
    for p in range(n_sums):
        r, k = p // sums_per_tile, p % sums_per_tile
        at = r * n_k + 2 * k + sum_lag
        if n_acc == 1:
            at = min(at, (r + 1) * n_k + v_lag - 1)
        due[at].append(("add_up", p))
    n_parts = 2 * n_items
    jobs = [(t, (what, n, of)) for of in (-1, 0) for t in range(steps) for what, n in due[t - of * steps]]
    products = [job for job in jobs if job[1][0] == "weigh"]
    sum_jobs = [job for job in jobs if job[1][0] == "add_up"]
    schedule = order_of_work(steps, heads, n_parts, products, sum_jobs, n_sums, first_steps, item_cost)
    at = schedule.index(("first", n_parts - 1, 1))
    for _ in range(2):
        at += 1
        while schedule[at][0] != "second":
            at += 1
    schedule.insert(at + 1, ("turn", 0, 1))
    tail = [(what, n, 0) for t in range(steps, 2 * steps) for what, n in due[t]]

    def put(job, after, n_seconds):
        at, (what, n, of) = schedule.index(after), job
        while n_seconds:
            at += 1
            if at == len(schedule):
                at, of = 0, of - 1
            n_seconds -= schedule[at][0] == "second"
        schedule.insert(at + 1, (what, n, of))

    for r in range(r_tiles):
        last_product = [job for job in schedule if job[0] == "weigh" and job[1] == (r + 1) * n_k - 1][0]
        last_sum = [job for job in schedule if job[0] == "add_up" and job[1] == (r + 1) * sums_per_tile - 1][0]
        of = last_sum[2]
        if divide_late:
            put(("take_weighted", r, last_product[2]), last_product, 1)
            put(("take_total", r, of), last_sum, 1)
            schedule.append(("divide", r, of))
        else:
            put(("divide", r, of), last_sum, 0)
            put(("take_weighted", r, of), last_sum, 0)
            put(("take_total", r, of), last_sum, 0)
    tail += [(what, r, 0) for r in range(r_tiles) for what in ("take_weighted", "take_total", "divide")
             if (what, r, -1) in schedule]

    position = {job: n for n, job in enumerate(schedule)}
    store_delay = len(schedule) // steps
    traffic = []
    for job, n in position.items():
        what, number, of = job
        if what == "divide":
            at = n + (0 if divide_late else store_delay)
            traffic.append((at % len(schedule), "store", number, of - (at >= len(schedule))))
        if what == "first" and number % 2 == 1:
            for h, members in enumerate(head_sets):
                if number // 2 == per_head * (members[-1] + 1) - 1:
                    traffic.append((n, "heads", h, of))
        if what == "turn":
            traffic.append((n, "max", 0, of))
        for j, tiles in enumerate(sets):
            if what == "second" and number == heads * (steps - n_k + tiles[-1]) + heads - 1:
                traffic.append((n, "k", j, of))
            if what == "weigh" and number == steps - n_k + tiles[-1]:
                traffic.append((n, "v", j, of))
    traffic.sort(key=lambda event: event[0])
    assert len([event for event in traffic if event[1] == "store"]) == r_tiles

    with ExitStack() as stack:
        m = Memory(nc, stack, name)
        k_move = m.sbuf("k_move", [P, heads, keys], F32R)
        k_hold = m.sbuf("k_hold", [P, heads, keys], F32R)
        q_hold = m.sbuf("q_hold", [P, heads, span], F32R)
        q_move = m.sbuf("q_move", [P, 2, heads, span], F32R)
        v_sb = m.sbuf("v_sb", [P, n_k, P])
        expo = m.sbuf("expo", [P, p_slots, heads, TOK])
        pair_sum = m.sbuf("pair_sum", [P, 2, heads, TOK])
        ones = m.sbuf("ones", [P, HEAD_DIM])
        identity = m.sbuf("identity", [P, P])
        part_max = m.sbuf("part_max", [P, n_max, keys // (2 * TOK)]) if long else None
        row_max = m.sbuf("row_max", [P, n_turned])
        max_high = m.sbuf("max_high", [n_max, P], F32R)
        max_low = m.sbuf("max_low", [n_max, P], F32R)
        sums = m.sbuf("sums", [P, TOK])
        inverse = m.sbuf("inverse", [P, TOK])
        unscaled = m.sbuf("unscaled", [P, TOK])
        mean = m.sbuf("mean", [P, 2, TOK])
        first = m.psum("first", [P, 2, item_banks * TOK])
        second = m.psum("second", [P, 2, TOK])
        weighted = m.psum("weighted", [P, n_acc, TOK])
        total = m.psum("total", [P, n_acc, TOK])

        ident_done = m.sem("ident_done")
        first_constants = m.sem("first_constants")
        second_constants = m.sem("second_constants")
        k_move_loaded = [m.sem(f"k_move_loaded{h}") for h in range(len(head_sets))]
        k_hold_loaded = [m.sem(f"k_hold_loaded{j}") for j in range(len(sets))]
        v_loaded = [m.sem(f"v_loaded{j}") for j in range(len(sets))]
        q_hold_loaded = [m.sem(f"q_hold_loaded{h}") for h in range(len(head_sets))]
        q_move_loaded = m.sem("q_move_loaded")
        max_loaded = m.sem("max_loaded")
        first_done = m.sem("first_done")
        first_read = m.sem("first_read")
        row_max_done = m.sem("row_max_done")
        turned = m.sem("turned")
        max_high_done = m.sem("max_high_done")
        second_done = m.sem("second_done")
        exp_done = m.sem("exp_done")
        pair_done = m.sem("pair_done")
        weighted_done = m.sem("weighted_done")
        total_done = m.sem("total_done")
        sums_read = m.sem("sums_read")
        weighted_read = m.sem("weighted_read")
        inverse_done = m.sem("inverse_done")
        mean_done = m.sem("mean_done")
        out_stored = [m.sem(f"out_stored{u}") for u in range(2)]
        waits_passed = m.sem("waits_passed")

        def ge(eng, sem, value, alone=False):
            if isinstance(value, int) and value <= 0:
                return
            if alone and not isinstance(value, int):
                wait_alone(eng, sem, value, waits_passed)
            else:
                eng.wait_ge(sem, value)

        k_count = 16 * (3 + masked)
        n_constants = 2 + masked

        with nc.Block() as block:

            @block.sync
            def _(sp):
                def stacked(dst, src, parts, rows, cols, sem):
                    for j, part in enumerate(parts):
                        sp.dma_start(dst[j * HEAD_DIM:(j + 1) * HEAD_DIM].bitcast(F32),
                                     src[part, rows, cols].rearrange("(a d) t -> d a t", d=HEAD_DIM)).then_inc(sem, 16)

                def group_of(g):
                    return g // groups_per_batch, g % groups_per_batch

                def mask_of(b, n_heads, k0, n):
                    return mask_rows[b, :, k0:k0 + n].unsqueeze(1).to_broadcast([2, n_heads, n])

                def load_k_move(g, h):
                    b, group = group_of(g)
                    a, n = head_sets[h][0], len(head_sets[h])
                    stacked(k_move[:, a:a + n], k_t, (0, 0, 1), bass.ds(group * P + a * HEAD_DIM, n * HEAD_DIM),
                            bass.ds(b * keys, keys), k_move_loaded[h])
                    if masked:
                        sp.dma_start(k_move[base:base + 2, a:a + n].bitcast(F32), mask_of(b, n, 0, keys)).then_inc(
                            k_move_loaded[h], 16)

                def load_k_hold(g, j):
                    b, group = group_of(g)
                    k0, n = sets[j][0] * width, len(sets[j]) * width
                    stacked(k_hold[:, :, k0:k0 + n], k_t, (0, 0, 1), bass.ds(group * P, P),
                            bass.ds(b * keys + k0, n), k_hold_loaded[j])
                    if masked:
                        sp.dma_start(k_hold[base:base + 2, :, k0:k0 + n].bitcast(F32), mask_of(b, heads, k0, n)).then_inc(
                            k_hold_loaded[j], 16)

                def load_v(g, j):
                    b, group = group_of(g)
                    k0, n = sets[j][0], len(sets[j])
                    sp.dma_start(v_sb[0:width, k0:k0 + n],
                                 v[bass.ds(b * keys + k0 * width, n * width), bass.ds(group * P, P)]
                                 .rearrange("(k p) d -> p k d", p=width)).then_inc(v_loaded[j], 16)

                def query_slice(i, r=0, n=span):
                    b, group = group_of(i // stages_per_group)
                    return group, bass.ds(b * (tokens // batches) + (i % stages_per_group) * span + r * TOK, n)

                def load_q_hold(i, h):
                    group, cols = query_slice(i)
                    a, n = head_sets[h][0], len(head_sets[h])
                    stacked(q_hold[:, a:a + n], q_t, (0, 1, 0), bass.ds(group * P + a * HEAD_DIM, n * HEAD_DIM), cols,
                            q_hold_loaded[h])

                def load_q_move(i):
                    group, cols = query_slice(i)
                    stacked(q_move[:, i % 2], q_t, (0, 1, 0), bass.ds(group * P, P), cols, q_move_loaded)

                def load_max(i):
                    ge(sp, first_read, n_reads * (i + 1), alone=True)
                    for row, src in ((score_rows, max_high), (score_rows + 1, max_low)):
                        sp.dma_start(q_move[row:row + 1, i % 2].rearrange("o a (s t) -> o (a s) t", t=P).bitcast(F32),
                                     src[:].bitcast(F32)).then_inc(max_loaded, 16)

                def store_out(i, r):
                    n = i * r_tiles + r
                    ge(sp, mean_done, n + 1, alone=True)
                    group, cols = query_slice(i, r, TOK)
                    sp.dma_start(out[bass.ds(group * P, P), cols], mean[:, r % n_acc]).then_inc(out_stored[r % n_acc], 16)

                def stage(i, g, qt):
                    first_one = isinstance(i, int) and i == 0
                    last = isinstance(i, int) and i == stages - 1
                    last2 = isinstance(i, int) and i >= stages - 2
                    new_next = (qt + 1) % stages_per_group == 0 and not last
                    new_after = (qt + 2) % stages_per_group == 0 and not last2
                    after = (i + 2) // stages_per_group if isinstance(i, int) or stages_per_group == 1 else g + 1
                    if not last:
                        ge(sp, second_done, heads * steps * i, alone=True)
                        ge(sp, q_move_loaded, 48 * (i + 1), alone=True)
                        load_q_move(i + 1)
                    for _, what, n, of in traffic:
                        if of == -1 and first_one:
                            continue
                        if what == "store":
                            store_out(i + of, n)
                        elif what == "max" and not last:
                            load_max(i + 1)
                        elif what == "heads" and not last2:
                            ge(sp, first_done, n_items * (i + 1) + per_head * (head_sets[n][-1] + 1), alone=True)
                            load_q_hold(i + 2, n)
                            if new_after:
                                load_k_move(after, n)
                        elif what == "k" and new_next:
                            ge(sp, second_done, heads * (steps * i + steps - n_k + sets[n][-1] + 1), alone=True)
                            load_k_hold(g + 1, n)
                        elif what == "v" and (new_next if of == 0 else qt == 0):
                            ge(sp, weighted_done, steps * (i + of) + steps - n_k + sets[n][-1] + 1, alone=True)
                            load_v(g + 1 + of, n)

                for h in range(len(head_sets)):
                    load_q_hold(0, h)
                    load_k_move(0, h)
                load_q_move(0)
                sp.wait_ge(second_constants, 1)
                for j in range(len(sets)):
                    load_k_hold(0, j)
                    load_v(0, j)
                for h in range(len(head_sets)):
                    if h == len(head_sets) - 1:
                        sp.wait_ge(second_constants, 3)
                        load_max(0)
                    sp.wait_ge(first_done, per_head * (head_sets[h][-1] + 1))
                    load_q_hold(1, h)
                    if stages_per_group == 1:
                        load_k_move(1, h)
                peel = max(1, 2 // stages_per_group)
                for g in range(peel):
                    for qt in range(stages_per_group):
                        stage(g * stages_per_group + qt, g, qt)
                with sp.Fori(peel, groups - 2) as g:
                    for qt in range(stages_per_group):
                        stage(g * stages_per_group + qt, g, qt)
                for g in range(groups - 2, groups):
                    for qt in range(stages_per_group):
                        stage(g * stages_per_group + qt, g, qt)
                for _, what, n, of in traffic:
                    if what == "store" and of == -1:
                        store_out(stages - 1, n)
                for u in range(n_acc):
                    sp.wait_ge(out_stored[u], 16 * stages * r_tiles // n_acc)

            @block.gpsimd
            def _(pool):
                make_identity(nc, pool, identity, ident_done)
                pool.wait_ge(ident_done, 2)
                nc.gpsimd.memset(k_hold[base:base + 4].bitcast(F32), -1.0).then_inc(second_constants, 1)
                for u in range(2):
                    pool.wait_ge(second_constants, u + 1)
                    nc.gpsimd.memset(q_move[base:base + 4, u].bitcast(F32), 1.0).then_inc(second_constants, 1)
                pool.wait_ge(second_constants, 3)

                def add_pairs(i):
                    for p in range(n_sums):
                        t = 2 * p
                        ge(pool, exp_done, heads * (steps * i + t + 2))
                        ge(pool, total_done, n_sums * i + p - 1)
                        nc.gpsimd.tensor_tensor(pair_sum[0:width, p % 2], expo[0:width, t % p_slots],
                                                expo[0:width, (t + 1) % p_slots], ALU.add).then_inc(pair_done, 1)

                add_pairs(0)
                with pool.Fori(1, stages) as i:
                    add_pairs(i)

            @block.tensor
            def _(pe):
                def first_pass(i, part):
                    n, half = part // 2, part % 2
                    a, s, k0 = items[n]
                    if half == 0:
                        for h, members in enumerate(head_sets):
                            if a == members[0] and n % per_head == 0:
                                ge(pe, q_hold_loaded[h], 48 * (i + 1))
                                ge(pe, k_move_loaded[h], k_count * (i // stages_per_group + 1))
                        ge(pe, first_read, n_reads * i + (n - 1 if n > 1 else 0))
                    if long:
                        mm = nc.tensor.matmul(first[:, n % 2, half * TOK:(half + 1) * TOK],
                                              q_hold[0:score_rows, a, s * P:(s + 1) * P],
                                              k_move[0:score_rows, a, k0 + half * TOK:k0 + (half + 1) * TOK],
                                              start=True, stop=True)
                    else:
                        mm = nc.tensor.matmul(first[:, n % 2, half * keys:(half + 1) * keys],
                                              q_hold[0:score_rows, a, (s + half) * P:(s + half + 1) * P],
                                              k_move[0:score_rows, a], start=True, stop=True)
                    if half == 1:
                        mm.then_inc(first_done, 1)

                def turn_max(i):
                    ge(pe, row_max_done, i + 1)
                    nc.tensor.transpose(first[0:n_turned, 0, 0:P], row_max[:], identity[:]).then_inc(turned, 1)

                def second_pass(i, n):
                    t, a = n // heads, n % heads
                    r, k = t // n_k, t % n_k
                    if a == 0 and r == 0:
                        for j, tiles in enumerate(sets):
                            if k == tiles[0]:
                                ge(pe, k_hold_loaded[j], k_count * (i // stages_per_group + 1))
                    if n == 0:
                        ge(pe, q_move_loaded, 48 * (i + 1))
                        ge(pe, max_loaded, 32 * (i + 1))
                    ge(pe, exp_done, heads * steps * i + n - 1)
                    nc.tensor.matmul(second[0:width, n % 2], k_hold[0:exp_rows, a, k * width:(k + 1) * width],
                                     q_move[0:exp_rows, i % 2, a, r * TOK:(r + 1) * TOK],
                                     start=True, stop=True).then_inc(second_done, 1)

                def weigh(i, t):
                    r, k = t // n_k, t % n_k
                    if r == 0:
                        for j, tiles in enumerate(sets):
                            if k == tiles[0]:
                                ge(pe, v_loaded[j], 16 * (i // stages_per_group + 1))
                    if k == 0:
                        ge(pe, weighted_read, i * r_tiles + r - n_acc + 1)
                    ge(pe, exp_done, heads * (steps * i + t) + heads)
                    for a in range(heads):
                        cols = slice(a * HEAD_DIM, (a + 1) * HEAD_DIM)
                        mm = nc.tensor.matmul(weighted[cols, r % n_acc], v_sb[0:width, k, cols],
                                              expo[0:width, t % p_slots, a], start=k == 0, stop=k == n_k - 1)
                    mm.then_inc(weighted_done, 1)

                def add_up(i, p):
                    r, k = p // sums_per_tile, p % sums_per_tile
                    if k == 0:
                        ge(pe, sums_read, i * r_tiles + r - n_acc + 1)
                    ge(pe, pair_done, n_sums * i + p + 1)
                    for a in range(heads):
                        cols = slice(a * HEAD_DIM, (a + 1) * HEAD_DIM)
                        mm = nc.tensor.matmul(total[cols, r % n_acc], ones[0:width], pair_sum[0:width, p % 2, a],
                                              start=k == 0, stop=k == sums_per_tile - 1)
                    mm.then_inc(total_done, 1)

                def stage(i, with_last, with_next):
                    for what, n, of in schedule:
                        if of == -1 and not with_last or of == 1 and not with_next:
                            continue
                        if what == "second":
                            second_pass(i, n)
                        elif what == "first":
                            first_pass(i + 1, n)
                        elif what == "turn":
                            turn_max(i + 1)
                        elif what == "weigh":
                            weigh(i + of, n)
                        elif what == "add_up":
                            add_up(i + of, n)

                pe.wait_ge(ident_done, 2)
                pe.wait_ge(first_constants, n_constants)
                for n in range(n_parts):
                    first_pass(0, n)
                turn_max(0)
                pe.wait_ge(second_constants, 3)
                stage(0, False, True)
                with pe.Fori(1, stages - 1) as i:
                    stage(i, True, True)
                stage(stages - 1, True, False)
                for what, n, _ in tail:
                    if what == "weigh":
                        weigh(stages - 1, n)
                    elif what == "add_up":
                        add_up(stages - 1, n)

            @block.scalar
            def _(act):
                def exponential(i, n):
                    t, a = n // heads, n % heads
                    if a == 0:
                        ge(act, weighted_done, steps * i + t - p_slots + 1)
                        if t % 2 == 0:
                            ge(act, pair_done, n_sums * i + (t - p_slots) // 2 + 1)
                    ge(act, second_done, heads * steps * i + n + 1)
                    nc.scalar.activation(expo[0:width, t % p_slots, a], second[0:width, n % 2], ACT.Exp,
                                         scale=scale).then_inc(exp_done, 1)

                def take_weighted(i, r):
                    n = i * r_tiles + r
                    ge(act, weighted_done, steps * i + n_k * (r + 1))
                    ge(act, mean_done, n)
                    nc.scalar.activation(unscaled[:], weighted[:, r % n_acc], ACT.Copy).then_inc(weighted_read, 1)

                def take_total(i, r):
                    n = i * r_tiles + r
                    ge(act, total_done, n_sums * i + sums_per_tile * (r + 1))
                    ge(act, inverse_done, 2 * n)
                    nc.scalar.activation(sums[:], total[:, r % n_acc], ACT.Copy).then_inc(sums_read, 1)

                def stage(i, jobs, with_last):
                    for what, n, of in jobs:
                        if of == -1 and not with_last:
                            continue
                        if what == "second":
                            exponential(i, n)
                        elif what == "take_weighted":
                            take_weighted(i + of, n)
                        elif what == "take_total":
                            take_total(i + of, n)

                stage(0, schedule, False)
                with act.Fori(1, stages) as i:
                    stage(i, schedule, True)
                stage(stages - 1, tail, True)

            @block.vector
            def _(dve):
                if masked:
                    nc.vector.memset(q_hold[base:base + 2].bitcast(F32), 1.0).then_inc(first_constants, 1)
                nc.vector.memset(row_max[:], 0.0).then_inc(first_constants, 1)
                nc.vector.memset(ones[:], 1.0).then_inc(first_constants, 1)
                dve.wait_ge(first_constants, n_constants)

                def maxima(i, n):
                    a, s, k0 = items[n]
                    ge(dve, first_done, n_items * i + n + 1)
                    if long:
                        if n == 0:
                            ge(dve, row_max_done, i)
                        k = k0 // (2 * TOK)
                        nc.vector.tensor_reduce(part_max[:, a * r_tiles * SUB + s, k:k + 1], first[:, n % 2],
                                                AX_X, ALU.max).then_inc(first_read, 1)
                    else:
                        if n == 0:
                            ge(dve, turned, i)
                        at = a * r_tiles * SUB + s
                        nc.vector.tensor_reduce(
                            row_max[:, at:at + 2], first[:, n % 2, 0:2 * keys].rearrange("p (s k) -> p s k", k=keys),
                            AX_X, ALU.max).then_inc(first_read if n < n_items - 1 else row_max_done, 1)

                def split_max(i):
                    if long:
                        ge(dve, first_read, n_reads * i + n_items)
                        ge(dve, turned, i)
                        nc.vector.tensor_reduce(row_max[:, 0:n_max], part_max[:], AX_X, ALU.max).then_inc(row_max_done, 1)
                    ge(dve, max_loaded, 32 * i)
                    ge(dve, turned, i + 1)
                    nc.vector.tensor_copy(max_high[:], first[0:n_max, 0, 0:P]).then_inc(max_high_done, 1)
                    ge(dve, max_high_done, i + 1)
                    nc.vector.tensor_tensor(max_low[:], first[0:n_max, 0, 0:P], max_high[:].bitcast(F32),
                                            ALU.subtract).then_inc(first_read, 1 if long else 2)

                def divide(i, r, part):
                    n = i * r_tiles + r
                    if part < 2:
                        ge(dve, sums_read, n + 1)
                        ge(dve, mean_done, n)
                        cols = slice(part * (TOK // 2), (part + 1) * (TOK // 2))
                        nc.vector.reciprocal(inverse[:, cols], sums[:, cols]).then_inc(inverse_done, 1)
                    else:
                        u = r % n_acc
                        ge(dve, inverse_done, 2 * (n + 1))
                        ge(dve, weighted_read, n + 1)
                        ge(dve, out_stored[u], 16 * (i * (r_tiles // n_acc) + r // n_acc))
                        nc.vector.tensor_tensor(mean[:, u], unscaled[:], inverse[:], ALU.mult).then_inc(mean_done, 1)

                def stage(i, with_last, with_next):
                    pending = []
                    for what, n, of in schedule:
                        if of == -1 and not with_last or of == 1 and not with_next:
                            continue
                        if what == "first" and n % 2 == 1:
                            maxima(i + 1, n // 2)
                        elif what == "turn":
                            split_max(i + 1)
                        elif what == "divide":
                            pending += [(i + of, n, part) for part in range(3)]
                        if pending and (what == "second" and n % 2 == 1 or not with_next):
                            divide(*pending.pop(0))
                    for job in pending:
                        divide(*job)

                for n in range(n_items):
                    maxima(0, n)
                split_max(0)
                stage(0, False, True)
                with dve.Fori(1, stages - 1) as i:
                    stage(i, True, True)
                stage(stages - 1, True, False)
                for what, n, _ in tail:
                    if what == "divide":
                        for part in range(3):
                            divide(stages - 1, n, part)


def context_phase(nc, ctx_t, mask, k_w, v_w, k_t, v, mask_rows):
    dim, keys = ctx_t.shape
    batches, batch_keys = mask.shape
    chunks = dim // P
    pieces = next(n for n in range(-(-keys // P), keys) if keys % n == 0)
    piece = keys // pieces
    assert keys <= TOK

    with ExitStack() as stack:
        m = Memory(nc, stack, "context")
        raw = m.sbuf("raw", [P, 2, chunks, dim])
        w_high = m.sbuf("w_high", [P, 2, chunks, dim], F32R)
        w_low = m.sbuf("w_low", [P, 2, chunks, dim], F32R)
        c_raw = m.sbuf("c_raw", [P, chunks, keys])
        c_high = m.sbuf("c_high", [P, chunks, keys], F32R)
        c_low = m.sbuf("c_low", [P, chunks, keys], F32R)
        k_high = m.sbuf("k_high", [P, chunks, keys], F32R)
        k_low = m.sbuf("k_low", [P, chunks, keys], F32R)
        v_sb = m.sbuf("v_sb", [P, pieces, dim])
        mask_raw = m.sbuf("mask_raw", [batches, batch_keys], I32)
        bias = m.sbuf("bias", [batches, batch_keys])
        bias_high = m.sbuf("bias_high", [batches, batch_keys], F32R)
        bias_low = m.sbuf("bias_low", [batches, batch_keys], F32R)
        result = m.psum("result", [P, 4 + pieces, TOK])

        c_loaded = m.sem("c_loaded")
        mask_loaded = m.sem("mask_loaded")
        w_loaded = [m.sem(f"w_loaded{k}") for k in range(2)]
        high_done = m.sem("high_done")
        split_done = m.sem("split_done")
        bias_done = m.sem("bias_done")
        product_done = m.sem("product_done")
        k_high_done = m.sem("k_high_done")
        result_ready = m.sem("result_ready")
        stored = m.sem("stored")

        with nc.Block() as block:

            @block.sync
            def _(sp):
                sp.dma_start(c_raw[:], ctx_t.rearrange("(c p) t -> p c t", p=P)).then_inc(c_loaded, 16)
                for k, w in enumerate((k_w, v_w)):
                    sp.dma_start(raw[:, k], w.rearrange("(c p) n -> p c n", p=P)).then_inc(w_loaded[k], 16)
                sp.dma_start(mask_raw[:], mask).then_inc(mask_loaded, 16)
                sp.wait_ge(bias_done, 4)
                for part, src in ((0, bias_high), (1, bias_low)):
                    sp.dma_start(mask_rows[:, part], src[:].bitcast(F32)).then_inc(stored, 16)
                for g in range(chunks):
                    sp.wait_ge(result_ready, g + 1)
                    for part, src in ((0, k_high), (1, k_low)):
                        sp.dma_start(k_t[part, g * P:(g + 1) * P, :], src[:, g].bitcast(F32)).then_inc(stored, 16)
                for n in range(pieces):
                    sp.wait_ge(result_ready, chunks + n + 1)
                    sp.dma_start(v[n * piece:(n + 1) * piece, :], v_sb[0:piece, n]).then_inc(stored, 16)
                sp.wait_ge(stored, 16 * (2 + 2 * chunks + pieces))

            @block.scalar
            def _(act):
                act.wait_ge(c_loaded, 16)
                nc.scalar.activation(c_high[:], c_raw[:], ACT.Copy).then_inc(high_done, 1)
                for k in range(2):
                    act.wait_ge(w_loaded[k], 16)
                    nc.scalar.activation(w_high[:, k], raw[:, k], ACT.Copy).then_inc(high_done, 1)
                for g in range(chunks):
                    act.wait_ge(product_done, g + 1)
                    nc.scalar.activation(k_high[:, g], result[:, g, 0:keys], ACT.Copy).then_inc(k_high_done, 1)

            @block.vector
            def _(dve):
                dve.wait_ge(high_done, 1)
                nc.vector.tensor_tensor(c_low[:], c_raw[:], c_high[:].bitcast(F32), ALU.subtract).then_inc(split_done, 1)
                for k in range(2):
                    dve.wait_ge(high_done, k + 2)
                    nc.vector.tensor_tensor(w_low[:, k], raw[:, k], w_high[:, k].bitcast(F32),
                                            ALU.subtract).then_inc(split_done, 1)
                dve.wait_ge(mask_loaded, 16)
                nc.vector.tensor_scalar(bias[:], mask_raw[:], -1.0, 1.0, ALU.mult, ALU.add).then_inc(bias_done, 1)
                dve.wait_ge(bias_done, 1)
                nc.vector.tensor_scalar(bias[:], bias[:], MASK_BIAS * math.sqrt(HEAD_DIM), None,
                                        ALU.mult).then_inc(bias_done, 1)
                dve.wait_ge(bias_done, 2)
                nc.vector.tensor_copy(bias_high[:], bias[:]).then_inc(bias_done, 1)
                dve.wait_ge(bias_done, 3)
                nc.vector.tensor_tensor(bias_low[:], bias[:], bias_high[:].bitcast(F32), ALU.subtract).then_inc(bias_done, 1)
                for g in range(chunks):
                    dve.wait_ge(k_high_done, g + 1)
                    nc.vector.tensor_tensor(k_low[:, g], result[:, g, 0:keys], k_high[:, g].bitcast(F32),
                                            ALU.subtract).then_inc(result_ready, 1)
                for n in range(pieces):
                    dve.wait_ge(product_done, chunks + n + 1)
                    nc.vector.tensor_copy(v_sb[0:piece, n], result[0:piece, chunks + n]).then_inc(result_ready, 1)

            @block.tensor
            def _(pe):
                pe.wait_ge(split_done, 2)
                for g in range(chunks):
                    for c in range(chunks):
                        cols = slice(g * P, (g + 1) * P)
                        mm = product(nc, result[:, g, 0:keys], (w_high[:, 0, c, cols], w_low[:, 0, c, cols]),
                                     (c_high[:, c], c_low[:, c]), c == 0, c == chunks - 1)
                    mm.then_inc(product_done, 1)
                pe.wait_ge(split_done, 3)
                for n in range(pieces):
                    for c in range(chunks):
                        cols = slice(n * piece, (n + 1) * piece)
                        mm = product(nc, result[0:piece, chunks + n], (c_high[:, c, cols], c_low[:, c, cols]),
                                     (w_high[:, 1, c], w_low[:, 1, c]), c == 0, c == chunks - 1)
                    mm.then_inc(product_done, 1)


def mlp_phase(nc, x_in, xn, w1, b1, w2, b2, out):
    dim, hidden = w1.shape
    tiles = x_in.shape[0] // TOK
    chunks = dim // P
    steps = hidden // P
    lag = 2
    per_set = 4
    sets = steps // per_set
    ring = 4
    slots = 2

    with ExitStack() as stack:
        m = Memory(nc, stack, "mlp")
        raw = m.sbuf("raw", [P, 2, per_set, dim])
        w1_high = m.sbuf("w1_high", [P, sets, chunks, per_set * P], F32R)
        w1_low = m.sbuf("w1_low", [P, sets, chunks, per_set * P], F32R)
        w2_high = m.sbuf("w2_high", [P, sets, per_set, dim], F32R)
        w2_low = m.sbuf("w2_low", [P, sets, per_set, dim], F32R)
        b1_col = m.sbuf("b1_col", [P, steps])
        b2_row = m.sbuf("b2_row", [P, dim])
        xt_high = m.sbuf("xt_high", [P, 2, chunks, TOK], F32R)
        xt_low = m.sbuf("xt_low", [P, 2, chunks, TOK], F32R)
        x = m.sbuf("x", [P, 2, SUB, dim])
        h = m.sbuf("h", [P, 2, TOK])
        h_high = m.sbuf("h_high", [P, slots, TOK], F32R)
        h_low = m.sbuf("h_low", [P, slots, TOK], F32R)
        hidden_sum = m.psum("hidden_sum", [P, ring, TOK])
        out_sum = m.psum("out_sum", [P, SUB, TOK])

        w_loaded = [m.sem(f"w_loaded{k}") for k in range(2)]
        w_high_done = m.sem("w_high_done")
        w_ready = m.sem("w_ready")
        bias_loaded = m.sem("bias_loaded")
        xn_loaded = [m.sem(f"xn_loaded{u}") for u in range(2)]
        x_loaded = [m.sem(f"x_loaded{u}") for u in range(2)]
        hidden_done = m.sem("hidden_done")
        gelu_done = m.sem("gelu_done")
        h_high_done = m.sem("h_high_done")
        h_ready = m.sem("h_ready")
        h_used = m.sem("h_used")
        bias_added = m.sem("bias_added")
        out_done = m.sem("out_done")
        stored = [m.sem(f"stored{u}") for u in range(2)]
        waits_passed = m.sem("waits_passed")

        def split_after(j):
            k = 2 * (j // per_set + 1) + j % per_set // 2
            return k if j % 2 == 1 and k < 2 * sets else None

        def in_pairs(eng, body):
            body(0, 0)
            body(1, 1)
            with eng.Fori(1, tiles // 2 - 1) as pair:
                body(2 * pair, 0)
                body(2 * pair + 1, 1)
            body(tiles - 2, 0)
            body(tiles - 1, 1)

        with nc.Block() as block:

            @block.sync
            def _(sp):
                x_view = x_in.rearrange("(t s p) d -> t p s d", p=P, s=SUB)
                out_view = out.rearrange("(t s p) d -> t p s d", p=P, s=SUB)

                def load_norm(t, u):
                    for part, to in ((0, xt_high), (1, xt_low)):
                        sp.dma_start(to[:, u].bitcast(F32), xn[part].rearrange("(c p) t -> p c t", p=P)[
                            :, :, bass.ds(t * TOK, TOK)]).then_inc(xn_loaded[u], 16)

                def load_x(t, u):
                    sp.dma_start(x[:, u], x_view[t]).then_inc(x_loaded[u], 16)

                def load_set(k):
                    j = k // 2
                    if k >= 2:
                        sp.wait_ge(w_ready, k - 1)
                    if k % 2 == 0:
                        src = w1.rearrange("(c p) n -> p c n", p=P)[:, :, j * per_set * P:(j + 1) * per_set * P]
                    else:
                        src = w2.rearrange("(k p) n -> p k n", p=P)[:, j * per_set:(j + 1) * per_set]
                    sp.dma_start(raw[:, k % 2], src).then_inc(w_loaded[k % 2], 16)

                load_set(0)
                sp.dma_start(b1_col[:], b1).then_inc(bias_loaded, 16)
                sp.dma_start(b2_row[:], b2.unsqueeze(0).to_broadcast([P, dim])).then_inc(bias_loaded, 16)
                load_norm(0, 0)
                for k in range(1, 4):
                    load_set(k)
                load_x(0, 0)
                for k in range(4, 2 * sets):
                    load_set(k)
                load_norm(1, 1)
                load_x(1, 1)

                def traffic(t, u):
                    wait_alone(sp, out_done, SUB * (t + 1), waits_passed)
                    sp.dma_start(out_view[t], x[:, u]).then_inc(stored[u], 16)
                    if not (isinstance(t, int) and t >= tiles - 2):
                        wait_alone(sp, stored[u], 16 * (t // 2 + 1), waits_passed)
                        load_norm(t + 2, u)
                        load_x(t + 2, u)

                in_pairs(sp, traffic)
                for u in range(2):
                    sp.wait_ge(stored[u], 16 * tiles // 2)

            @block.tensor
            def _(pe):
                def first_product(t, u, j):
                    if j == 0:
                        pe.wait_ge(xn_loaded[u], 32 * (t // 2 + 1))
                    if isinstance(t, int) and t == 0 and j % per_set == 0:
                        pe.wait_ge(w_ready, 2 * (j // per_set) + 1)
                    if not (isinstance(t, int) and t == 0 and j < ring):
                        pe.wait_ge(gelu_done, steps * t + j - ring + 1)
                    cols = slice(j % per_set * P, (j % per_set + 1) * P)
                    for c in range(chunks):
                        mm = product(nc, hidden_sum[:, j % ring],
                                     (w1_high[:, j // per_set, c, cols], w1_low[:, j // per_set, c, cols]),
                                     (xt_high[:, u, c], xt_low[:, u, c]), c == 0, c == chunks - 1)
                    mm.then_inc(hidden_done, 1)

                def second_product(t, j):
                    if isinstance(t, int) and t == 0 and j % per_set == 0:
                        pe.wait_ge(w_ready, 2 * (j // per_set) + 2)
                    pe.wait_ge(h_ready, steps * t + j + 1)
                    for s in range(SUB):
                        if j == 0 and not (isinstance(t, int) and t == 0):
                            pe.wait_ge(out_done, SUB * (t - 1) + s + 1)
                        cols = slice(s * P, (s + 1) * P)
                        mm = product(nc, out_sum[:, s], (h_high[:, j % slots, cols], h_low[:, j % slots, cols]),
                                     (w2_high[:, j // per_set, j % per_set], w2_low[:, j // per_set, j % per_set]),
                                     j == 0, j == steps - 1)
                    mm.then_inc(h_used, 1)

                def tile(t, u):
                    for j in range(steps):
                        first_product(t, u, j)
                        if j >= lag:
                            second_product(t, j - lag)
                        elif not (isinstance(t, int) and t == 0):
                            second_product(t - 1, steps - lag + j)

                in_pairs(pe, tile)
                for j in range(steps - lag, steps):
                    second_product(tiles - 1, j)

            @block.scalar
            def _(act):
                def gelu(t, j):
                    act.wait_ge(hidden_done, steps * t + j + 1)
                    if not (isinstance(t, int) and t == 0 and j < 2):
                        act.wait_ge(h_ready, steps * t + j - 1)
                    nc.scalar.activation(h[:, j % 2], hidden_sum[:, j % ring], ACT.Gelu,
                                         bias=b1_col[:, j:j + 1]).then_inc(gelu_done, 1)

                def split_high(k):
                    act.wait_ge(w_loaded[k % 2], 16 * (k // 2 + 1))
                    to = w1_high if k % 2 == 0 else w2_high
                    nc.scalar.activation(to[:, k // 2], raw[:, k % 2], ACT.Copy).then_inc(w_high_done, 1)

                def tile(t, u):
                    for j in range(steps):
                        gelu(t, j)
                        if isinstance(t, int) and t == 0 and split_after(j):
                            split_high(split_after(j))

                split_high(0)
                split_high(1)
                act.wait_ge(bias_loaded, 32)
                in_pairs(act, tile)

            @block.vector
            def _(dve):
                def split_h(t, j):
                    dve.wait_ge(gelu_done, steps * t + j + 1)
                    if not (isinstance(t, int) and t == 0 and j < slots):
                        dve.wait_ge(h_used, steps * t + j - slots + 1)
                    nc.vector.tensor_copy(h_high[:, j % slots], h[:, j % 2]).then_inc(h_high_done, 1)
                    dve.wait_ge(h_high_done, steps * t + j + 1)
                    nc.vector.tensor_tensor(h_low[:, j % slots], h[:, j % 2], h_high[:, j % slots].bitcast(F32),
                                            ALU.subtract).then_inc(h_ready, 1)

                def add_bias(t, u):
                    dve.wait_ge(x_loaded[u], 16 * (t // 2 + 1))
                    for s in range(SUB):
                        nc.vector.tensor_tensor(x[:, u, s], x[:, u, s], b2_row[:], ALU.add).then_inc(bias_added, 1)

                def finish(t, u):
                    dve.wait_ge(h_used, steps * (t + 1))
                    dve.wait_ge(bias_added, SUB * (t + 1))
                    for s in range(SUB):
                        nc.vector.tensor_tensor(x[:, u, s], out_sum[:, s], x[:, u, s], ALU.add).then_inc(out_done, 1)

                def tile(t, u):
                    for j in range(steps):
                        split_h(t, j)
                        if isinstance(t, int) and t == 0 and split_after(j):
                            split_low(split_after(j))
                        if j == lag - 1 and not (isinstance(t, int) and t == 0):
                            finish(t - 1, 1 - u)
                        if j == lag + 1:
                            add_bias(t, u)

                def split_low(k):
                    dve.wait_ge(w_high_done, k + 1)
                    high, low = (w1_high, w1_low) if k % 2 == 0 else (w2_high, w2_low)
                    nc.vector.tensor_tensor(low[:, k // 2], raw[:, k % 2], high[:, k // 2].bitcast(F32),
                                            ALU.subtract).then_inc(w_ready, 1)

                split_low(0)
                split_low(1)
                dve.wait_ge(bias_loaded, 32)
                in_pairs(dve, tile)
                finish(tiles - 1, 1)


def transformer_block(nc, x, ctx_t, mask, ln0_w, ln0_b, wq, wk, wv, sa_w, ln1_w, ln1_b, cq_w, ck_w, cv_w, ca_w,
                      ln2_w, ln2_b, fc1_w, fc1_b, fc2_w, fc2_b, out):
    tokens, dim = x.shape
    batches, batch_keys = mask.shape

    def scratch(name, shape):
        return nc.dram_tensor(name, shape, F32, kind="Internal").ap()

    q_t = scratch("q_t", [2, dim, tokens])
    k_t = scratch("k_t", [2, dim, tokens])
    v = scratch("v", [tokens, dim])
    self_t = scratch("self_t", [dim, tokens])
    x1 = scratch("x1", [tokens, dim])
    cq_t = scratch("cq_t", [2, dim, tokens])
    ck_t = scratch("ck_t", [2, dim, batches * batch_keys])
    cv = scratch("cv", [batches * batch_keys, dim])
    mask_rows = scratch("mask_rows", [batches, 2, batch_keys])
    cross_t = scratch("cross_t", [dim, tokens])
    x2 = scratch("x2", [tokens, dim])
    xn_t = scratch("xn_t", [2, dim, tokens])

    token_phase(nc, "qkv", x, ln0_w, ln0_b, v_w=wv, v_out=v, qk=[(wq, q_t), (wk, k_t)])
    attention_phase(nc, "self", q_t, k_t, v, self_t, tokens // batches, 1)
    context_phase(nc, ctx_t, mask, ck_w, cv_w, ck_t, cv, mask_rows)
    token_phase(nc, "mid", x, ln1_w, ln1_b, attn=self_t, proj_w=sa_w, x_out=x1, qk=[(cq_w, cq_t)])
    attention_phase(nc, "cross", cq_t, ck_t, cv, cross_t, batch_keys, 4, mask_rows)
    token_phase(nc, "late", x1, ln2_w, ln2_b, attn=cross_t, proj_w=ca_w, x_out=x2, xn_out=xn_t)
    mlp_phase(nc, x2, xn_t, fc1_w, fc1_b, fc2_w, fc2_b, out)


def kernel(**inputs):
    import numpy as np
    import concourse.bacc as bacc
    from concourse.bass_utils import run_bass_kernel_spmd

    def arr(name):
        return np.asarray(inputs[name])

    def turned(a):
        return np.ascontiguousarray(a.T)

    def columns(a):
        return np.ascontiguousarray(a.reshape(-1, P).T)

    x = arr("x")
    batches, length, dim = x.shape
    w = {k: arr(f"L0_xattn_{k}") for k in ("ln0_w", "ln0_b", "qkv_w", "sa_proj_w", "ln1_w", "ln1_b", "q_w", "k_w", "v_w",
                                           "ca_proj_w", "ln2_w", "ln2_b", "fc1_w", "fc1_b", "fc2_w", "fc2_b")}
    arrays = {
        "x": np.ascontiguousarray(x.reshape(batches * length, dim)),
        "ctx_t": turned(arr("ctx_1024").reshape(-1, dim)),
        "mask": np.ascontiguousarray(arr("mask_BxS2_ik0")),
        "ln0_w": columns(w["ln0_w"]), "ln0_b": columns(w["ln0_b"]),
        "wq": turned(w["qkv_w"][0:dim]), "wk": turned(w["qkv_w"][dim:2 * dim]), "wv": turned(w["qkv_w"][2 * dim:]),
        "sa_w": turned(w["sa_proj_w"]),
        "ln1_w": columns(w["ln1_w"]), "ln1_b": columns(w["ln1_b"]),
        "cq_w": turned(w["q_w"]), "ck_w": turned(w["k_w"]), "cv_w": turned(w["v_w"]), "ca_w": turned(w["ca_proj_w"]),
        "ln2_w": columns(w["ln2_w"]), "ln2_b": columns(w["ln2_b"]),
        "fc1_w": turned(w["fc1_w"]), "fc1_b": columns(w["fc1_b"]),
        "fc2_w": turned(w["fc2_w"]), "fc2_b": np.ascontiguousarray(w["fc2_b"]),
    }
    nc = bacc.Bacc("TRN2", target_bir_lowering=False, num_devices=1)
    args = [nc.dram_tensor(f"in_{k}", a.shape, mybir.dt.from_np(a.dtype), kind="ExternalInput").ap()
            for k, a in arrays.items()]
    out = nc.dram_tensor("out", [batches * length, dim], F32, kind="ExternalOutput").ap()
    transformer_block(nc, *args, out)
    r = run_bass_kernel_spmd(nc, [{f"in_{k}": a for k, a in arrays.items()}], core_ids=[0])
    return r.results[0]["out"].reshape(batches, length, dim)
```
